# Optimizing a Trainium2 kernel written in Bass

```python
import numpy as np
import jax
import jax.numpy as jnp

def _softmax(x, axis=-1):
    return jax.nn.softmax(x, axis=axis)

def _gelu(x):
    return jax.nn.gelu(x, approximate=True)

def _silu(x):
    return jax.nn.silu(x)

def _sigmoid(x):
    return jax.nn.sigmoid(x)

def _layernorm(x, axis=-1, eps=1e-05):
    m = jnp.mean(x, axis=axis, keepdims=True)
    v = jnp.var(x, axis=axis, keepdims=True)
    return (x - m) / jnp.sqrt(v + eps)

def _scatter_add(tgt, idx, src, axis=0):
    return tgt.at[idx].add(src)

def _segment_sum(src, seg, n):
    return jax.ops.segment_sum(src, seg, n)
kernel_name = 'mk_xattn_ffn_d2_seqx_r8_9e6200'

def setup_inputs(seed: int=0):
    np.random.seed(seed)
    _w = jnp.asarray

    def _rec_inputs():
        import jax
        import jax.numpy as jnp
        _rk = jax.random.key(seed)
        x = -0.0002928 + 1 * jax.random.normal(jax.random.fold_in(_rk, 1), (16, 256, 128), jnp.float32)
        _lenS = 256 - jax.random.randint(jax.random.fold_in(_rk, 7), (16,), 0, max(1, 256 // 4) + 1, jnp.int32)
        _lenS2 = 64 - jax.random.randint(jax.random.fold_in(_rk, 8), (16,), 0, max(1, 64 // 4) + 1, jnp.int32)
        _ctx_512P = jax.random.normal(jax.random.fold_in(_rk, 11), (16, 16, 64), jnp.float32)
        _ctx_512c = jax.random.dirichlet(jax.random.fold_in(_rk, 511), 0.3 * jnp.ones((16,), jnp.float32), (16, 64))
        _ctx_512t = jnp.einsum('bsk,bkd->bsd', _ctx_512c, _ctx_512P)
        _ctx_512t = _ctx_512t * jax.lax.rsqrt(jnp.mean(jnp.square(_ctx_512t)) + 1e-12) * 0.953939
        ctx_512 = 0.00222621 + 0.99962 * (_ctx_512t + 0.3 * jax.random.normal(jax.random.fold_in(_rk, 611), (16, 64, 64), jnp.float32))
        return (x, ctx_512)
    x, ctx_512 = _rec_inputs()

    def _L0_xattn_setup():
        import jax, jax.numpy as jnp
        import numpy as np
        B, T, TC, C, CC, H = (2, 256, 64, 128, 64, 16)
        D = C // H

        def _heads(t):
            b, l, _ = t.shape
            return t.reshape(b, l, H, D).transpose(0, 2, 1, 3)
        key = jax.random.key(seed)
        ks = jax.random.split(key, 18)
        w = lambda k, i, o: jax.random.normal(k, (i, o), jnp.float32) / np.sqrt(i).astype(np.float32)
        return {'x': jax.random.normal(ks[0], (B, T, C), jnp.float32), 'cross_input': jax.random.normal(ks[1], (B, TC, CC), jnp.float32), 'Wk': w(ks[2], C, C), 'bk': jnp.zeros((C,), jnp.float32), 'Wq': w(ks[3], C, C), 'bq': jnp.zeros((C,), jnp.float32), 'Wv': w(ks[4], C, C), 'bv': jnp.zeros((C,), jnp.float32), 'Wck': w(ks[5], CC, C), 'bck': jnp.zeros((C,), jnp.float32), 'Wcq': w(ks[6], C, C), 'bcq': jnp.zeros((C,), jnp.float32), 'Wcv': w(ks[7], CC, C), 'bcv': jnp.zeros((C,), jnp.float32), 'Wp': w(ks[8], C, C), 'bp': jnp.zeros((C,), jnp.float32)}
    _L0_xattn_all = _L0_xattn_setup()
    _L0_xattn_in = {k: v for k, v in _L0_xattn_all.items() if k in ('Wk', 'bk', 'Wq', 'bq', 'Wv', 'bv', 'Wck', 'bck', 'Wcq', 'bcq', 'Wcv', 'bcv', 'Wp', 'bp')}
    del _L0_xattn_all

    def _L0_ffn_setup():
        import jax, jax.numpy as jnp
        import numpy as np
        D_IN, D_HID = (128, 512)

        def _ternary(key, shape):
            return jax.random.randint(key, shape, -1, 2).astype(jnp.float32)

        def _tlin(x, w, s):
            return jnp.einsum('bsi,oi->bso', x, w) * s
        key = jax.random.key(seed)
        ks = jax.random.split(key, 12)
        inv = lambda fan: 1.0 / np.sqrt(fan).astype(np.float32)
        return {'x': jax.random.normal(ks[0], (4, 256, D_IN), dtype=jnp.float32), 'w1_w': _ternary(ks[1], (D_HID, D_IN)), 'w1_s': jax.random.uniform(ks[2], (D_HID,), dtype=jnp.float32) * inv(D_IN), 'w2_w': _ternary(ks[3], (D_HID, D_IN)), 'w2_s': jax.random.uniform(ks[4], (D_HID,), dtype=jnp.float32) * inv(D_IN), 'h1_w': _ternary(ks[5], (D_HID, D_HID)), 'h1_s': jax.random.uniform(ks[6], (D_HID,), dtype=jnp.float32) * inv(D_HID), 'h2_w': _ternary(ks[7], (D_HID, D_HID)), 'h2_s': jax.random.uniform(ks[8], (D_HID,), dtype=jnp.float32) * inv(D_HID), 'w3_w': _ternary(ks[9], (D_IN, D_HID)), 'w3_s': jax.random.uniform(ks[10], (D_IN,), dtype=jnp.float32) * inv(D_HID)}
    _L0_ffn_all = _L0_ffn_setup()
    _L0_ffn_in = {k: v for k, v in _L0_ffn_all.items() if k in ('w1_w', 'w1_s', 'w2_w', 'w2_s', 'h1_w', 'h1_s', 'h2_w', 'h2_s', 'w3_w', 'w3_s')}
    del _L0_ffn_all

    def _L1_xattn_setup():
        import jax, jax.numpy as jnp
        import numpy as np
        H, D, C1, C2, S, M, B, W = (16, 32, 128, 64, 256, 64, 2, 4)

        def _ln(x, g, b):
            m = jnp.mean(x, -1, keepdims=True)
            v = jnp.var(x, -1, keepdims=True)
            return (x - m) * jax.lax.rsqrt(v + 1e-05) * g + b

        def _mha(x, y, wq, wk, wv, li1_w, li1_b, lnx_g, lnx_b, lny_g, lny_b, ln3_g, ln3_b, li2_w, li2_b, li3_w, li3_b, causal):
            xn = _ln(x, lnx_g, lnx_b)
            yn = _ln(y, lny_g, lny_b)
            q = jnp.einsum('bsc,hcd->bhsd', xn, wq)
            k = jnp.einsum('btc,hcd->bhtd', yn, wk)
            v = jnp.einsum('btc,hcd->bhtd', yn, wv)
            a = jax.nn.softmax(jnp.einsum('bhsd,bhtd->bhst', q, k) * D ** (-0.5), axis=-1)
            if causal:
                s, t = (a.shape[-2], a.shape[-1])
                mask = (jnp.arange(t)[None, :] > jnp.arange(s)[:, None]).astype(a.dtype)
                a = a * mask
            o = jnp.einsum('bhst,bhtd->bhsd', a, v)
            o = o.transpose(0, 2, 1, 3).reshape(x.shape[0], x.shape[1], H * D)
            x_out = x + o @ li1_w + li1_b
            h = jax.nn.gelu(_ln(x_out, ln3_g, ln3_b) @ li2_w + li2_b, approximate=False)
            return x_out + h @ li3_w + li3_b
        key = jax.random.key(seed)
        ks = iter(jax.random.split(key, 64))

        def w(shape, scale=0.02):
            return jax.random.normal(next(ks), shape, jnp.float32) * scale
        inp = {'xx': jax.random.normal(next(ks), (B, S, C1), jnp.float32), 'ee': jax.random.normal(next(ks), (B, M, C2), jnp.float32), 'ln1_g': jnp.ones(C1, jnp.float32), 'ln1_b': jnp.zeros(C1, jnp.float32), 'ln2_g': jnp.ones(C1, jnp.float32), 'ln2_b': jnp.zeros(C1, jnp.float32)}
        for pfx, cy in (('a1', C1), ('a2', C2)):
            inp[pfx + '_wq'] = w((H, C1, D))
            inp[pfx + '_wk'] = w((H, cy, D))
            inp[pfx + '_wv'] = w((H, cy, D))
            inp[pfx + '_li1_w'] = w((H * D, C1))
            inp[pfx + '_li1_b'] = jnp.zeros(C1, jnp.float32)
            inp[pfx + '_lnx_g'] = jnp.ones(C1, jnp.float32)
            inp[pfx + '_lnx_b'] = jnp.zeros(C1, jnp.float32)
            inp[pfx + '_lny_g'] = jnp.ones(cy, jnp.float32)
            inp[pfx + '_lny_b'] = jnp.zeros(cy, jnp.float32)
            inp[pfx + '_ln3_g'] = jnp.ones(C1, jnp.float32)
            inp[pfx + '_ln3_b'] = jnp.zeros(C1, jnp.float32)
            inp[pfx + '_li2_w'] = w((C1, C1 * W))
            inp[pfx + '_li2_b'] = jnp.zeros(C1 * W, jnp.float32)
            inp[pfx + '_li3_w'] = w((C1 * W, C1))
            inp[pfx + '_li3_b'] = jnp.zeros(C1, jnp.float32)
        inp['training'] = 0
        return inp
    _L1_xattn_all = _L1_xattn_setup()
    _L1_xattn_in = {k: v for k, v in _L1_xattn_all.items() if k in ('ln1_g', 'ln1_b', 'ln2_g', 'ln2_b', 'a1_wq', 'a1_wk', 'a1_wv', 'a1_li1_w', 'a1_li1_b', 'a1_lnx_g', 'a1_lnx_b', 'a1_lny_g', 'a1_lny_b', 'a1_ln3_g', 'a1_ln3_b', 'a1_li2_w', 'a1_li2_b', 'a1_li3_w', 'a1_li3_b', 'a2_wq', 'a2_wk', 'a2_wv', 'a2_li1_w', 'a2_li1_b', 'a2_lnx_g', 'a2_lnx_b', 'a2_lny_g', 'a2_lny_b', 'a2_ln3_g', 'a2_ln3_b', 'a2_li2_w', 'a2_li2_b', 'a2_li3_w', 'a2_li3_b')}
    del _L1_xattn_all

    def _L1_ffn_setup():
        import math
        import jax, jax.numpy as jnp
        import numpy as np
        B, L, D, F_FF, E = (4, 256, 128, 512, 8)
        TOP_K = 1
        CAPACITY_FACTOR = 1.25
        key = jax.random.key(seed)
        ks = jax.random.split(key, 4)
        h = jax.random.normal(ks[0], (B, L, D), dtype=jnp.float32)
        gate_w = jax.random.normal(ks[1], (E, D), dtype=jnp.float32) * 0.02
        gate_b = jnp.zeros((E,), dtype=jnp.float32)
        w1 = jax.random.normal(ks[2], (E, D, F_FF), dtype=jnp.float32) * 0.02
        b1 = jnp.zeros((E, F_FF), dtype=jnp.float32)
        w2 = jax.random.normal(ks[3], (E, F_FF, D), dtype=jnp.float32) * 0.02
        b2 = jnp.zeros((E, D), dtype=jnp.float32)
        return {'h': h, 'gate_w': gate_w, 'gate_b': gate_b, 'w1': w1, 'b1': b1, 'w2': w2, 'b2': b2}
    _L1_ffn_all = _L1_ffn_setup()
    _L1_ffn_in = {k: v for k, v in _L1_ffn_all.items() if k in ('gate_w', 'gate_b', 'w1', 'b1', 'w2', 'b2')}
    del _L1_ffn_all
    return {'x': x, 'ctx_512': ctx_512, 'L0_xattn_Wk': _L0_xattn_in['Wk'], 'L0_xattn_bk': _L0_xattn_in['bk'], 'L0_xattn_Wq': _L0_xattn_in['Wq'], 'L0_xattn_bq': _L0_xattn_in['bq'], 'L0_xattn_Wv': _L0_xattn_in['Wv'], 'L0_xattn_bv': _L0_xattn_in['bv'], 'L0_xattn_Wck': _L0_xattn_in['Wck'], 'L0_xattn_bck': _L0_xattn_in['bck'], 'L0_xattn_Wcq': _L0_xattn_in['Wcq'], 'L0_xattn_bcq': _L0_xattn_in['bcq'], 'L0_xattn_Wcv': _L0_xattn_in['Wcv'], 'L0_xattn_bcv': _L0_xattn_in['bcv'], 'L0_xattn_Wp': _L0_xattn_in['Wp'], 'L0_xattn_bp': _L0_xattn_in['bp'], 'L0_ffn_w1_w': _L0_ffn_in['w1_w'], 'L0_ffn_w1_s': _L0_ffn_in['w1_s'], 'L0_ffn_w2_w': _L0_ffn_in['w2_w'], 'L0_ffn_w2_s': _L0_ffn_in['w2_s'], 'L0_ffn_h1_w': _L0_ffn_in['h1_w'], 'L0_ffn_h1_s': _L0_ffn_in['h1_s'], 'L0_ffn_h2_w': _L0_ffn_in['h2_w'], 'L0_ffn_h2_s': _L0_ffn_in['h2_s'], 'L0_ffn_w3_w': _L0_ffn_in['w3_w'], 'L0_ffn_w3_s': _L0_ffn_in['w3_s'], 'L1_xattn_ln1_g': _L1_xattn_in['ln1_g'], 'L1_xattn_ln1_b': _L1_xattn_in['ln1_b'], 'L1_xattn_ln2_g': _L1_xattn_in['ln2_g'], 'L1_xattn_ln2_b': _L1_xattn_in['ln2_b'], 'L1_xattn_a1_wq': _L1_xattn_in['a1_wq'], 'L1_xattn_a1_wk': _L1_xattn_in['a1_wk'], 'L1_xattn_a1_wv': _L1_xattn_in['a1_wv'], 'L1_xattn_a1_li1_w': _L1_xattn_in['a1_li1_w'], 'L1_xattn_a1_li1_b': _L1_xattn_in['a1_li1_b'], 'L1_xattn_a1_lnx_g': _L1_xattn_in['a1_lnx_g'], 'L1_xattn_a1_lnx_b': _L1_xattn_in['a1_lnx_b'], 'L1_xattn_a1_lny_g': _L1_xattn_in['a1_lny_g'], 'L1_xattn_a1_lny_b': _L1_xattn_in['a1_lny_b'], 'L1_xattn_a1_ln3_g': _L1_xattn_in['a1_ln3_g'], 'L1_xattn_a1_ln3_b': _L1_xattn_in['a1_ln3_b'], 'L1_xattn_a1_li2_w': _L1_xattn_in['a1_li2_w'], 'L1_xattn_a1_li2_b': _L1_xattn_in['a1_li2_b'], 'L1_xattn_a1_li3_w': _L1_xattn_in['a1_li3_w'], 'L1_xattn_a1_li3_b': _L1_xattn_in['a1_li3_b'], 'L1_xattn_a2_wq': _L1_xattn_in['a2_wq'], 'L1_xattn_a2_wk': _L1_xattn_in['a2_wk'], 'L1_xattn_a2_wv': _L1_xattn_in['a2_wv'], 'L1_xattn_a2_li1_w': _L1_xattn_in['a2_li1_w'], 'L1_xattn_a2_li1_b': _L1_xattn_in['a2_li1_b'], 'L1_xattn_a2_lnx_g': _L1_xattn_in['a2_lnx_g'], 'L1_xattn_a2_lnx_b': _L1_xattn_in['a2_lnx_b'], 'L1_xattn_a2_lny_g': _L1_xattn_in['a2_lny_g'], 'L1_xattn_a2_lny_b': _L1_xattn_in['a2_lny_b'], 'L1_xattn_a2_ln3_g': _L1_xattn_in['a2_ln3_g'], 'L1_xattn_a2_ln3_b': _L1_xattn_in['a2_ln3_b'], 'L1_xattn_a2_li2_w': _L1_xattn_in['a2_li2_w'], 'L1_xattn_a2_li2_b': _L1_xattn_in['a2_li2_b'], 'L1_xattn_a2_li3_w': _L1_xattn_in['a2_li3_w'], 'L1_xattn_a2_li3_b': _L1_xattn_in['a2_li3_b'], 'L1_ffn_gate_w': _L1_ffn_in['gate_w'], 'L1_ffn_gate_b': _L1_ffn_in['gate_b'], 'L1_ffn_w1': _L1_ffn_in['w1'], 'L1_ffn_b1': _L1_ffn_in['b1'], 'L1_ffn_w2': _L1_ffn_in['w2'], 'L1_ffn_b2': _L1_ffn_in['b2']}

def reference(x, ctx_512, L0_xattn_Wk, L0_xattn_bk, L0_xattn_Wq, L0_xattn_bq, L0_xattn_Wv, L0_xattn_bv, L0_xattn_Wck, L0_xattn_bck, L0_xattn_Wcq, L0_xattn_bcq, L0_xattn_Wcv, L0_xattn_bcv, L0_xattn_Wp, L0_xattn_bp, L0_ffn_w1_w, L0_ffn_w1_s, L0_ffn_w2_w, L0_ffn_w2_s, L0_ffn_h1_w, L0_ffn_h1_s, L0_ffn_h2_w, L0_ffn_h2_s, L0_ffn_w3_w, L0_ffn_w3_s, L1_xattn_ln1_g, L1_xattn_ln1_b, L1_xattn_ln2_g, L1_xattn_ln2_b, L1_xattn_a1_wq, L1_xattn_a1_wk, L1_xattn_a1_wv, L1_xattn_a1_li1_w, L1_xattn_a1_li1_b, L1_xattn_a1_lnx_g, L1_xattn_a1_lnx_b, L1_xattn_a1_lny_g, L1_xattn_a1_lny_b, L1_xattn_a1_ln3_g, L1_xattn_a1_ln3_b, L1_xattn_a1_li2_w, L1_xattn_a1_li2_b, L1_xattn_a1_li3_w, L1_xattn_a1_li3_b, L1_xattn_a2_wq, L1_xattn_a2_wk, L1_xattn_a2_wv, L1_xattn_a2_li1_w, L1_xattn_a2_li1_b, L1_xattn_a2_lnx_g, L1_xattn_a2_lnx_b, L1_xattn_a2_lny_g, L1_xattn_a2_lny_b, L1_xattn_a2_ln3_g, L1_xattn_a2_ln3_b, L1_xattn_a2_li2_w, L1_xattn_a2_li2_b, L1_xattn_a2_li3_w, L1_xattn_a2_li3_b, L1_ffn_gate_w, L1_ffn_gate_b, L1_ffn_w1, L1_ffn_b1, L1_ffn_w2, L1_ffn_b2):
    import jax
    import jax.numpy as jnp

    def _L0_xattn_ref(x, cross_input, Wk, bk, Wq, bq, Wv, bv, Wck, bck, Wcq, bcq, Wcv, bcv, Wp, bp):
        import jax, jax.numpy as jnp
        import numpy as np
        B, T, TC, C, CC, H = (2, 256, 64, 128, 64, 16)
        D = C // H

        def _heads(t):
            b, l, _ = t.shape
            return t.reshape(b, l, H, D).transpose(0, 2, 1, 3)
        scale = np.float32(1.0 / np.sqrt(D))
        q = _heads(x @ Wq + bq)
        k = _heads(x @ Wk + bk)
        v = _heads(x @ Wv + bv)
        att = jnp.einsum('bhqd,bhkd->bhqk', q, k) * scale
        causal = jnp.tril(jnp.ones((T, T), bool))
        att = jnp.where(causal[None, None], att, -jnp.inf)
        y = jnp.einsum('bhqk,bhkd->bhqd', jax.nn.softmax(att, axis=-1), v)
        qc = _heads(x @ Wcq + bcq)
        kc = _heads(cross_input @ Wck + bck)
        vc = _heads(cross_input @ Wcv + bcv)
        attc = jnp.einsum('bhqd,bhkd->bhqk', qc, kc) * scale
        y = y + jnp.einsum('bhqk,bhkd->bhqd', jax.nn.softmax(attc, axis=-1), vc)
        y = y.transpose(0, 2, 1, 3).reshape(x.shape[0], T, C)
        return y @ Wp + bp

    def _L0_ffn_ref(x, w1_w, w1_s, w2_w, w2_s, h1_w, h1_s, h2_w, h2_s, w3_w, w3_s):
        import jax, jax.numpy as jnp
        import numpy as np
        D_IN, D_HID = (128, 512)

        def _ternary(key, shape):
            return jax.random.randint(key, shape, -1, 2).astype(jnp.float32)

        def _tlin(x, w, s):
            return jnp.einsum('bsi,oi->bso', x, w) * s
        h = jax.nn.silu(_tlin(x, w1_w, w1_s)) * _tlin(x, w2_w, w2_s)
        h = jax.nn.gelu(_tlin(h, h1_w, h1_s), approximate=False)
        h = jax.nn.gelu(_tlin(h, h2_w, h2_s), approximate=False)
        return _tlin(h, w3_w, w3_s)

    def _L1_xattn_ref(xx, ee, ln1_g, ln1_b, ln2_g, ln2_b, a1_wq, a1_wk, a1_wv, a1_li1_w, a1_li1_b, a1_lnx_g, a1_lnx_b, a1_lny_g, a1_lny_b, a1_ln3_g, a1_ln3_b, a1_li2_w, a1_li2_b, a1_li3_w, a1_li3_b, a2_wq, a2_wk, a2_wv, a2_li1_w, a2_li1_b, a2_lnx_g, a2_lnx_b, a2_lny_g, a2_lny_b, a2_ln3_g, a2_ln3_b, a2_li2_w, a2_li2_b, a2_li3_w, a2_li3_b, training):
        import jax, jax.numpy as jnp
        import numpy as np
        H, D, C1, C2, S, M, B, W = (16, 32, 128, 64, 256, 64, 2, 4)

        def _ln(x, g, b):
            m = jnp.mean(x, -1, keepdims=True)
            v = jnp.var(x, -1, keepdims=True)
            return (x - m) * jax.lax.rsqrt(v + 1e-05) * g + b

        def _mha(x, y, wq, wk, wv, li1_w, li1_b, lnx_g, lnx_b, lny_g, lny_b, ln3_g, ln3_b, li2_w, li2_b, li3_w, li3_b, causal):
            xn = _ln(x, lnx_g, lnx_b)
            yn = _ln(y, lny_g, lny_b)
            q = jnp.einsum('bsc,hcd->bhsd', xn, wq)
            k = jnp.einsum('btc,hcd->bhtd', yn, wk)
            v = jnp.einsum('btc,hcd->bhtd', yn, wv)
            a = jax.nn.softmax(jnp.einsum('bhsd,bhtd->bhst', q, k) * D ** (-0.5), axis=-1)
            if causal:
                s, t = (a.shape[-2], a.shape[-1])
                mask = (jnp.arange(t)[None, :] > jnp.arange(s)[:, None]).astype(a.dtype)
                a = a * mask
            o = jnp.einsum('bhst,bhtd->bhsd', a, v)
            o = o.transpose(0, 2, 1, 3).reshape(x.shape[0], x.shape[1], H * D)
            x_out = x + o @ li1_w + li1_b
            h = jax.nn.gelu(_ln(x_out, ln3_g, ln3_b) @ li2_w + li2_b, approximate=False)
            return x_out + h @ li3_w + li3_b
        x = _ln(xx, ln1_g, ln1_b)
        x = x + _mha(x, x, a1_wq, a1_wk, a1_wv, a1_li1_w, a1_li1_b, a1_lnx_g, a1_lnx_b, a1_lny_g, a1_lny_b, a1_ln3_g, a1_ln3_b, a1_li2_w, a1_li2_b, a1_li3_w, a1_li3_b, causal=True)
        x = _ln(x, ln2_g, ln2_b)
        return x + _mha(x, ee, a2_wq, a2_wk, a2_wv, a2_li1_w, a2_li1_b, a2_lnx_g, a2_lnx_b, a2_lny_g, a2_lny_b, a2_ln3_g, a2_ln3_b, a2_li2_w, a2_li2_b, a2_li3_w, a2_li3_b, causal=False)

    def _L1_ffn_ref(h, gate_w, gate_b, w1, b1, w2, b2):
        import math
        import jax, jax.numpy as jnp
        import numpy as np
        B, L, D, F_FF, E = (4, 256, 128, 512, 8)
        TOP_K = 1
        CAPACITY_FACTOR = 1.25
        Bh, Lh, Dh = h.shape
        T = Bh * Lh
        capacity = max(1, math.ceil(CAPACITY_FACTOR * (T * TOP_K / E)))
        x = h.reshape(T, Dh)
        logits = x @ gate_w.T + gate_b
        probs = jax.nn.softmax(logits, axis=-1)
        idx = jnp.argmax(probs, axis=-1)
        top_prob = jnp.max(probs, axis=-1)
        one_hot = jax.nn.one_hot(idx, E, dtype=jnp.int32)
        pos = jnp.take_along_axis(jnp.cumsum(one_hot, axis=0), idx[:, None], axis=1)[:, 0] - 1
        keep = pos < capacity
        safe_pos = jnp.where(keep, pos, 0)
        buf = jnp.zeros((E, capacity, Dh), dtype=x.dtype)
        buf = buf.at[idx, safe_pos].add(x * keep[:, None].astype(x.dtype))
        hdn = jax.nn.relu(jnp.einsum('ecd,edf->ecf', buf, w1) + b1[:, None, :])
        eout = jnp.einsum('ecf,efd->ecd', hdn, w2) + b2[:, None, :]
        gathered = eout[idx, safe_pos]
        out = gathered * (top_prob * keep.astype(x.dtype))[:, None]
        return out.reshape(Bh, Lh, Dh)
    x = x + _L0_xattn_ref(_layernorm(x, axis=-1), ctx_512, L0_xattn_Wk, L0_xattn_bk, L0_xattn_Wq, L0_xattn_bq, L0_xattn_Wv, L0_xattn_bv, L0_xattn_Wck, L0_xattn_bck, L0_xattn_Wcq, L0_xattn_bcq, L0_xattn_Wcv, L0_xattn_bcv, L0_xattn_Wp, L0_xattn_bp)
    x = x + _L0_ffn_ref(_layernorm(x, axis=-1), L0_ffn_w1_w, L0_ffn_w1_s, L0_ffn_w2_w, L0_ffn_w2_s, L0_ffn_h1_w, L0_ffn_h1_s, L0_ffn_h2_w, L0_ffn_h2_s, L0_ffn_w3_w, L0_ffn_w3_s)
    x = x + _L1_xattn_ref(_layernorm(x, axis=-1), ctx_512, L1_xattn_ln1_g, L1_xattn_ln1_b, L1_xattn_ln2_g, L1_xattn_ln2_b, L1_xattn_a1_wq, L1_xattn_a1_wk, L1_xattn_a1_wv, L1_xattn_a1_li1_w, L1_xattn_a1_li1_b, L1_xattn_a1_lnx_g, L1_xattn_a1_lnx_b, L1_xattn_a1_lny_g, L1_xattn_a1_lny_b, L1_xattn_a1_ln3_g, L1_xattn_a1_ln3_b, L1_xattn_a1_li2_w, L1_xattn_a1_li2_b, L1_xattn_a1_li3_w, L1_xattn_a1_li3_b, L1_xattn_a2_wq, L1_xattn_a2_wk, L1_xattn_a2_wv, L1_xattn_a2_li1_w, L1_xattn_a2_li1_b, L1_xattn_a2_lnx_g, L1_xattn_a2_lnx_b, L1_xattn_a2_lny_g, L1_xattn_a2_lny_b, L1_xattn_a2_ln3_g, L1_xattn_a2_ln3_b, L1_xattn_a2_li2_w, L1_xattn_a2_li2_b, L1_xattn_a2_li3_w, L1_xattn_a2_li3_b, 0)
    x = x + _L1_ffn_ref(_layernorm(x, axis=-1), L1_ffn_gate_w, L1_ffn_gate_b, L1_ffn_w1, L1_ffn_b1, L1_ffn_w2, L1_ffn_b2)
    return x

_drawn_inputs = setup_inputs


def setup_inputs(seed=0):
    import zlib

    import numpy as np

    out = dict(_drawn_inputs(seed))
    spreads = {'L0_xattn_bk': (0.0, 0.1),
     'L0_xattn_bq': (0.0, 0.1),
     'L0_xattn_bv': (0.0, 0.1),
     'L0_xattn_bck': (0.0, 0.1),
     'L0_xattn_bcq': (0.0, 0.1),
     'L0_xattn_bcv': (0.0, 0.1),
     'L0_xattn_bp': (0.0, 0.1),
     'L1_xattn_ln1_g': (1.0, 0.2),
     'L1_xattn_ln1_b': (0.0, 0.1),
     'L1_xattn_ln2_g': (1.0, 0.2),
     'L1_xattn_ln2_b': (0.0, 0.1),
     'L1_xattn_a1_li1_b': (0.0, 0.1),
     'L1_xattn_a1_lnx_g': (1.0, 0.2),
     'L1_xattn_a1_lnx_b': (0.0, 0.1),
     'L1_xattn_a1_lny_g': (1.0, 0.2),
     'L1_xattn_a1_lny_b': (0.0, 0.1),
     'L1_xattn_a1_ln3_g': (1.0, 0.2),
     'L1_xattn_a1_ln3_b': (0.0, 0.1),
     'L1_xattn_a1_li2_b': (0.0, 0.1),
     'L1_xattn_a1_li3_b': (0.0, 0.1),
     'L1_xattn_a2_li1_b': (0.0, 0.1),
     'L1_xattn_a2_lnx_g': (1.0, 0.2),
     'L1_xattn_a2_lnx_b': (0.0, 0.1),
     'L1_xattn_a2_lny_g': (1.0, 0.2),
     'L1_xattn_a2_lny_b': (0.0, 0.1),
     'L1_xattn_a2_ln3_g': (1.0, 0.2),
     'L1_xattn_a2_ln3_b': (0.0, 0.1),
     'L1_xattn_a2_li2_b': (0.0, 0.1),
     'L1_xattn_a2_li3_b': (0.0, 0.1),
     'L1_ffn_gate_b': (0.0, 0.1),
     'L1_ffn_b1': (0.0, 0.1),
     'L1_ffn_b2': (0.0, 0.1)}
    factors = {}
    for name, (base, spread) in spreads.items():
        noise = np.random.default_rng([zlib.crc32(name.encode()), seed]).standard_normal(out[name].shape)
        drawn = base * np.exp(spread * noise) if base else spread * noise
        out[name] = jnp.asarray(drawn.astype(out[name].dtype))
    for name, factor in factors.items():
        out[name] = (out[name] * factor).astype(out[name].dtype)
    return out
```

```python
from contextlib import ExitStack, contextmanager

import numpy as np

import concourse.bass as bass
from concourse import mybir
from concourse.alu_op_type import AluOpType as ALU

F32 = mybir.dt.float32
F16 = mybir.dt.float16
BF16 = mybir.dt.bfloat16
U32 = mybir.dt.uint32
ACT = mybir.ActivationFunctionType
X = mybir.AxisListType.X

P = 128
B, T, C, CC, TC = 16, 256, 128, 64, 64
TILES = B * T // P
H = 16
EPS = 1e-5
NEG = -1e30


class Counter:

    def __init__(self, stage, name, unit=1):
        prog = stage.prog
        self.name, self.unit, self.prog, self.stage = name, unit, prog, stage
        self.sem = prog.nc.alloc_semaphore(name)
        self.per = prog.per.get(name, 0)
        self.k = 0
        prog.counters.append(self)

    def mark(self, instruction):
        instruction.then_inc(self.sem, self.unit)
        self.k += 1
        self.prog.seen[self.name] = max(self.prog.seen.get(self.name, 0), self.k)
        return self.k

    def latest(self, engine, apart=False):
        self.wait(engine, self.stage.n, self.k, apart)

    def wait(self, engine, n, k, apart=False):
        if self.per == 0:
            return
        value = (n * self.per + k) * self.unit
        if not (isinstance(value, int) and value <= 0):
            engine.wait_ge(self.sem, value)
            if (apart or engine is self.prog.nc.gpsimd) and not isinstance(value, int):
                engine.nop(nofuse=True)

    def wait_all(self, engine, n):
        self.wait(engine, n, self.per)


class Chain:

    def __init__(self, stage, engine, name):
        self.stage, self.engine = stage, engine
        self.event = stage.counter(name)

    def __call__(self, instruction):
        k = self.event.mark(instruction)
        self.event.wait(self.engine, self.stage.n, k, apart=True)


class Stage:

    def __init__(self, prog, name):
        self.prog, self.name, self.n, self.mine = prog, name, 0, []

    def counter(self, name, unit=1):
        s = Counter(self, f"{self.name}_{name}", unit)
        self.mine.append(s)
        return s

    def chain(self, engine, name):
        return Chain(self, engine, name)

    def begin(self, n):
        self.n = n
        for s in self.mine:
            s.k = 0


class Prog:
    def __init__(self, nc, ctx, per, io):
        self.nc, self.ctx, self.per, self.io = nc, ctx, per, io
        self.seen, self.counters = {}, []

    def sb(self, name, shape, dt=F32, ctx=None):
        return (ctx or self.ctx).enter_context(self.nc.sbuf_tensor(name, shape, dt))

    def fence(self):
        self.nc.all_engine_barrier()

    @contextmanager
    def phase(self):
        before = self.nc.snapshot_sems()
        with ExitStack() as mem:
            yield mem
        self.fence()
        self.nc.clear_and_free_semaphores(self.nc.allocated_since(before))
        self.fence()


def advance(gen, pieces=1):
    for _ in range(pieces):
        if gen is not None:
            next(gen, None)


def finish(gen):
    if gen is not None:
        for _ in gen:
            pass


def pipeline(nc, nb, step):
    step(0, 0, True, False)
    with nc.Fori(0, (nb - 2) // 2) as j:
        step(j * 2 + 1, 1, False, False)
        step(j * 2 + 2, 0, False, False)
    step(nb - 1, (nb - 1) % 2, False, True)


class Bank:

    def __init__(self, stage, name, tensor):
        self.stage, self.bank, self.nc = stage, tensor, stage.prog.nc
        self.full = stage.counter(name + "_full")
        self.out = {e: stage.counter(f"{name}_out_{e}") for e in "va"}
        self.engine = {"v": self.nc.vector, "a": self.nc.scalar}

    def claim(self, apart=False):
        for s in self.out.values():
            s.latest(self.nc.tensor, apart)
        return self.bank

    def filled(self, inst):
        self.full.mark(inst)

    def drain(self, who):
        self.full.latest(self.engine[who])
        return self.engine[who]

    def drained(self, who, inst):
        return self.out[who].mark(inst)


class LayerNorm:

    def __init__(self, pr, stage, name, tiles, mem, width=C, twice=False):
        nc = pr.nc
        self.pr, self.stage, self.tiles, self.twice = pr, stage, tiles, twice
        name = stage.name + name
        self.stat = pr.sb(name + "_stat", [P, tiles, 6], F32, mem)
        self.mv = pr.sb(name + "_mv", [P, tiles, 2], F32, mem)
        self.tmp = pr.sb(name + "_tmp", [P, 3, tiles], F32, mem)
        self.rstd = pr.sb(name + "_rstd", [P, tiles], F32, mem)
        self.var_ready = stage.counter(name + "_var")
        self.rstd_ready = stage.counter(name + "_rstd")
        self.chain_p = stage.chain(nc.gpsimd, name + "_pow")
        self.chain_v = stage.chain(nc.vector, name + "_stats")

    def __call__(self, src, rows=P):
        nc, n = self.pr.nc, self.stage.n
        mv, tmp = self.mv[0:rows], self.tmp[0:rows]
        for t in range(self.tiles):
            inst = nc.vector.bn_stats(self.stat[0:rows, t, :], src[:, t, :])
        self.chain_v(inst)
        for t in range(self.tiles):
            inst = nc.vector.bn_aggr(mv[:, t, :], self.stat[0:rows, t, :])
        self.chain_v(inst)
        k = self.var_ready.mark(nc.vector.tensor_scalar(tmp[:, 0, :], mv[:, :, 1], EPS, None, ALU.add))
        self.var_ready.wait(nc.gpsimd, n, k)
        half, minus = self.pr.pow_half[0:rows, 0:self.tiles], self.pr.pow_one[0:rows, 0:self.tiles]
        r = self.rstd[0:rows, :]
        if not self.twice:
            k = self.rstd_ready.mark(nc.gpsimd.tensor_tensor(r, tmp[:, 0, :], half, ALU.pow))
        else:
            nc.gpsimd.tensor_tensor(tmp[:, 1, :], tmp[:, 0, :], minus, ALU.pow)
            self.chain_p(nc.gpsimd.tensor_tensor(r, tmp[:, 0, :], half, ALU.pow))
            self.chain_p(nc.gpsimd.tensor_tensor(tmp[:, 2, :], mv[:, :, 1], tmp[:, 1, :], ALU.mult))
            self.chain_p(nc.gpsimd.tensor_scalar(tmp[:, 2, :], tmp[:, 2, :], EPS, None, ALU.add))
            self.chain_p(nc.gpsimd.tensor_tensor(tmp[:, 1, :], tmp[:, 2, :], half, ALU.pow))
            k = self.rstd_ready.mark(nc.gpsimd.tensor_tensor(r, r, tmp[:, 1, :], ALU.mult))
        self.rstd_ready.wait(nc.vector, n, k)

    def normalise(self, out, src, rows=P):
        nc = self.pr.nc
        for t in range(self.tiles):
            inst = nc.vector.tensor_scalar(out[:, t, :], src[:, t, :], self.mv[0:rows, t, 0:1],
                                           self.rstd[0:rows, t:t + 1], ALU.subtract, ALU.mult)
        return inst


def constants(pr):
    nc = pr.nc
    pr.ident = pr.sb("ident", [P, P])
    pr.ident16 = pr.sb("ident16", [P, P], F16)
    pr.identb = pr.sb("identb", [P, P], BF16)
    pr.hide_later = pr.sb("hide_later", [P, 4, P], BF16)
    pr.quadrant = pr.sb("quadrant", [P, 4])
    pr.pow_half = pr.sb("pow_half", [P, 8])
    pr.pow_one = pr.sb("pow_one", [P, 8])
    pr.ones = pr.sb("ones", [P, P])
    s = pr.ctx.enter_context(nc.semaphore("const"))
    for m in (pr.ident, pr.ident16, pr.identb):
        nc.gpsimd.memset(m[:, :], 0.0).then_inc(s, 1)
    nc.gpsimd.memset(pr.hide_later[:, :, :], 0.0).then_inc(s, 1)
    nc.gpsimd.memset(pr.pow_half[:, :], -0.5).then_inc(s, 1)
    nc.gpsimd.memset(pr.pow_one[:, :], -1.0).then_inc(s, 1)
    nc.gpsimd.memset(pr.ones[:, :], 1.0).then_inc(s, 1)
    nc.gpsimd.wait_ge(s, 7)
    for m in (pr.ident, pr.ident16, pr.identb):
        nc.gpsimd.affine_select(out=m[:, :], in_=m[:, :], compare_op=ALU.not_equal, fill=1.0, base=0,
                                pattern=[[-1, P]], channel_multiplier=1).then_inc(s, 1)
    nc.gpsimd.affine_select(out=pr.hide_later[:, :, :], in_=pr.hide_later[:, :, :], compare_op=ALU.is_ge,
                            fill=NEG, base=0, pattern=[[0, 4], [-1, P]], channel_multiplier=1).then_inc(s, 1)
    nc.gpsimd.wait_ge(s, 11)
    sq = pr.ctx.enter_context(nc.semaphore("const_q"))
    nc.vector.memset(pr.quadrant[:, :], 0.0).then_inc(sq, 1)
    nc.vector.wait_ge(sq, 1)
    for j in range(4):
        nc.vector.memset(pr.quadrant[32 * j:32 * j + 32, j:j + 1], 1.0).then_inc(sq, 1)
    nc.vector.wait_ge(sq, 5)


def load(pr, dst, src, sem):
    pr.nc.sync.dma_start(dst, src).then_inc(sem, 16)


def l0_attention(pr, mem):
    nc, io = pr.nc, pr.io
    D, G, W = 8, 4, 32
    NM = 3 * D
    SCALE = 1.0 / float(np.sqrt(D))
    wload = pr.nc.alloc_semaphore("l0a_w")
    Wcat = pr.sb("a_wcat", [P, 4, C], F32, mem)
    bcat = pr.sb("a_bcat", [P, 4, C], F32, mem)
    Wctx = pr.sb("a_wctx", [CC, 2, C], F32, mem)
    bctx = pr.sb("a_bctx", [P, 2, C], F32, mem)
    Wp = pr.sb("a_wp", [P, C], F32, mem)
    bp = pr.sb("a_bp", [P, 2, C], F32, mem)
    for i, x in enumerate("q cq k v".split()):
        load(pr, Wcat[:, i, :], io["L0_xattn_W" + x], wload)
        load(pr, bcat[:, i, :], io["L0_xattn_b" + x].partition_broadcast(P), wload)
    for i, x in enumerate("ck cv".split()):
        load(pr, Wctx[:, i, :], io["L0_xattn_W" + x], wload)
        load(pr, bctx[:, i, :], io["L0_xattn_b" + x].partition_broadcast(P), wload)
        load(pr, bp[:, i, :], io["L0_xattn_bp"].partition_broadcast(P), wload)
    load(pr, Wp[:, :], io["L0_xattn_Wp"], wload)
    nc.sync.wait_ge(wload, 16 * 15)

    z = pr.sb("a_z", [P, 2, C], F32, mem)
    zT = pr.sb("a_zT", [P, T], F32, mem)
    ctx2 = pr.sb("a_ctx2", [CC, P], F32, mem)
    qf = pr.sb("a_qf", [P, 3, C], F32, mem)
    kcf = pr.sb("a_kcf", [CC, C], F32, mem)
    tok = pr.sb("a_tok", [P, 2, 3, H, W], F16, mem)
    kctok = pr.sb("a_kctok", [CC, H, W], F16, mem)
    QT = [pr.sb(f"a_QT{i}", [P, 2, G, T], F16, mem) for i in range(2)]
    KT = [pr.sb(f"a_KT{i}", [P, 4, G, T], F16, mem) for i in range(2)]
    KcT = [pr.sb(f"a_KcT{i}", [P, G, 4, TC], F16, mem) for i in range(2)]
    V = [pr.sb(f"a_V{i}", [P, 2, H, W], F32, mem) for i in range(2)]
    Vc = [pr.sb(f"a_Vc{i}", [P, H // 2, 2, W // 2], F32, mem) for i in range(2)]
    KTall = pr.sb("a_KTall", [P, G * T], F16, mem)
    nm = pr.sb("a_nm", [P, 2, 4, 2, G], F16, mem)
    nmT = pr.sb("a_nmT", [W, T], F16, mem)
    prob = [pr.sb(f"a_prob{i}", [P, 512], F32, mem) for i in range(4)]
    ysT = pr.sb("a_ysT", [P, 3, 512], F32, mem)
    den = pr.sb("a_den", [P, 2, H], F32, mem)
    denc = pr.sb("a_denc", [P, 2, H], F32, mem)
    y = pr.sb("a_y", [P, 2, H, D], F32, mem)
    yc = pr.sb("a_yc", [P, 2, H, D], F32, mem)
    yT = pr.sb("a_yT", [P, T], F32, mem)
    res = pr.sb("a_res", [P, 2, C], F32, mem)
    psum = pr.psum
    s0 = pr.nc.alloc_semaphore("a_init")
    cnt = 0
    for m in [*V, *Vc, tok, kctok]:
        nc.gpsimd.memset(m[...], 0.0).then_inc(s0, 1); cnt += 1
    nc.gpsimd.wait_ge(s0, cnt)
    nc.vector.wait_ge(s0, cnt)
    for i in range(2):
        nc.vector.memset(V[i][:, :, :, D:D + 1], 1.0)
        for a in range(2):
            nc.vector.memset(Vc[i][TC * a:TC * a + TC, :, a, D:D + 1], 1.0)
    nc.vector.memset(tok[:, :, 2, :, NM:NM + 1], 1.0)
    nc.vector.memset(kctok[:, :, NM:NM + 1], 1.0).then_inc(s0, 1)
    nc.vector.wait_ge(s0, cnt + 1)
    pr.fence()

    SP, SM, SE = Stage(pr, "ap"), Stage(pr, "am"), Stage(pr, "ae")
    ln = LayerNorm(pr, SP, "ln", 2, mem)
    pro = Bank(SP, "pro", psum[:, 0, :])
    bank16 = psum[:, 0, :].bitcast(F16)
    z_ready, ctx_ready, high, low = (SP.counter(x) for x in ("z", "ctx", "high", "low"))
    kt_masked = SP.counter("kt_masked")
    mx_full, mx_out = SP.counter("mx_full"), SP.counter("mx_out")
    nm_placed = SP.counter("nm_placed", 16)
    st_full, exp_done, sel_done, av_done, ys_full, ys_ready = (
        SM.counter(x) for x in ("st_full", "exp", "sel", "av", "ys_full", "ys"))
    epi = Bank(SE, "epi", psum[:, 7, :])
    chain_e = SE.chain(nc.vector, "chain")
    x_done = SE.counter("x")
    xs = pr.x

    def parts(ap, rows, heads):
        return ap.rearrange("p (h k d) -> p h k d", k=4, d=D)

    def prologue(n, p):
        SP.begin(n)
        src = xs[:, bass.ds(n * 2, 2), :]
        ln(src)
        z_ready.mark(ln.normalise(z, src))
        z_ready.latest(nc.gpsimd)
        ctx_ready.mark(nc.gpsimd.tensor_copy(ctx2[:, :].rearrange("c (a t) -> c a t", a=2),
                       pr.ctxT[:, bass.ds(n, 1), :].to_broadcast([CC, 2, TC])))
        yield
        z_ready.latest(nc.tensor)
        bank = pro.claim()
        for t in range(2):
            inst = nc.tensor.transpose(bank[:, t * P:t * P + P], z[:, t, :], pr.ident[:, :])
        pro.filled(inst)
        pro.drain("a")
        pro.drained("a", nc.scalar.activation(zT[:, :], bank[:, 0:T], ACT.Copy))
        yield
        for t in range(2):
            bank = pro.claim()
            pro.filled(nc.tensor.matmul(bank[:, :], zT[:, t * P:t * P + P], Wcat[:, :, :].rearrange("p a c -> p (a c)"),
                                        start=True, stop=True))
            pro.drain("v")
            high.latest(nc.vector)
            low.latest(nc.vector)
            nc.vector.tensor_tensor(V[p][:, t, :, 0:D], bank[:, 3 * C:4 * C].rearrange("p (h d) -> p h d", d=D),
                                    bcat[:, 3, :].rearrange("p (h d) -> p h d", d=D), ALU.add)
            pro.drained("v", nc.vector.tensor_tensor(qf[:, :, :].rearrange("p a c -> p (a c)"), bank[:, 0:3 * C],
                                                     bcat[:, 0:3, :].rearrange("p a c -> p (a c)"), ALU.add))
            pro.out["v"].latest(nc.scalar)
            qtok = parts(tok[:, t, 0:2, :, :].rearrange("p a h w -> p (a h w)"), P, 2 * H)
            ktok = parts(tok[:, t, 2, :, :].rearrange("p h w -> p (h w)"), P, H)
            q8 = qf[:, 0:2, :].rearrange("p a (h d) -> p (a h) d", d=D)
            k8 = qf[:, 2, :].rearrange("p (h d) -> p h d", d=D)
            nc.scalar.activation(qtok[:, :, 0:3:2, :], q8.unsqueeze(2).to_broadcast([P, 2 * H, 2, D]), ACT.Copy)
            high.mark(nc.scalar.activation(ktok[:, :, 0:2, :], k8.unsqueeze(2).to_broadcast([P, H, 2, D]), ACT.Copy))
            high.latest(nc.gpsimd)
            nc.gpsimd.tensor_tensor(qtok[:, :, 1, :], q8, qtok[:, :, 0, :], ALU.subtract)
            low.mark(nc.gpsimd.tensor_tensor(ktok[:, :, 2, :], k8, ktok[:, :, 0, :], ALU.subtract))
            yield
        ctx_ready.latest(nc.tensor)
        bank = pro.claim()
        pro.filled(nc.tensor.matmul(bank[:, 0:2 * C], ctx2[:, :], Wctx[:, :, :].rearrange("p a c -> p (a c)"),
                                    start=True, stop=True))
        pro.drain("v")
        for a in range(2):
            half = slice(TC * a, TC * a + TC)
            nc.vector.tensor_tensor(Vc[p][half, :, a, 0:D],
                                    bank[half, C:2 * C].rearrange("p (i a d) -> p i a d", a=2, d=D)[:, :, a, :],
                                    bctx[half, 1, :].rearrange("p (i a d) -> p i a d", a=2, d=D)[:, :, a, :], ALU.add)
        pro.drained("v", nc.vector.tensor_tensor(kcf[:, :], bank[0:TC, 0:C], bctx[0:TC, 0, :], ALU.add))
        pro.out["v"].latest(nc.scalar)
        kt_ = parts(kctok[:, :, :].rearrange("p h w -> p (h w)"), TC, H)
        k8 = kcf[:, :].rearrange("p (h d) -> p h d", d=D)
        high.mark(nc.scalar.activation(kt_[:, :, 0:2, :], k8.unsqueeze(2).to_broadcast([TC, H, 2, D]), ACT.Copy))
        high.latest(nc.gpsimd)
        low.mark(nc.gpsimd.tensor_tensor(kt_[:, :, 2, :], k8, kt_[:, :, 0, :], ALU.subtract))
        yield
        low.latest(nc.tensor)
        for t in range(2):
            pro.claim()
            for a in range(2):
                for g in range(G):
                    at = (a * G + g) * P
                    inst = nc.tensor.transpose(bank16[:, at:at + P],
                                               tok[:, t, a, 4 * g:4 * g + 4, :].rearrange("p h w -> p (h w)"),
                                               pr.ident16[:, :])
            pro.filled(inst)
            pro.drain("a")
            pro.drained("a", nc.scalar.activation(QT[p][:, :, :, t * P:t * P + P].rearrange("p a g t -> p (a g) t"),
                                                  bank16[:, :].rearrange("p (a t) -> p a t", t=P), ACT.Copy))
            yield
        pro.claim()
        for g in range(G):
            for t in range(2):
                at = (g * 2 + t) * P
                inst = nc.tensor.transpose(bank16[:, at:at + P],
                                           tok[:, t, 2, 4 * g:4 * g + 4, :].rearrange("p h w -> p (h w)"),
                                           pr.ident16[:, :])
        pro.filled(inst)
        pro.drain("a")
        kt_masked.wait_all(nc.scalar, n - 1)
        pro.drained("a", nc.scalar.activation(KTall[:, :], bank16[:, :], ACT.Copy))
        pro.out["a"].latest(nc.vector)
        for j in range(4):
            inst = nc.vector.tensor_scalar(KT[p][:, j, :, :].rearrange("p g t -> p (g t)"), KTall[:, :],
                                           pr.quadrant[:, j:j + 1], None, ALU.mult)
        kt_masked.mark(inst)
        yield
        pro.claim(apart=True)
        for g in range(G):
            inst = nc.tensor.transpose(bank16[:, g * TC:g * TC + TC],
                                       kctok[:, 4 * g:4 * g + 4, :].rearrange("p h w -> p (h w)"),
                                       pr.ident16[0:TC, 0:TC])
        pro.filled(inst)
        pro.drain("v")
        for j in range(4):
            inst = nc.vector.tensor_scalar(KcT[p][:, :, j, :],
                                           bank16[:, 0:G * TC].rearrange("p (g t) -> p g t", t=TC),
                                           pr.quadrant[:, j:j + 1], None, ALU.mult)
        pro.drained("v", inst)
        yield
        pro.out["a"].latest(nc.tensor), pro.out["v"].latest(nc.tensor)

        def mx_claim():
            mx_out.wait(nc.tensor, n, mx_full.k - 1)
            return psum[:, 1 + mx_full.k % 2, :]

        def mx_reduce(bank, out, shape):
            mx_full.latest(nc.vector)
            mx_out.mark(nc.vector.tensor_reduce(out, bank.rearrange("p (a b) -> p a b", a=shape), X, ALU.max, negate=True))

        for g in range(G):
            bank = mx_claim()
            for j in range(4):
                nc.tensor.matmul(bank[:, j * P:j * P + P], QT[p][:, 0, g, 0:P], KT[p][:, j, g, 0:P],
                                 start=(j == 0), stop=False, skip_group_check=True)
            mx_full.mark(nc.tensor.matmul(bank, pr.identb[:, :], pr.hide_later[:, :, :].rearrange("p a k -> p (a k)"),
                                          start=False, stop=True, skip_group_check=True))
            mx_reduce(bank, nm[:, 0, :, 0, g], 4)
            yield
            for jj in range(2):
                bank = mx_claim()
                for a in range(2):
                    nc.tensor.matmul(bank[:, a * T:a * T + T], QT[p][:, 0, g, P:T], KT[p][:, 2 * jj + a, g, :],
                                     start=(a == 0), stop=False, skip_group_check=True)
                diagonal = bank.rearrange("p (a h k) -> p a h k", a=2, h=2)[:, :, 1, :]
                mx_full.mark(nc.tensor.matmul(diagonal, pr.identb[:, :], pr.hide_later[:, 0:2, :],
                                              start=False, stop=True, skip_group_check=True))
                mx_reduce(bank, nm[:, 1, 2 * jj:2 * jj + 2, 0, g], 2)
                yield
        for t in range(2):
            for c in range(2):
                bank = mx_claim()
                for gg in range(2):
                    g = 2 * c + gg
                    inst = nc.tensor.matmul(bank[:, gg * 256:gg * 256 + 256], QT[p][:, 1, g, t * P:t * P + P],
                                            KcT[p][:, g, :, :].rearrange("p j t -> p (j t)"), start=(gg == 0),
                                            stop=True, skip_group_check=True)
                mx_full.mark(inst)
                mx_reduce(bank, nm[:, t, :, 1, 2 * c:2 * c + 2].rearrange("p j g -> p g j"), 8)
                yield
        mx_out.latest(nc.tensor)
        pro.claim()
        for t in range(2):
            inst = nc.tensor.transpose(bank16[0:W, t * P:t * P + P], nm[:, t, :, :, :].rearrange("p j s g -> p (j s g)"),
                                       pr.ident16[:, :])
        pro.filled(inst)
        pro.drain("a")
        nm_placed.wait_all(nc.scalar, n - 1)
        pro.drained("a", nc.scalar.activation(nmT[:, :], bank16[0:W, 0:T], ACT.Copy))
        pro.out["a"].latest(nc.sync)
        for j in range(4):
            nm_placed.mark(nc.sync.dma_start(QT[p][W * j + NM:W * j + NM + 1, :, :, :],
                                             nmT[8 * j:8 * j + 8, :]))
        yield

    units = [("self", h) for h in range(H)] + [("cross", g) for g in range(G)]

    def scores(n, p, i):
        kind, h = units[i]
        exp_done.wait(nc.tensor, n, i - 1)
        bank = psum[:, 3 + i % 2, :]
        if kind == "self":
            g, j = h // 4, h % 4
            nc.tensor.matmul(bank[:, 0:T], KT[p][:, j, g, 0:P], QT[p][:, 0, g, :], start=True, stop=True)
            inst = nc.tensor.matmul(bank[:, T:T + P], KT[p][:, j, g, P:T], QT[p][:, 0, g, P:T], start=False, stop=True,
                                    skip_group_check=True)
        else:
            for a in range(2):
                inst = nc.tensor.matmul(bank[:, a * T:a * T + T],
                                        KcT[p][:, h, 2 * a:2 * a + 2, :].rearrange("p j t -> p (j t)"),
                                        QT[p][:, 1, h, :], start=(a == 0), stop=True, skip_group_check=True)
        st_full.mark(inst)
        width = T + P if kind == "self" else 2 * T
        st_full.latest(nc.scalar)
        av_done.wait(nc.scalar, n, i - 3)
        exp_done.mark(nc.scalar.activation(prob[i % 4][:, 0:width], bank[:, 0:width], ACT.Exp, scale=SCALE))
        if kind == "self":
            exp_done.latest(nc.gpsimd)
            d = prob[i % 4][:, 0:2 * T].rearrange("p (a q) -> p a q", a=2)[:, :, 0:P]
            sel_done.mark(nc.gpsimd.affine_select(out=d, in_=d, compare_op=ALU.is_ge, fill=0.0, base=0,
                                                  pattern=[[0, 2], [1, P]], channel_multiplier=-1))

    def values(n, p, i):
        kind, h = units[i]
        g = h // 4
        pb = prob[i % 4]
        if kind == "self":
            sel_done.wait(nc.tensor, n, i + 1)
            j, use = h % 4, g // 2
            if h % 8 == 0:
                ys_ready.wait(nc.tensor, n, (0, -1)[use])
            o = psum[32 * j:32 * j + 32, 5 + use, (g % 2) * T:(g % 2) * T + T]
            nc.tensor.matmul(o, V[p][:, 0, h, :], pb[:, 0:T], start=True, stop=False, skip_group_check=True)
            inst = nc.tensor.matmul(o[:, P:T], V[p][:, 1, h, :], pb[:, T:T + P], start=False, stop=True,
                                    skip_group_check=True)
        else:
            use = 2
            exp_done.wait(nc.tensor, n, i + 1)
            if h == 0:
                ys_ready.wait(nc.tensor, n, 1)
            for a in range(2):
                q = 2 * (h % 2) + a
                inst = nc.tensor.matmul(psum[32 * q:32 * q + 32, 5, (h // 2) * T:(h // 2) * T + T],
                                        Vc[p][:, 2 * h + a, :, :].rearrange("p a w -> p (a w)"),
                                        pb[:, a * T:a * T + T], start=True, stop=True, skip_group_check=True)
        av_done.mark(inst)
        if (kind, h) in (("self", 7), ("self", 15), ("cross", 3)):
            av_done.latest(nc.scalar)
            if use == 0:
                epi.full.wait(nc.scalar, n - 1, 3)
            ys_ready.mark(nc.scalar.activation(ysT[:, use, :], psum[:, 5 + use % 2, :], ACT.Copy))

    def epilogue(n, p):
        SE.begin(n)
        for t in range(2):
            ys_ready.wait(nc.tensor, n, 2)
            bank = epi.claim()
            for g in range(G):
                at = (g % 2) * T + t * P
                inst = nc.tensor.transpose(bank[:, g * P:g * P + P], ysT[:, g // 2, at:at + P], pr.ident[:, :])
            epi.filled(inst)
            epi.drain("v")
            heads = bank.rearrange("p (h w) -> p h w", w=W)
            chain_e(nc.vector.reciprocal(den[:, t, :], heads[:, :, D]))
            epi.drained("v", nc.vector.tensor_tensor(y[:, t, :, :], heads[:, :, 0:D],
                                                     den[:, t, :].unsqueeze(2).to_broadcast([P, H, D]), ALU.mult))
            yield
        ys_ready.wait(nc.tensor, n, 3)
        bank = epi.claim()
        for t in range(2):
            for c in range(2):
                inst = nc.tensor.transpose(bank[:, t * T + c * P:t * T + c * P + P],
                                           ysT[:, 2, c * T + t * P:c * T + t * P + P], pr.ident[:, :])
        epi.filled(inst)
        epi.drain("v")
        heads = bank.rearrange("p (t w) -> p t w", w=W // 2)
        denf = denc[:, :, :].rearrange("p t h -> p (t h)")
        chain_e(nc.vector.reciprocal(denf, heads[:, :, D]))
        epi.drained("v", nc.vector.tensor_tensor(yc[:, :, :, :].rearrange("p t h d -> p (t h) d"), heads[:, :, 0:D],
                                                 denf.unsqueeze(2).to_broadcast([P, 2 * H, D]), ALU.mult))
        epi.out["v"].latest(nc.vector)
        flat = lambda m: m[:, :, :, :].rearrange("p t h d -> p (t h d)")
        chain_e(nc.vector.tensor_tensor(flat(y), flat(y), flat(yc), ALU.add))
        yield
        chain_e.event.latest(nc.tensor)
        bank = epi.claim()
        for t in range(2):
            inst = nc.tensor.transpose(bank[:, t * P:t * P + P], y[:, t, :, :].rearrange("p h d -> p (h d)"), pr.ident[:, :])
        epi.filled(inst)
        epi.drain("a")
        epi.drained("a", nc.scalar.activation(yT[:, :], bank[:, 0:T], ACT.Copy))
        yield
        bank = epi.claim()
        for t in range(2):
            inst = nc.tensor.matmul(bank[:, t * P:t * P + P], yT[:, t * P:t * P + P], Wp[:, :], start=(t == 0), stop=True,
                                    skip_group_check=True)
        epi.filled(inst)
        epi.drain("v")
        epi.drained("v", nc.vector.tensor_tensor(res[:, :, :].rearrange("p t c -> p (t c)"), bank[:, 0:T],
                                                 bp[:, :, :].rearrange("p t c -> p (t c)"), ALU.add))
        epi.out["v"].latest(nc.vector)
        dst = xs[:, bass.ds(n * 2, 2), :]
        chain_e(nc.vector.tensor_tensor(dst, dst, res[:, :, :], ALU.add))
        yield

    LAG = 2

    def step(n, p, first, last):
        SM.begin(n)
        pro_gen = None if last else prologue(n + 1, 1 - p)
        epi_gen = None if first else epilogue(n - 1, 1 - p)
        nm_placed.wait_all(nc.tensor, n)
        for i in range(len(units) + LAG):
            if i < len(units):
                scores(n, p, i)
            if i >= LAG:
                values(n, p, i - LAG)
            advance(epi_gen, 1 if i % 2 == 0 else 0)
            advance(pro_gen, 2 if i < 8 or i % 2 else 1)
        finish(epi_gen)
        finish(pro_gen)

    finish(prologue(0, 0))
    pipeline(nc, B, step)
    finish(epilogue(B - 1, (B - 1) % 2))
    pr.fence()


HID = 512
K4 = HID // P
N4 = 4 * P


def feed_forward(pr, mem, tag, src, dst, first, middle, last, out_scale, out_bias):
    nc, psum = pr.nc, pr.psum
    gated = len(first) == 2
    z = pr.sb(tag + "_z", [P, 4, C], F32, mem)
    zT = [pr.sb(f"{tag}_zT{i}", [P, N4], F32, mem) for i in range(2)]
    gate = [pr.sb(f"{tag}_gate{i}", [P, N4], F32, mem) for i in range(2)] if gated else None
    hT = [pr.sb(f"{tag}_hT{i}", [P, K4, N4], F32, mem) for i in range(2)]
    res = pr.sb(tag + "_res", [P, 4, C], F32, mem)
    SP, SM = Stage(pr, tag + "p"), Stage(pr, tag + "m")
    ln = LayerNorm(pr, SP, "ln", 4, mem)
    pro = Bank(SP, "pro", psum[:, 0, :])
    z_ready = SP.counter("z")
    full, out_a, out_v, silu_done = (SM.counter(x) for x in ("full", "out_a", "out_v", "silu"))
    y_full, y_out = SM.counter("y_full"), SM.counter("y_out")
    chain = SM.chain(nc.vector, "chain")
    RING = 4

    def prologue(n, p):
        SP.begin(n)
        tokens = src[:, bass.ds(n * 4, 4), :]
        ln(tokens)
        z_ready.mark(ln.normalise(z, tokens))
        yield
        z_ready.latest(nc.tensor)
        bank = pro.claim()
        for t in range(4):
            inst = nc.tensor.transpose(bank[:, t * P:t * P + P], z[:, t, :], pr.ident[:, :])
        pro.filled(inst)
        pro.drain("v")
        pro.drained("v", nc.vector.tensor_copy(zT[p][:, :], bank))
        yield

    def main(n, p):
        drains = []

        def bank_for():
            u = len(drains)
            if u >= RING:
                s, k = drains[u - RING]
                s.wait(nc.tensor, n, k)
            else:
                out_a.wait(nc.tensor, n, u - RING + 1)
            return psum[:, 1 + u % RING, :]

        def activate(bank, out, func, scale, bias, event):
            full.latest(nc.scalar)
            inst = nc.scalar.activation(out, bank, func, **({"scale": scale} if scale is not None else {}),
                                        **({"bias": bias} if bias is not None else {}))
            return event.mark(inst)

        pro.out["v"].wait_all(nc.tensor, n)
        ready = []
        for m in range(K4):
            if not gated:
                w, scale, bias = first[0]
                bank = bank_for()
                full.mark(nc.tensor.matmul(bank, w[:, m * P:m * P + P], zT[p][:, :], start=True, stop=True))
                k = activate(bank, hT[0][:, m, :], ACT.Gelu, scale, bias[:, m:m + 1], out_a)
                drains.append((out_a, k)), ready.append((out_a, k))
            else:
                (wa, sa, _), (wb, sb, _) = first
                bank = bank_for()
                full.mark(nc.tensor.matmul(bank, wa[:, m * P:m * P + P], zT[p][:, :], start=True, stop=True))
                out_v.latest(nc.scalar) if m >= 2 else None
                k = activate(bank, gate[m % 2][:, :], ACT.Silu, sa[:, m:m + 1], None, out_a)
                drains.append((out_a, k))
                bank = bank_for()
                full.mark(nc.tensor.matmul(bank, wb[:, m * P:m * P + P], zT[p][:, :], start=True, stop=True))
                full.latest(nc.vector), out_a.latest(nc.vector)
                k = out_v.mark(nc.vector.scalar_tensor_tensor(hT[0][:, m, :], bank, sb[:, m:m + 1], gate[m % 2][:, :],
                                                              ALU.mult, ALU.mult))
                drains.append((out_v, k)), ready.append((out_v, k))
            yield
        cur = 0
        for w, scale in middle:
            now = []
            for m in range(K4):
                bank = bank_for()
                for k in range(K4):
                    if m == 0:
                        ready[k][0].wait(nc.tensor, n, ready[k][1])
                    inst = nc.tensor.matmul(bank, w[:, k, m * P:m * P + P], hT[cur][:, k, :],
                                            start=(k == 0), stop=(k == K4 - 1))
                full.mark(inst)
                k = activate(bank, hT[1 - cur][:, m, :], ACT.Gelu, scale[:, m:m + 1], None, out_a)
                drains.append((out_a, k)), now.append((out_a, k))
                yield
            ready, cur = now, 1 - cur
        y_out.wait_all(nc.tensor, n - 1)
        bank = psum[:, 1 + RING, :]
        for t in range(4):
            for k in range(K4):
                if t == 0:
                    ready[k][0].wait(nc.tensor, n, ready[k][1])
                inst = nc.tensor.matmul(bank[:, t * P:t * P + P], hT[cur][:, k, t * P:t * P + P], last[:, k, :],
                                        start=(t == 0 and k == 0), stop=(k == K4 - 1), skip_group_check=True)
        y_full.mark(inst)
        y_full.latest(nc.vector)
        tokens, r = dst[:, bass.ds(n * 4, 4), :], res[:, :, :]
        bank = bank.rearrange("p (t c) -> p t c", t=4)
        if out_scale is not None:
            y_out.mark(nc.vector.tensor_tensor(r, bank, out_scale.unsqueeze(1).to_broadcast([P, 4, C]), ALU.mult))
        else:
            y_out.mark(nc.vector.tensor_tensor(r, bank, out_bias.unsqueeze(1).to_broadcast([P, 4, C]), ALU.add))
        y_out.latest(nc.vector)
        chain(nc.vector.tensor_tensor(tokens, tokens, r, ALU.add))
        yield

    def step(n, p, first_, last_):
        SM.begin(n)
        pro_gen = None if last_ else prologue(n + 1, 1 - p)
        for i, _ in enumerate(main(n, p)):
            if i in (1, 3):
                advance(pro_gen)
        finish(pro_gen)

    finish(prologue(0, 0))
    pipeline(nc, TILES // 4, step)
    pr.fence()


def l0_ffn_weights(pr, mem):
    io, w = pr.io, {}
    sem = pr.nc.alloc_semaphore("l0f_w")
    for name, shape in (("w1_w", [P, HID]), ("w2_w", [P, HID]), ("h1_w", [P, K4, HID]), ("h2_w", [P, K4, HID]),
                        ("w3_w", [P, K4, C]), ("w1_s", [P, K4]), ("w2_s", [P, K4]), ("h1_s", [P, K4]),
                        ("h2_s", [P, K4])):
        w[name] = pr.sb("f_" + name, shape, F32, mem)
        load(pr, w[name][...], io["L0_ffn_" + name], sem)
    w["w3_s"] = pr.sb("f_w3s", [P, C], F32, mem)
    load(pr, w["w3_s"][:, :], io["L0_ffn_w3_s"].partition_broadcast(P), sem)
    return w, (sem, 160)


def l0_ffn(pr, mem):
    w, (sem, v) = l0_ffn_weights(pr, mem)
    pr.nc.sync.wait_ge(sem, v)
    pr.fence()
    feed_forward(pr, mem, "f", pr.x, pr.x, [(w["w1_w"], w["w1_s"], None), (w["w2_w"], w["w2_s"], None)],
                 [(w["h1_w"], w["h1_s"]), (w["h2_w"], w["h2_s"])], w["w3_w"], w["w3_s"][:, :], None)


def fold_weights(pr, mem, tag, weights, biases):
    nc, psum = pr.nc, pr.psum
    sv, sp = (pr.nc.alloc_semaphore(tag + x) for x in ("_fold_v", "_fold_p"))
    wide = pr.sb(tag + "_offset", [P, P], F32, mem)
    v = 0
    for n, (w, gain, offset, out, plus) in enumerate(weights):
        rows, by_token = w.shape[0], out.shape[1] == HID
        bank = psum[:, n % 8, :]
        if by_token:
            if n:
                nc.vector.wait_ge(sp, n)
            v += 1
            nc.vector.tensor_copy(wide[0:rows, :], offset.to_broadcast([rows, P])).then_inc(sv, 1)
            nc.tensor.wait_ge(sv, v)
            nc.tensor.matmul(bank, wide[0:rows, :], w, start=True, stop=True).then_inc(sp, 1)
            nc.vector.wait_ge(sp, n + 1)
            v += 1
            nc.vector.tensor_copy(out, bank).then_inc(sv, 1)
        else:
            for m in range(K4):
                inst = nc.tensor.matmul(bank[:, m:m + 1], w[:, m * P:m * P + P], offset, start=(m == 0), stop=True,
                                        skip_group_check=True)
            inst.then_inc(sp, 1)
            nc.vector.wait_ge(sp, n + 1)
            v += 1
            nc.vector.tensor_tensor(out, bank[:, 0:K4], plus, ALU.add).then_inc(sv, 1)
        v += 1
        nc.vector.tensor_scalar(w, w, gain, None, ALU.mult).then_inc(sv, 1)


def mha_weights(pr, mem, tag, pre, norm):
    io, w = pr.io, {}
    ck = C if pre == "a1" else CC
    sem = pr.nc.alloc_semaphore(tag + "_w")
    q = lambda x: io[f"L1_xattn_{x}"]
    for name, rows in (("wq", C), ("wk", ck), ("wv", ck)):
        w[name] = pr.sb(f"{tag}_{name}", [rows, HID], F32, mem)
        load(pr, w[name][:, :], q(f"{pre}_{name}"), sem)
    w["li1"] = pr.sb(tag + "_li1", [P, K4, C], F32, mem)
    load(pr, w["li1"][:, :, :], q(pre + "_li1_w"), sem)
    for name, src, rows in (("gx", "lnx_g", C), ("bx", "lnx_b", C), ("gy", "lny_g", ck), ("by", "lny_b", ck)):
        w[name] = pr.sb(f"{tag}_{name}", [rows, 1], F32, mem)
        load(pr, w[name][:, :], q(f"{pre}_{src}").unsqueeze(1), sem)
    for name, src in (("li1_b", pre + "_li1_b"), ("g", norm + "_g"), ("b", norm + "_b")):
        w[name] = pr.sb(f"{tag}_{name}_row", [P, C], F32, mem)
        load(pr, w[name][:, :], q(src).partition_broadcast(P), sem)
    for name in ("bq", "bk", "bv"):
        w[name] = pr.sb(f"{tag}_{name}", [P, HID], F32, mem)
    return w, (sem, 11 * 16)


def mha_attention(pr, mem, tag, own):
    nc, psum = pr.nc, pr.psum
    D, G = 32, 4
    R = 3 * D + 1
    NM = 3 * D
    RP = R + 1
    SCALE = float(D) ** -0.5
    w, (sem, v) = mha_weights(pr, mem, tag, "a1" if own else "a2", "ln1" if own else "ln2")
    nc.sync.wait_ge(sem, v)
    pr.fence()
    fold_weights(pr, mem, tag, [(w["wq"][:, :], w["gx"][:, :], w["bx"][:, :], w["bq"][:, :], None),
                                (w["wk"][:, :], w["gy"][:, :], w["by"][:, :], w["bk"][:, :], None),
                                (w["wv"][:, :], w["gy"][:, :], w["by"][:, :], w["bv"][:, :], None)], None)
    z = pr.sb(tag + "_z", [P, 2, C], F32, mem)
    zT = pr.sb(tag + "_zT", [P, T], F32, mem)
    qf = [pr.sb(f"{tag}_qf{i}", [P, HID], F32, mem) for i in range(2)]
    qtok = pr.sb(tag + "_qtok", [P, 2, H, RP], F16, mem)
    ktok = pr.sb(tag + "_ktok", [P, 2 if own else 1, H, RP], F16, mem)
    KW = T if own else TC
    QT = [pr.sb(f"{tag}_QT{i}", [R, H, T], F16, mem) for i in range(2)]
    KT = [pr.sb(f"{tag}_KT{i}", [R, H, KW], F16, mem) for i in range(2)]
    nm = pr.sb(tag + "_nm", [P, 2, H], F16, mem)
    nmT = pr.sb(tag + "_nmT", [H, T], F16, mem)
    prob = [pr.sb(f"{tag}_prob{i}", [P, 2 * T], F32, mem) for i in range(4)]
    late = [pr.sb(f"{tag}_late{i}", [P, 2, P], F32, mem) for i in range(4)] if own else None
    ndT = pr.sb(tag + "_ndT", [P, G, 2 * T], F32, mem)
    rden = pr.sb(tag + "_rden", [P, 2, H], F32, mem)
    o = pr.sb(tag + "_o", [P, 2, H, D], F32, mem)
    oT = pr.sb(tag + "_oT", [P, G, T], F32, mem)
    res = pr.sb(tag + "_res", [P, 2, C], F32, mem)
    if own:
        V = [pr.sb(f"{tag}_V{i}", [P, 2, HID], F32, mem) for i in range(2)]
        zeroed = []
        sums = pr.ones[:, 0:D]
    else:
        V = [pr.sb(f"{tag}_V{i}", [P, H // 2, 2, D], F32, mem) for i in range(2)]
        pair_ones = pr.sb(tag + "_pair_ones", [P, 2, D], F32, mem)
        zeroed = [*V, pair_ones]
        sums = pair_ones[:, :, :].rearrange("p a d -> p (a d)")
        zc = pr.sb(tag + "_zc", [P, 1, CC], F32, mem)
        cT = pr.sb(tag + "_cT", [CC, P], F32, mem)
    s0 = pr.nc.alloc_semaphore(tag + "_init")
    for m in [*zeroed, qtok, ktok]:
        inst = nc.vector.memset(m[...], 0.0)
    inst.then_inc(s0, 1)
    nc.vector.wait_ge(s0, 1)
    if not own:
        for a in range(2):
            nc.vector.memset(pair_ones[TC * a:TC * a + TC, a, :], 1.0)
    nc.vector.memset(ktok[:, :, :, NM:NM + 1], 1.0).then_inc(s0, 1)
    nc.vector.wait_ge(s0, 2)
    pr.fence()

    SP, SM, SE = Stage(pr, tag + "p"), Stage(pr, tag + "m"), Stage(pr, tag + "e")
    ln_in = LayerNorm(pr, SP, "lni", 2, mem, twice=own)
    ln_x = LayerNorm(pr, SP, "lnx", 2, mem)
    ln_c = None if own else LayerNorm(pr, SP, "lnc", 1, mem)
    pro = Bank(SP, "pro", psum[:, 0, :])
    bank16 = psum[:, 0, :].bitcast(F16)
    z_ready, high, low = (SP.counter(x) for x in ("z", "high", "low"))
    chain_p = SP.chain(nc.vector, "chain")
    mx_full, mx_out = SP.counter("mx_full"), SP.counter("mx_out")
    nm_placed = SP.counter("nm_placed", 16)
    st_full, exp_done, sel_done, av_done, nd_ready = (SM.counter(x) for x in ("st_full", "exp", "sel", "av", "nd"))
    epi = Bank(SE, "epi", psum[:, 7, :])
    chain_e = SE.chain(nc.vector, "chain")
    src, u, xo, xs = (pr.x if own else pr.u), pr.u, pr.xo, pr.x
    two = lambda m, n: m[:, bass.ds(n * 2, 2), :]
    row2 = lambda m: m[:, :].unsqueeze(1).to_broadcast([P, 2, C])

    def stack(bank, bias, dst, turn, key, rows=P):
        pro.drain("v")
        f = qf[turn][0:rows, :]
        low.wait(nc.vector, SP.n, low.k - 1)
        pro.drained("v", nc.vector.tensor_tensor(f, bank[0:rows, :], bias[0:rows, :], ALU.add))
        pro.out["v"].latest(nc.scalar)
        f3 = f.rearrange("p (h d) -> p h d", d=D)
        d3 = dst[:, :, 0:NM].rearrange("p h (k d) -> p h k d", d=D)
        twice = d3[:, :, 0:2, :] if key else d3[:, :, 0:3:2, :]
        high.mark(nc.scalar.activation(twice, f3.unsqueeze(2).to_broadcast([rows, H, 2, D]), ACT.Copy))
        high.latest(nc.gpsimd)
        low.mark(nc.gpsimd.tensor_tensor(d3[:, :, 2 if key else 1, :], f3, d3[:, :, 0, :], ALU.subtract))

    def turned(tok, out, rows, width, who):
        pro.claim(apart=rows < P)
        for h in range(8):
            inst = nc.tensor.transpose(bank16[0:R, h * width:h * width + width], tok[:, h, 0:R],
                                       pr.ident16[0:rows, 0:rows])
        pro.filled(inst)
        pro.drain(who)
        source = bank16[0:R, 0:8 * width].rearrange("p (h t) -> p h t", h=8)
        pro.drained(who, nc.vector.tensor_copy(out, source) if who == "v" else
                    nc.scalar.activation(out, source, ACT.Copy))

    def prologue(n, p):
        SP.begin(n)
        un = two(u, n)
        ln_in(two(src, n))
        chain_p(ln_in.normalise(z, two(src, n)))
        chain_p(nc.vector.tensor_tensor(z[:, :, :], z[:, :, :], row2(w["g"]), ALU.mult))
        chain_p(nc.vector.tensor_tensor(un, z[:, :, :], row2(w["b"]), ALU.add))
        yield
        ln_x(un)
        z_ready.mark(ln_x.normalise(z, un))
        if not own:
            cn = pr.ctx2[:, bass.ds(n, 1), :]
            ln_c(cn)
            z_ready.mark(ln_c.normalise(zc, cn))
        yield
        z_ready.latest(nc.tensor)
        bank = pro.claim()
        for t in range(2):
            inst = nc.tensor.transpose(bank[:, t * P:t * P + P], z[:, t, :], pr.ident[:, :])
        if not own:
            inst = nc.tensor.transpose(bank[0:CC, T:T + P], zc[:, 0, :], pr.ident[:, :])
        pro.filled(inst)
        pro.drain("a")
        if not own:
            nc.scalar.activation(cT[:, :], bank[0:CC, T:T + P], ACT.Copy)
        pro.drained("a", nc.scalar.activation(zT[:, :], bank[:, 0:T], ACT.Copy))
        yield
        turn = 0
        for t in range(2):
            zt = zT[:, t * P:t * P + P]
            bank = pro.claim()
            pro.filled(nc.tensor.matmul(bank, zt, w["wq"][:, :], start=True, stop=True))
            stack(bank, w["bq"], qtok[:, t, :, :], turn, False)
            turn ^= 1
            yield
            if own:
                bank = pro.claim()
                pro.filled(nc.tensor.matmul(bank, zt, w["wk"][:, :], start=True, stop=True))
                stack(bank, w["bk"], ktok[:, t, :, :], turn, True)
                turn ^= 1
                yield
                bank = pro.claim()
                pro.filled(nc.tensor.matmul(bank, zt, w["wv"][:, :], start=True, stop=True))
                pro.drain("v")
                pro.drained("v", nc.vector.tensor_tensor(V[p][:, t, :], bank, w["bv"][:, :], ALU.add))
                yield
        if not own:
            bank = pro.claim()
            pro.filled(nc.tensor.matmul(bank, cT[:, :], w["wk"][:, :], start=True, stop=True))
            stack(bank, w["bk"], ktok[0:TC, 0, :, :], turn, True, TC)
            yield
            bank = pro.claim()
            pro.filled(nc.tensor.matmul(bank, cT[:, :], w["wv"][:, :], start=True, stop=True))
            pro.drain("v")
            for a in range(2):
                half = slice(TC * a, TC * a + TC)
                pick = lambda m: m[half, :].rearrange("p (i a d) -> p i a d", a=2, d=D)[:, :, a, :]
                inst = nc.vector.tensor_tensor(V[p][half, :, a, :], pick(bank), pick(w["bv"]), ALU.add)
            pro.drained("v", inst)
            yield
        low.latest(nc.tensor)
        for t in range(2):
            for e in range(2):
                turned(qtok[:, t, 8 * e:8 * e + 8, :], QT[p][:, 8 * e:8 * e + 8, t * P:t * P + P], P, P, "av"[e])
                yield
                if own:
                    turned(ktok[:, t, 8 * e:8 * e + 8, :], KT[p][:, 8 * e:8 * e + 8, t * P:t * P + P], P, P, "va"[e])
                    yield
        if not own:
            for e in range(2):
                turned(ktok[0:TC, 0, 8 * e:8 * e + 8, :], KT[p][:, 8 * e:8 * e + 8, :], TC, TC, "av"[e])
            yield
        pro.claim()

        def mx_use(matmuls, out, groups):
            mx_out.wait(nc.tensor, n, mx_full.k - 1)
            bank = psum[:, 1 + mx_full.k % 2, :]
            for i, (at, width, lhsT, rhs) in enumerate(matmuls):
                inst = nc.tensor.matmul(bank[:, at:at + width], lhsT, rhs, start=(i == 0), stop=True,
                                        skip_group_check=True)
            mx_full.mark(inst)
            mx_full.latest(nc.vector)
            mx_out.mark(nc.vector.tensor_reduce(out, bank.rearrange("p (a b) -> p a b", a=groups), X, ALU.max,
                                                negate=True))

        if own:
            for h in range(H):
                mx_use([(t * T, T, QT[p][:, h, t * P:t * P + P], KT[p][:, h, :]) for t in range(2)], nm[:, :, h], 2)
                yield
        else:
            for t in range(2):
                for e in range(2):
                    mx_use([(i * TC, TC, QT[p][:, 8 * e + i, t * P:t * P + P], KT[p][:, 8 * e + i, :])
                            for i in range(8)], nm[:, t, 8 * e:8 * e + 8], 8)
                    yield
        mx_out.latest(nc.tensor)
        pro.claim()
        for t in range(2):
            inst = nc.tensor.transpose(bank16[0:H, t * P:t * P + P], nm[:, t, :], pr.ident16[:, :])
        pro.filled(inst)
        pro.drain("a")
        nm_placed.wait_all(nc.scalar, n - 1)
        pro.drained("a", nc.scalar.activation(nmT[:, :], bank16[0:H, 0:T], ACT.Copy))
        pro.out["a"].latest(nc.sync)
        nm_placed.mark(nc.sync.dma_start(QT[p][NM:NM + 1, :, :], nmT[:, :]))
        yield

    units = H if own else G

    def scores(n, p, i):
        exp_done.wait(nc.tensor, n, i - 1)
        bank = psum[:, 3 + i % 2, :]
        if own:
            for kb in range(2):
                inst = nc.tensor.matmul(bank[:, kb * T:kb * T + T], KT[p][:, i, kb * P:kb * P + P], QT[p][:, i, :],
                                        start=(kb == 0), stop=True, skip_group_check=True)
        else:
            for j in range(4):
                a, pair = j % 2, j // 2
                inst = nc.tensor.matmul(bank[TC * a:TC * a + TC, pair * T:pair * T + T], KT[p][:, 4 * i + j, :],
                                        QT[p][:, 4 * i + j, :], start=(pair == 0), stop=True, skip_group_check=True)
        st_full.mark(inst)
        st_full.latest(nc.scalar)
        av_done.wait(nc.scalar, n, i - 3)
        exp_done.mark(nc.scalar.activation(prob[i % 4][:, :], bank, ACT.Exp, scale=SCALE))
        if own:
            exp_done.latest(nc.gpsimd)
            av_done.wait(nc.gpsimd, n, i - 3)
            pm = prob[i % 4][:, :]
            for b, at in enumerate((0, T + P)):
                inst = nc.gpsimd.affine_select(out=late[i % 4][:, b, :], in_=pm[:, at:at + P], compare_op=ALU.is_gt,
                                               fill=0.0, base=0, pattern=[[-1, P]], channel_multiplier=1)
            sel_done.mark(inst)

    def values(n, p, i):
        g = i // 4 if own else i
        j = i % 4
        pb = prob[i % 4]
        bank = psum[:, 5 + g % 2, :]
        if j == 0 or not own:
            nd_ready.wait(nc.tensor, n, g - 1)
        exp_done.wait(nc.tensor, n, i + 1)
        if own:
            o_ = bank[32 * j:32 * j + 32, :]
            for kb in range(2):
                nc.tensor.matmul(o_[:, T:2 * T], sums, pb[:, kb * T:kb * T + T], start=(kb == 0), stop=(kb == 1),
                                 skip_group_check=True)
            sel_done.wait(nc.tensor, n, i + 1)
            vh = lambda kb: V[p][:, kb, i * D:i * D + D]
            nc.tensor.matmul(o_[:, 0:P], vh(1), pb[:, T:T + P], start=True, stop=False, skip_group_check=True)
            nc.tensor.matmul(o_[:, P:T], vh(1), late[i % 4][:, 1, :], start=False, stop=True, skip_group_check=True)
            inst = nc.tensor.matmul(o_[:, 0:P], vh(0), late[i % 4][:, 0, :], start=False, stop=True,
                                    skip_group_check=True)
        else:
            for pair in range(2):
                o_ = bank[64 * pair:64 * pair + 64, :]
                q = pb[:, pair * T:pair * T + T]
                nc.tensor.matmul(o_[:, T:2 * T], sums, q, start=True, stop=True, skip_group_check=True)
                inst = nc.tensor.matmul(o_[:, 0:T], V[p][:, 2 * i + pair, :, :].rearrange("p a d -> p (a d)"), q,
                                        start=True, stop=True, skip_group_check=True)
        av_done.mark(inst)
        if j == 3 or not own:
            av_done.latest(nc.scalar)
            if g == 0:
                epi.full.wait(nc.scalar, n - 1, 5)
            nd_ready.mark(nc.scalar.activation(ndT[:, g, :], bank, ACT.Copy))

    def epilogue(n, p):
        SE.begin(n)
        nd_ready.wait(nc.tensor, n, G)
        for t in range(2):
            bank = epi.claim()
            for g in range(G):
                inst = nc.tensor.transpose(bank[:, g * P:g * P + P], ndT[:, g, T + t * P:T + t * P + P], pr.ident[:, :])
            epi.filled(inst)
            epi.drain("v")
            epi.drained("v", nc.vector.reciprocal(rden[:, t, :], bank.rearrange("p (h d) -> p h d", d=D)[:, :, 0]))
            yield
            bank = epi.claim()
            for g in range(G):
                inst = nc.tensor.transpose(bank[:, g * P:g * P + P], ndT[:, g, t * P:t * P + P], pr.ident[:, :])
            epi.filled(inst)
            epi.drain("v")
            epi.out["v"].latest(nc.vector)
            epi.drained("v", nc.vector.tensor_tensor(o[:, t, :, :], bank.rearrange("p (h d) -> p h d", d=D),
                                                     rden[:, t, :].unsqueeze(2).to_broadcast([P, H, D]), ALU.mult))
            yield
            bank = epi.claim()
            flat = o[:, t, :, :].rearrange("p h d -> p (h d)")
            for g in range(G):
                inst = nc.tensor.transpose(bank[:, g * P:g * P + P], flat[:, g * P:g * P + P], pr.ident[:, :])
            epi.filled(inst)
            epi.drain("a")
            epi.drained("a", nc.scalar.activation(oT[:, :, t * P:t * P + P], bank.rearrange("p (g t) -> p g t", g=G),
                                                  ACT.Copy))
            yield
        bank = epi.claim()
        for t in range(2):
            for g in range(G):
                inst = nc.tensor.matmul(bank[:, t * P:t * P + P], oT[:, g, t * P:t * P + P], w["li1"][:, g, :],
                                        start=(t == 0 and g == 0), stop=(g == G - 1), skip_group_check=True)
        epi.filled(inst)
        epi.drain("v")
        un, xon, xn, r = two(u, n), two(xo, n), two(xs, n), res[:, :, :]
        epi.drained("v", nc.vector.tensor_tensor(r, bank[:, 0:T].rearrange("p (t c) -> p t c", t=2), row2(w["li1_b"]),
                                                 ALU.add))
        epi.out["v"].latest(nc.vector)
        chain_e(nc.vector.tensor_tensor(xon, un, r, ALU.add))
        if own:
            chain_e(nc.vector.tensor_tensor(un, un, xon, ALU.add))
        else:
            chain_e(nc.vector.tensor_tensor(r, un, xon, ALU.add))
            chain_e(nc.vector.tensor_tensor(xn, xn, r, ALU.add))
        yield

    LAG = 2 if own else 1

    def step(n, p, first, last):
        SM.begin(n)
        pro_gen = None if last else prologue(n + 1, 1 - p)
        epi_gen = None if first else epilogue(n - 1, 1 - p)
        nm_placed.wait_all(nc.tensor, n)
        for i in range(units + LAG):
            if i < units:
                scores(n, p, i)
            if i >= LAG:
                values(n, p, i - LAG)
            if own:
                advance(epi_gen)
                advance(pro_gen, 2)
            else:
                advance(epi_gen, 5)
                advance(pro_gen, 3)
        finish(epi_gen)
        finish(pro_gen)

    finish(prologue(0, 0))
    pipeline(nc, B, step)
    finish(epilogue(B - 1, (B - 1) % 2))
    pr.fence()


def mha_ffn(pr, mem, tag, pre, dst):
    nc, io = pr.nc, pr.io
    q = lambda x: io[f"L1_xattn_{pre}_{x}"]
    sem = pr.nc.alloc_semaphore(tag + "_w")
    li2 = pr.sb(tag + "_li2", [P, HID], F32, mem)
    li3 = pr.sb(tag + "_li3", [P, K4, C], F32, mem)
    cols = pr.sb(tag + "_cols", [P, 2, 1], F32, mem)
    b2 = pr.sb(tag + "_b2", [P, K4], F32, mem)
    bias = pr.sb(tag + "_bias", [P, K4], F32, mem)
    b3 = pr.sb(tag + "_b3", [P, C], F32, mem)
    load(pr, li2[:, :], q("li2_w"), sem)
    load(pr, li3[:, :, :], q("li3_w"), sem)
    load(pr, cols[:, 0, :], q("ln3_g").unsqueeze(1), sem)
    load(pr, cols[:, 1, :], q("ln3_b").unsqueeze(1), sem)
    load(pr, b2[:, :], q("li2_b"), sem)
    load(pr, b3[:, :], q("li3_b").partition_broadcast(P), sem)
    nc.sync.wait_ge(sem, 96)
    pr.fence()
    fold_weights(pr, mem, tag, [(li2[:, :], cols[:, 0, :], cols[:, 1, :], bias[:, :], b2[:, :])], None)
    pr.fence()
    feed_forward(pr, mem, tag, pr.xo, dst, [(li2, None, bias)], [], li3, None, b3[:, :])


E = 8
CAP = 640
CT = CAP // P


def moe(pr, mem):
    nc, io, psum, xn = pr.nc, pr.io, pr.psum, pr.u
    tokens_in = nc.dram_tensor("expert_in", [E * CAP + TILES * P, C], F32).ap()
    tokens_out = nc.dram_tensor("expert_out", [E * CAP, C], F32).ap()
    sem = pr.nc.alloc_semaphore("m_w")
    gate_w = pr.sb("m_gate_w", [P, E], F32, mem)
    gate_b = pr.sb("m_gate_b", [P, E], F32, mem)
    logits = pr.sb("m_logits", [P, TILES, E], F32, mem)
    load(pr, gate_w[:, :], io["gate_wT"], sem)
    load(pr, gate_b[:, :], io["L1_ffn_gate_b"].partition_broadcast(P), sem)
    nc.sync.wait_ge(sem, 32)

    zero = pr.sb("m_zero", [P, CT, C], F32, mem)
    s_zero, s_zeroed = pr.nc.alloc_semaphore("m_z0"), pr.nc.alloc_semaphore("m_z1")
    nc.vector.memset(zero[:, :, :], 0.0).then_inc(s_zero, 1)
    nc.sync.wait_ge(s_zero, 1)
    by_tile = lambda m, e: m[bass.ds(e * CAP, CAP), :].rearrange("(t p) c -> p t c", p=P)
    with nc.sync.Fori(0, E) as e:
        nc.sync.dma_start(by_tile(tokens_in, e), zero[:, :, :]).then_inc(s_zeroed, 16)
    pr.fence()

    SP, SM = Stage(pr, "mp"), Stage(pr, "mm")
    ln = LayerNorm(pr, SP, "ln", 4, mem)
    z = pr.sb("m_z", [P, 4, C], F32, mem)
    zT = pr.sb("m_zT", [P, N4], F32, mem)
    pro, out = Bank(SP, "pro", psum[:, 0, :]), Bank(SP, "out", psum[:, 1, :])
    z_ready, copied = SP.counter("z"), SP.counter("copied")

    def route(n, p, first, last):
        SP.begin(n)
        tokens = pr.x[:, bass.ds(n * 4, 4), :]
        ln(tokens)
        copied.wait_all(nc.vector, n - 1)
        z_ready.mark(ln.normalise(z, tokens))
        z_ready.latest(nc.scalar)
        copied.mark(nc.scalar.activation(xn[:, bass.ds(n * 4, 4), :], z[:, :, :], ACT.Copy))
        z_ready.latest(nc.tensor)
        bank = pro.claim()
        for t in range(4):
            inst = nc.tensor.transpose(bank[:, t * P:t * P + P], z[:, t, :], pr.ident[:, :])
        pro.filled(inst)
        pro.drain("v")
        pro.drained("v", nc.vector.tensor_copy(zT[:, :], bank))
        pro.out["v"].latest(nc.tensor)
        bank = out.claim()
        for t in range(4):
            inst = nc.tensor.matmul(bank[:, t * E:t * E + E], zT[:, t * P:t * P + P], gate_w[:, :], start=(t == 0),
                                    stop=True, skip_group_check=True)
        out.filled(inst)
        out.drain("v")
        out.drained("v", nc.vector.tensor_tensor(logits[:, bass.ds(n * 4, 4), :],
                                                 bank[:, 0:4 * E].rearrange("p (t e) -> p t e", e=E),
                                                 gate_b[:, :].unsqueeze(1).to_broadcast([P, 4, E]), ALU.add))

    pipeline(nc, TILES // 4, route)
    pr.fence()

    small = lambda name, *shape: pr.sb("m_" + name, [P, *shape], F32, mem)
    d, pe_, pick, hot, count, scan = (small(x, TILES, E) for x in ("d", "pe", "pick", "hot", "count", "scan"))
    iota_e, tri, token = small("iota_e", TILES, E), small("tri", P), small("token", TILES)
    top, total, idx, place, keep, gate, row, back, tmp = (
        small(x, TILES) for x in ("top", "total", "idx", "place", "keep", "gate", "row", "back", "tmp"))
    iota_i = pr.sb("m_iota_i", [P, TILES, E], mybir.dt.int32, mem)
    token_i = pr.sb("m_token_i", [P, TILES], mybir.dt.int32, mem)
    row_u, back_u = pr.sb("m_row_u", [P, TILES], U32, mem), pr.sb("m_back_u", [P, TILES], U32, mem)
    sv, sg, st_, sa = (pr.nc.alloc_semaphore("m_" + x) for x in ("v", "g", "t", "a"))
    nv = [0]

    def v(inst):
        nv[0] += 1
        inst.then_inc(sv, 1)
        nc.vector.wait_ge(sv, nv[0])

    wide = lambda m: m[:, :].unsqueeze(2).to_broadcast([P, TILES, E])
    flat = lambda m: m[:, :, :].rearrange("p t e -> p (t e)")
    nc.gpsimd.iota(iota_i[:, :, :], [[0, TILES], [1, E]], base=0, channel_multiplier=0).then_inc(sg, 1)
    nc.gpsimd.iota(token_i[:, :], [[P, TILES]], base=0, channel_multiplier=1).then_inc(sg, 1)
    nc.gpsimd.affine_select(out=tri[:, :], in_=pr.ones[:, :], compare_op=ALU.is_ge, fill=0.0, base=0,
                            pattern=[[1, P]], channel_multiplier=-1).then_inc(sg, 1)
    v(nc.vector.tensor_reduce(tmp[:, :], logits[:, :, :], X, ALU.max))
    v(nc.vector.tensor_tensor(d[:, :, :], logits[:, :, :], wide(tmp), ALU.subtract))
    nc.scalar.wait_ge(sv, nv[0])
    nc.scalar.activation(pe_[:, :, :], d[:, :, :], ACT.Exp).then_inc(sa, 1)
    nc.vector.wait_ge(sg, 3)
    v(nc.vector.tensor_copy(iota_e[:, :, :], iota_i[:, :, :]))
    v(nc.vector.tensor_copy(token[:, :], token_i[:, :]))
    v(nc.vector.tensor_scalar(pick[:, :, :], d[:, :, :], 0.0, float(E), ALU.is_ge, ALU.mult))
    v(nc.vector.tensor_tensor(pick[:, :, :], iota_e[:, :, :], pick[:, :, :], ALU.subtract))
    v(nc.vector.tensor_reduce(idx[:, :], pick[:, :, :], X, ALU.min))
    v(nc.vector.tensor_tensor(hot[:, :, :], pick[:, :, :], wide(idx), ALU.is_equal))
    nc.tensor.wait_ge(sv, nv[0])
    nc.tensor.wait_ge(sg, 3)
    nc.tensor.matmul(psum[:, 0, 0:TILES * E], tri[:, :], flat(hot), start=True, stop=True)
    nc.tensor.matmul(psum[:, 1, 0:TILES * E], pr.ones[:, :], flat(hot), start=True, stop=True).then_inc(st_, 1)
    nc.vector.wait_ge(sa, 1)
    v(nc.vector.tensor_reduce(total[:, :], pe_[:, :, :], X, ALU.add))
    v(nc.vector.reciprocal(top[:, :], total[:, :]))
    nc.vector.wait_ge(st_, 1)
    v(nc.vector.tensor_copy(flat(count), psum[:, 1, 0:TILES * E]))
    for e in range(E):
        inst = nc.vector.tensor_tensor_scan(scan[:, :, e], pr.ones[:, 0:TILES], count[:, :, e], 0.0, ALU.mult, ALU.add)
    v(inst)
    v(nc.vector.tensor_tensor(scan[:, :, :], scan[:, :, :], count[:, :, :], ALU.subtract))
    v(nc.vector.tensor_tensor(flat(count), psum[:, 0, 0:TILES * E], flat(scan), ALU.add))
    v(nc.vector.tensor_tensor(count[:, :, :], count[:, :, :], hot[:, :, :], ALU.mult))
    v(nc.vector.tensor_reduce(place[:, :], count[:, :, :], X, ALU.add))
    v(nc.vector.tensor_scalar(place[:, :], place[:, :], -1.0, None, ALU.add))
    v(nc.vector.tensor_scalar(keep[:, :], place[:, :], float(CAP), None, ALU.is_lt))
    v(nc.vector.tensor_tensor(gate[:, :], top[:, :], keep[:, :], ALU.mult))
    v(nc.vector.tensor_scalar(idx[:, :], idx[:, :], float(E), float(CAP), ALU.add, ALU.mult))
    v(nc.vector.tensor_tensor(tmp[:, :], place[:, :], keep[:, :], ALU.mult))
    v(nc.vector.tensor_tensor(back[:, :], idx[:, :], tmp[:, :], ALU.add))
    v(nc.vector.tensor_scalar(token[:, :], token[:, :], float(E * CAP), None, ALU.add))
    v(nc.vector.tensor_tensor(tmp[:, :], back[:, :], token[:, :], ALU.subtract))
    v(nc.vector.tensor_tensor(tmp[:, :], tmp[:, :], keep[:, :], ALU.mult))
    v(nc.vector.tensor_tensor(row[:, :], tmp[:, :], token[:, :], ALU.add))
    v(nc.vector.tensor_copy(row_u[:, :], row[:, :]))
    v(nc.vector.tensor_copy(back_u[:, :], back[:, :]))

    s_there = pr.nc.alloc_semaphore("m_there")
    nc.gpsimd.wait_ge(sv, nv[0])
    nc.gpsimd.wait_ge(s_zeroed, 16 * E)
    for t in range(TILES):
        nc.gpsimd.indirect_dma_start(out=tokens_in, out_offset=bass.IndirectOffsetOnAxis(ap=row_u[:, t:t + 1], axis=0),
                                     in_=xn[:, t, :], in_offset=None).then_inc(s_there, 16)
    nc.sync.wait_ge(s_there, 16 * TILES)

    w1 = [pr.sb(f"m_w1_{i}", [P, HID], F32, mem) for i in range(2)]
    w2 = [pr.sb(f"m_w2_{i}", [P, K4, C], F32, mem) for i in range(2)]
    b1 = [pr.sb(f"m_b1_{i}", [P, K4], F32, mem) for i in range(2)]
    b2 = [pr.sb(f"m_b2_{i}", [P, C], F32, mem) for i in range(2)]
    xt = [pr.sb(f"m_xt{i}", [P, CT, C], F32, mem) for i in range(2)]
    xT = [pr.sb(f"m_xT{i}", [P, CAP], F32, mem) for i in range(2)]
    hT = pr.sb("m_hT", [P, K4, CAP], F32, mem)
    ys = pr.sb("m_ys", [P, CT, C], F32, mem)
    SL, SX = Stage(pr, "el"), Stage(pr, "ex")
    loaded = SL.counter("loaded", 16)
    xT_full, xT_out = SL.counter("xT_full"), SL.counter("xT_out")
    h_full, h_out, y_full, y_out = (SX.counter(x) for x in ("h_full", "h_out", "y_full", "y_out"))
    stored = SX.counter("stored", 16)
    HALF = CAP // 2

    def fetch(n, p):
        SL.begin(n)
        y_out.wait_all(nc.sync, n - 2)
        loaded.wait_all(nc.sync, n - 1)
        one = lambda name: io["L1_ffn_" + name][bass.ds(n, 1), :, :].rearrange("e p f -> (e p) f")
        loaded.mark(nc.sync.dma_start(xt[p][:, :, :], by_tile(tokens_in, n)))
        loaded.mark(nc.sync.dma_start(w1[p][:, :], one("w1")))
        loaded.mark(nc.sync.dma_start(b1[p][:, :], one("b1")))
        loaded.mark(nc.sync.dma_start(w2[p][:, :, :].rearrange("p k c -> p (k c)"), one("w2")))
        loaded.mark(nc.sync.dma_start(b2[p][:, :], one("b2").partition_broadcast(P).rearrange("q e c -> q (e c)")))
        yield
        loaded.wait_all(nc.tensor, n)
        xT_out.wait_all(nc.tensor, n - 1)
        for t in range(CT):
            inst = nc.tensor.transpose(psum[:, t // 4, (t % 4) * P:(t % 4) * P + P], xt[p][:, t, :], pr.ident[:, :])
        xT_full.mark(inst)
        xT_full.latest(nc.vector)
        nc.vector.tensor_copy(xT[p][:, 0:N4], psum[:, 0, :])
        xT_out.mark(nc.vector.tensor_copy(xT[p][:, N4:CAP], psum[:, 1, 0:CAP - N4]))
        yield

    def expert(n, p):
        SX.begin(n)
        xT_out.wait_all(nc.tensor, n)
        for m in range(K4):
            h_out.wait(nc.tensor, n, m - 1)
            b = 2 + 2 * (m % 2)
            for half in range(2):
                inst = nc.tensor.matmul(psum[:, b + half, 0:HALF], w1[p][:, m * P:m * P + P],
                                        xT[p][:, half * HALF:half * HALF + HALF], start=True, stop=True)
            h_full.mark(inst)
            h_full.latest(nc.scalar)
            loaded.wait_all(nc.scalar, n)
            h_out.mark(nc.scalar.activation(hT[:, m, :].rearrange("p (a f) -> p a f", a=2), psum[:, b:b + 2, 0:HALF],
                                            ACT.Relu, bias=b1[p][:, m:m + 1]))
            yield
        y_out.wait_all(nc.tensor, n - 1)
        for t in range(CT):
            for k in range(K4):
                if t == 0:
                    h_out.wait(nc.tensor, n, k + 1)
                inst = nc.tensor.matmul(psum[:, 6 + t // 4, (t % 4) * P:(t % 4) * P + P], hT[:, k, t * P:t * P + P],
                                        w2[p][:, k, :], start=(t % 4 == 0 and k == 0), stop=(k == K4 - 1),
                                        skip_group_check=True)
        y_full.mark(inst)
        y_full.latest(nc.vector)
        loaded.wait_all(nc.vector, n)
        stored.wait(nc.vector, n - 1, 1)
        b2w = lambda t: b2[p][:, :].unsqueeze(1).to_broadcast([P, t, C])
        nc.vector.tensor_tensor(ys[:, 0:4, :], psum[:, 6, :].rearrange("p (t c) -> p t c", c=C), b2w(4), ALU.add)
        y_out.mark(nc.vector.tensor_tensor(ys[:, 4, :], psum[:, 7, 0:C], b2[p][:, :], ALU.add))
        y_out.latest(nc.sync)
        stored.mark(nc.sync.dma_start(by_tile(tokens_out, n), ys[:, :, :]))
        yield

    def step(n, p, first, last):
        gen = None if last else fetch(n + 1, 1 - p)
        for i, _ in enumerate(expert(n, p)):
            if i in (0, 3):
                advance(gen)
        finish(gen)

    finish(fetch(0, 0))
    pipeline(nc, E, step)
    stored.wait_all(nc.gpsimd, E - 1)

    s_back = pr.nc.alloc_semaphore("m_back")
    for t in range(TILES):
        nc.gpsimd.indirect_dma_start(out=xn[:, t, :], out_offset=None, in_=tokens_out,
                                     in_offset=bass.IndirectOffsetOnAxis(ap=back_u[:, t:t + 1], axis=0))\
            .then_inc(s_back, 16)
    nc.vector.wait_ge(s_back, 16 * TILES)
    for t in range(TILES):
        inst = nc.vector.scalar_tensor_tensor(out=pr.x[:, t, :], in0=xn[:, t, :], scalar=gate[:, t:t + 1],
                                              in1=pr.x[:, t, :], op0=ALU.mult, op1=ALU.add)
    inst.then_inc(sv, 1)
    pr.fence()


def program(nc, io, out, per, upto=4):
    with ExitStack() as ctx:
        pr = Prog(nc, ctx, per, io)
        pr.psum = ctx.enter_context(nc.psum_tensor("psum", [P, 8, 512], F32))
        constants(pr)
        pr.x = pr.sb("x_sb", [P, TILES, C])
        io_in = ctx.enter_context(nc.semaphore("io_in"))
        io_out = ctx.enter_context(nc.semaphore("io_out"))
        nc.sync.dma_start(pr.x[:, :, :], io["x"].rearrange("b (t p) c -> p (b t) c", p=P)).then_inc(io_in, 16)
        pr.ctxT = pr.sb("ctxT", [CC, B, TC])
        nc.sync.dma_start(pr.ctxT[:, :, :], io["ctxT"]).then_inc(io_in, 16)
        nc.sync.wait_ge(io_in, 32)
        pr.fence()
        with pr.phase() as mem:
            l0_attention(pr, mem)
        if upto >= 2:
            with pr.phase() as mem:
                l0_ffn(pr, mem)
        if upto >= 3:
            pr.u = pr.sb("u_sb", [P, TILES, C])
            pr.xo = pr.sb("xo_sb", [P, TILES, C])
            pr.ctx2 = pr.sb("ctx2", [P, B, CC])
            for a in range(2):
                nc.sync.dma_start(pr.ctx2[TC * a:TC * a + TC, :, :], io["ctx"]).then_inc(io_in, 16)
            nc.sync.wait_ge(io_in, 64)
            pr.fence()
            for tag, own, dst in (("b", True, pr.u), ("c", False, pr.x)):
                with pr.phase() as mem:
                    mha_attention(pr, mem, tag, own)
                with pr.phase() as mem:
                    mha_ffn(pr, mem, tag + "f", "a1" if own else "a2", dst)
        if upto >= 4:
            with pr.phase() as mem:
                moe(pr, mem)
        nc.sync.dma_start(out.rearrange("b (t p) c -> p (b t) c", p=P), pr.x[:, :, :]).then_inc(io_out, 16)
        nc.sync.wait_ge(io_out, 16)
        return pr.seen


def by_chunk(v):
    return np.ascontiguousarray(v.reshape(-1, P, *v.shape[1:]).swapaxes(0, 1))


def ffn_layout(k, v):
    if k.endswith("_w"):
        v = by_chunk(v.T)
        return np.ascontiguousarray(v[:, 0]) if v.shape[1] == 1 else v
    return v if k.endswith("w3_s") else by_chunk(v)


def layout(inputs):
    a = {k: np.ascontiguousarray(v) for k, v in inputs.items()}
    for k, v in list(a.items()):
        if k.startswith("L0_ffn_"):
            a[k] = ffn_layout(k, v)
        elif k[-3:] in ("_wq", "_wk", "_wv"):
            a[k] = np.ascontiguousarray(v.transpose(1, 0, 2).reshape(v.shape[1], -1))
        elif k.endswith(("li1_w", "li3_w", "li2_b")):
            a[k] = by_chunk(v)
    for k in ("w2", "b1", "b2"):
        v = a["L1_ffn_" + k].reshape(E, -1, P if k == "b1" else C)
        a["L1_ffn_" + k] = np.ascontiguousarray(
            v if k == "b2" else v.transpose(0, 2, 1) if k == "b1" else
            v.reshape(E, K4, P, C).transpose(0, 2, 1, 3).reshape(E, P, K4 * C))
    a["gate_wT"] = np.ascontiguousarray(a.pop("L1_ffn_gate_w").T)
    a["ctx"] = np.ascontiguousarray(a["ctx_512"].transpose(1, 0, 2))
    a["ctxT"] = np.ascontiguousarray(a.pop("ctx_512").transpose(2, 0, 1))
    return a


def kernel(**inputs):
    import concourse.bacc as bacc
    from concourse.bass_utils import run_bass_kernel_spmd

    arrays = layout({k: np.asarray(v) for k, v in inputs.items()})
    per = {}
    for _ in range(2):
        nc = bacc.Bacc("TRN2", target_bir_lowering=False, num_devices=1)
        io = {k: nc.dram_tensor(f"in_{k}_dram", v.shape, mybir.dt.from_np(v.dtype), kind="ExternalInput").ap()
              for k, v in arrays.items()}
        out = nc.dram_tensor("out_0_dram", (B, T, C), F32, kind="ExternalOutput").ap()
        per = program(nc, io, out, per)
    r = run_bass_kernel_spmd(nc, [{f"in_{k}_dram": v for k, v in arrays.items()}], core_ids=[0])
    return r.results[0]["out_0_dram"]
```

```python
from contextlib import ExitStack, contextmanager

import numpy as np

import concourse.bass as bass
from concourse import mybir
from concourse.alu_op_type import AluOpType as ALU

F32 = mybir.dt.float32
F16 = mybir.dt.float16
BF16 = mybir.dt.bfloat16
U32 = mybir.dt.uint32
ACT = mybir.ActivationFunctionType
X = mybir.AxisListType.X

P = 128
B, T, C, CC, TC = 16, 256, 128, 64, 64
TILES = B * T // P
H = 16
EPS = 1e-5
NEG = -1e30


class Counter:

    def __init__(self, stage, name, unit=1):
        prog = stage.prog
        self.name, self.unit, self.prog, self.stage = name, unit, prog, stage
        self.sem = prog.nc.alloc_semaphore(name)
        self.per = prog.per.get(name, 0)
        self.k = 0
        prog.counters.append(self)

    def mark(self, instruction):
        instruction.then_inc(self.sem, self.unit)
        self.k += 1
        self.prog.seen[self.name] = max(self.prog.seen.get(self.name, 0), self.k)
        return self.k

    def latest(self, engine, apart=False):
        self.wait(engine, self.stage.n, self.k, apart)

    def wait(self, engine, n, k, apart=False):
        if self.per == 0:
            return
        value = (n * self.per + k) * self.unit
        if not (isinstance(value, int) and value <= 0):
            engine.wait_ge(self.sem, value)
            if (apart or engine is self.prog.nc.gpsimd) and not isinstance(value, int):
                engine.nop(nofuse=True)

    def wait_all(self, engine, n):
        self.wait(engine, n, self.per)


class Chain:

    def __init__(self, stage, engine, name):
        self.stage, self.engine = stage, engine
        self.event = stage.counter(name)

    def __call__(self, instruction):
        k = self.event.mark(instruction)
        self.event.wait(self.engine, self.stage.n, k, apart=True)


class Stage:

    def __init__(self, prog, name):
        self.prog, self.name, self.n, self.mine, self.rings = prog, name, 0, [], []

    def counter(self, name, unit=1):
        s = Counter(self, f"{self.name}_{name}", unit)
        self.mine.append(s)
        return s

    def chain(self, engine, name):
        return Chain(self, engine, name)

    def begin(self, n):
        self.n = n
        for s in self.mine:
            s.k = 0
        for r in self.rings:
            r.drains = []


class Prog:
    def __init__(self, nc, ctx, per, io):
        self.nc, self.ctx, self.per, self.io = nc, ctx, per, io
        self.seen, self.counters = {}, []

    def sb(self, name, shape, dt=F32, ctx=None):
        return (ctx or self.ctx).enter_context(self.nc.sbuf_tensor(name, shape, dt))

    def fence(self):
        self.nc.all_engine_barrier()

    @contextmanager
    def phase(self):
        before = self.nc.snapshot_sems()
        with ExitStack() as mem:
            yield mem
        self.fence()
        self.nc.clear_and_free_semaphores(self.nc.allocated_since(before))
        self.fence()


def finish(gen):
    for _ in gen:
        pass


def weave(prog, *parts):
    left = []
    for name, gen, start, end in parts:
        left.append([start, name, gen, (end - start) / prog.per.get("pieces of " + name, 20), 0])
    while left:
        part = min(left, key=lambda x: x[0])
        try:
            next(part[2])
            part[0] += part[3]
            part[4] += 1
        except StopIteration:
            prog.seen["pieces of " + part[1]] = part[4]
            left.remove(part)


def pipeline(nc, nb, step, tail=1):
    pairs = (nb - 1 - tail) // 2
    step(0, 0, nb - 1)
    with nc.Fori(0, pairs) as j:
        step(j * 2 + 1, 1, nb)
        step(j * 2 + 2, 0, nb)
    for n in range(2 * pairs + 1, nb):
        step(n, n % 2, nb - 1 - n)


class Ring:

    def __init__(self, stage, name, banks):
        self.stage, self.banks, self.nc = stage, banks, stage.prog.nc
        self.full = stage.counter(name + "_full")
        self.out = {e: stage.counter(f"{name}_out_{e}") for e in "va"}
        self.engine = {"v": self.nc.vector, "a": self.nc.scalar}
        self.drains = []
        stage.rings.append(self)

    def claim(self, apart=False):
        turn = len(self.drains)
        if turn < len(self.banks):
            for s in self.out.values():
                s.wait(self.nc.tensor, self.stage.n, 0, apart)
        else:
            s, k = self.drains[turn - len(self.banks)]
            s.wait(self.nc.tensor, self.stage.n, k, apart)
        return self.banks[turn % len(self.banks)]

    def filled(self, inst):
        self.full.mark(inst)

    def drain(self, who):
        self.full.latest(self.engine[who])
        return self.engine[who]

    def drained(self, who, inst):
        self.drains.append((self.out[who], self.out[who].mark(inst)))


def run_pipeline(pr, tag, nb, normed, prologue, main, epilogue):

    def step(n, p, left):
        parts = []
        if not isinstance(n, int) or n > 0:
            e = epilogue(n - 1, 1 - p)
            next(e)
            parts.append((tag + "e", e, 0.05, 0.75))
        if left >= 1:
            parts.append((tag + "p", prologue(n + 1, 1 - p), 0.0, 0.88))
        if left >= 2:
            parts.append((tag + "a", normed(n + 2, p), 0.2, 0.7))
        weave(pr, *parts, (tag + "m", main(n, p), 0.02, 1.0))

    finish(normed(0, 0))
    finish(normed(1, 1))
    finish(prologue(0, 0))
    pipeline(pr.nc, nb, step, tail=2)
    finish(epilogue(nb - 1, (nb - 1) % 2))
    pr.fence()


class LayerNorm:

    def __init__(self, pr, stage, name, tiles, mem, width=C, twice=False):
        nc = pr.nc
        self.pr, self.stage, self.tiles, self.twice = pr, stage, tiles, twice
        name = stage.name + name
        self.stat = pr.sb(name + "_stat", [P, tiles, 6], F32, mem)
        self.mv = pr.sb(name + "_mv", [P, tiles, 2], F32, mem)
        self.tmp = pr.sb(name + "_tmp", [P, 3, tiles], F32, mem)
        self.rstd = pr.sb(name + "_rstd", [P, tiles], F32, mem)
        self.var_ready = stage.counter(name + "_var")
        self.rstd_ready = stage.counter(name + "_rstd")
        self.chain_p = stage.chain(nc.gpsimd, name + "_pow")
        self.chain_v = stage.chain(nc.vector, name + "_stats")

    def __call__(self, src, rows=P):
        nc, n = self.pr.nc, self.stage.n
        mv, tmp = self.mv[0:rows], self.tmp[0:rows]
        for t in range(self.tiles):
            inst = nc.vector.bn_stats(self.stat[0:rows, t, :], src[:, t, :])
        self.chain_v(inst)
        for t in range(self.tiles):
            inst = nc.vector.bn_aggr(mv[:, t, :], self.stat[0:rows, t, :])
        self.chain_v(inst)
        k = self.var_ready.mark(nc.vector.tensor_scalar(tmp[:, 0, :], mv[:, :, 1], EPS, None, ALU.add))
        self.var_ready.wait(nc.gpsimd, n, k)
        half, minus = self.pr.pow_half[0:rows, 0:self.tiles], self.pr.pow_one[0:rows, 0:self.tiles]
        r = self.rstd[0:rows, :]
        if not self.twice:
            k = self.rstd_ready.mark(nc.gpsimd.tensor_tensor(r, tmp[:, 0, :], half, ALU.pow))
        else:
            nc.gpsimd.tensor_tensor(tmp[:, 1, :], tmp[:, 0, :], minus, ALU.pow)
            self.chain_p(nc.gpsimd.tensor_tensor(r, tmp[:, 0, :], half, ALU.pow))
            self.chain_p(nc.gpsimd.tensor_tensor(tmp[:, 2, :], mv[:, :, 1], tmp[:, 1, :], ALU.mult))
            self.chain_p(nc.gpsimd.tensor_scalar(tmp[:, 2, :], tmp[:, 2, :], EPS, None, ALU.add))
            self.chain_p(nc.gpsimd.tensor_tensor(tmp[:, 1, :], tmp[:, 2, :], half, ALU.pow))
            k = self.rstd_ready.mark(nc.gpsimd.tensor_tensor(r, r, tmp[:, 1, :], ALU.mult))
        self.rstd_ready.wait(nc.vector, n, k)

    def normalise(self, out, src, rows=P):
        nc = self.pr.nc
        for t in range(self.tiles):
            inst = nc.vector.tensor_scalar(out[:, t, :], src[:, t, :], self.mv[0:rows, t, 0:1],
                                           self.rstd[0:rows, t:t + 1], ALU.subtract, ALU.mult)
        return inst


def constants(pr):
    nc = pr.nc
    pr.ident = pr.sb("ident", [P, P])
    pr.ident16 = pr.sb("ident16", [P, P], F16)
    pr.identb = pr.sb("identb", [P, P], BF16)
    pr.hide_later = pr.sb("hide_later", [P, 4, P], BF16)
    pr.quadrant = pr.sb("quadrant", [P, 4])
    pr.pow_half = pr.sb("pow_half", [P, 8])
    pr.pow_one = pr.sb("pow_one", [P, 8])
    pr.ones = pr.sb("ones", [P, P])
    s = pr.ctx.enter_context(nc.semaphore("const"))
    for m in (pr.ident, pr.ident16, pr.identb):
        nc.gpsimd.memset(m[:, :], 0.0).then_inc(s, 1)
    nc.gpsimd.memset(pr.hide_later[:, :, :], 0.0).then_inc(s, 1)
    nc.gpsimd.memset(pr.pow_half[:, :], -0.5).then_inc(s, 1)
    nc.gpsimd.memset(pr.pow_one[:, :], -1.0).then_inc(s, 1)
    nc.gpsimd.memset(pr.ones[:, :], 1.0).then_inc(s, 1)
    nc.gpsimd.wait_ge(s, 7)
    for m in (pr.ident, pr.ident16, pr.identb):
        nc.gpsimd.affine_select(out=m[:, :], in_=m[:, :], compare_op=ALU.not_equal, fill=1.0, base=0,
                                pattern=[[-1, P]], channel_multiplier=1).then_inc(s, 1)
    nc.gpsimd.affine_select(out=pr.hide_later[:, :, :], in_=pr.hide_later[:, :, :], compare_op=ALU.is_ge,
                            fill=NEG, base=0, pattern=[[0, 4], [-1, P]], channel_multiplier=1).then_inc(s, 1)
    nc.gpsimd.wait_ge(s, 11)
    sq = pr.ctx.enter_context(nc.semaphore("const_q"))
    nc.vector.memset(pr.quadrant[:, :], 0.0).then_inc(sq, 1)
    nc.vector.wait_ge(sq, 1)
    for j in range(4):
        nc.vector.memset(pr.quadrant[32 * j:32 * j + 32, j:j + 1], 1.0).then_inc(sq, 1)
    nc.vector.wait_ge(sq, 5)


def load(pr, dst, src, sem):
    pr.nc.sync.dma_start(dst, src).then_inc(sem, 16)


def l0_attention(pr, mem):
    nc, io = pr.nc, pr.io
    D, G, W = 8, 4, 32
    NM = 3 * D
    SCALE = 1.0 / float(np.sqrt(D))
    wload = pr.nc.alloc_semaphore("l0a_w")
    Wcat = pr.sb("a_wcat", [P, 4, C], F32, mem)
    bcat = pr.sb("a_bcat", [P, 4, C], F32, mem)
    Wctx = pr.sb("a_wctx", [CC, 2, C], F32, mem)
    bctx = pr.sb("a_bctx", [P, 2, C], F32, mem)
    Wp = pr.sb("a_wp", [P, C], F32, mem)
    bp = pr.sb("a_bp", [P, 2, C], F32, mem)
    for i, x in enumerate("q cq k v".split()):
        load(pr, Wcat[:, i, :], io["L0_xattn_W" + x], wload)
        load(pr, bcat[:, i, :], io["L0_xattn_b" + x].partition_broadcast(P), wload)
    for i, x in enumerate("ck cv".split()):
        load(pr, Wctx[:, i, :], io["L0_xattn_W" + x], wload)
        load(pr, bctx[:, i, :], io["L0_xattn_b" + x].partition_broadcast(P), wload)
        load(pr, bp[:, i, :], io["L0_xattn_bp"].partition_broadcast(P), wload)
    load(pr, Wp[:, :], io["L0_xattn_Wp"], wload)
    nc.sync.wait_ge(wload, 16 * 15)

    z = [pr.sb(f"a_z{i}", [P, 2, C], F32, mem) for i in range(2)]
    zT = pr.sb("a_zT", [P, T], F32, mem)
    ctx2 = [pr.sb(f"a_ctx2{i}", [CC, P], F32, mem) for i in range(2)]
    qf = pr.sb("a_qf", [P, 3, C], F32, mem)
    kcf = pr.sb("a_kcf", [CC, C], F32, mem)
    tok = pr.sb("a_tok", [P, 2, 3, H, W], F16, mem)
    kctok = pr.sb("a_kctok", [CC, H, W], F16, mem)
    QT = [pr.sb(f"a_QT{i}", [P, 2, G, T], F16, mem) for i in range(2)]
    KT = [pr.sb(f"a_KT{i}", [P, 4, G, T], F16, mem) for i in range(2)]
    KcT = [pr.sb(f"a_KcT{i}", [P, G, 4, TC], F16, mem) for i in range(2)]
    V = [pr.sb(f"a_V{i}", [P, 2, H, W], F32, mem) for i in range(2)]
    Vc = [pr.sb(f"a_Vc{i}", [P, H // 2, 2, W // 2], F32, mem) for i in range(2)]
    KTall = pr.sb("a_KTall", [P, G * T], F16, mem)
    nm = pr.sb("a_nm", [P, 2, 4, 2, G], F16, mem)
    nmT = pr.sb("a_nmT", [W, T], F16, mem)
    prob = [pr.sb(f"a_prob{i}", [P, 512], F32, mem) for i in range(4)]
    ysT = [pr.sb(f"a_ysT{i}", [P, 3, 512], F32, mem) for i in range(2)]
    den = pr.sb("a_den", [P, 2, H], F32, mem)
    denc = pr.sb("a_denc", [P, 2, H], F32, mem)
    y = pr.sb("a_y", [P, 2, H, D], F32, mem)
    yc = pr.sb("a_yc", [P, 2, H, D], F32, mem)
    yT = pr.sb("a_yT", [P, T], F32, mem)
    res = pr.sb("a_res", [P, 2, C], F32, mem)
    psum = pr.psum
    s0 = pr.nc.alloc_semaphore("a_init")
    cnt = 0
    for m in [*V, *Vc, tok, kctok]:
        nc.gpsimd.memset(m[...], 0.0).then_inc(s0, 1); cnt += 1
    nc.gpsimd.wait_ge(s0, cnt)
    nc.vector.wait_ge(s0, cnt)
    for i in range(2):
        nc.vector.memset(V[i][:, :, :, D:D + 1], 1.0)
        for a in range(2):
            nc.vector.memset(Vc[i][TC * a:TC * a + TC, :, a, D:D + 1], 1.0)
    nc.vector.memset(tok[:, :, 2, :, NM:NM + 1], 1.0)
    nc.vector.memset(kctok[:, :, NM:NM + 1], 1.0).then_inc(s0, 1)
    nc.vector.wait_ge(s0, cnt + 1)
    pr.fence()

    SA, SP, SM, SE = Stage(pr, "aa"), Stage(pr, "ap"), Stage(pr, "am"), Stage(pr, "ae")
    ln = LayerNorm(pr, SA, "ln", 2, mem)
    pro = Ring(SP, "pro", [psum[:, i, :] for i in range(3)])
    z_ready, ctx_ready = SA.counter("z"), SA.counter("ctx")
    high, low = SP.counter("high"), SP.counter("low")
    kt_masked = SP.counter("kt_masked")
    nm_placed = SP.counter("nm_placed", 16)
    st_full, exp_done, sel_done, av_done, ys_full, ys_ready = (
        SM.counter(x) for x in ("st_full", "exp", "sel", "av", "ys_full", "ys"))
    epi = Ring(SE, "epi", [psum[:, 7, :]])
    chain_e = SE.chain(nc.vector, "chain")
    x_done = SE.counter("x")
    xs = pr.x

    def parts(ap, rows, heads):
        return ap.rearrange("p (h k d) -> p h k d", k=4, d=D)

    def normed(n, p):
        SA.begin(n)
        src = xs[:, bass.ds(n * 2, 2), :]
        ln(src)
        yield
        pro.full.wait(nc.vector, n - 2, 4)
        z_ready.mark(ln.normalise(z[p], src))
        z_ready.latest(nc.gpsimd)
        ctx_ready.mark(nc.gpsimd.tensor_copy(ctx2[p][:, :].rearrange("c (a t) -> c a t", a=2),
                       pr.ctxT[:, bass.ds(n, 1), :].to_broadcast([CC, 2, TC])))
        yield

    def prologue(n, p):
        SP.begin(n)
        z_ready.wait_all(nc.tensor, n)
        bank = pro.claim()
        for t in range(2):
            inst = nc.tensor.transpose(bank[:, t * P:t * P + P], z[p][:, t, :], pr.ident[:, :])
        pro.filled(inst)
        pro.drain("a")
        pro.drained("a", nc.scalar.activation(zT[:, :], bank[:, 0:T], ACT.Copy))
        yield
        pro.out["a"].latest(nc.tensor)
        for t in range(2):
            bank = pro.claim()
            pro.filled(nc.tensor.matmul(bank[:, :], zT[:, t * P:t * P + P], Wcat[:, :, :].rearrange("p a c -> p (a c)"),
                                        start=True, stop=True))
            pro.drain("v")
            high.latest(nc.vector)
            low.latest(nc.vector)
            nc.vector.tensor_tensor(V[p][:, t, :, 0:D], bank[:, 3 * C:4 * C].rearrange("p (h d) -> p h d", d=D),
                                    bcat[:, 3, :].rearrange("p (h d) -> p h d", d=D), ALU.add)
            pro.drained("v", nc.vector.tensor_tensor(qf[:, :, :].rearrange("p a c -> p (a c)"), bank[:, 0:3 * C],
                                                     bcat[:, 0:3, :].rearrange("p a c -> p (a c)"), ALU.add))
            pro.out["v"].latest(nc.scalar)
            qtok = parts(tok[:, t, 0:2, :, :].rearrange("p a h w -> p (a h w)"), P, 2 * H)
            ktok = parts(tok[:, t, 2, :, :].rearrange("p h w -> p (h w)"), P, H)
            q8 = qf[:, 0:2, :].rearrange("p a (h d) -> p (a h) d", d=D)
            k8 = qf[:, 2, :].rearrange("p (h d) -> p h d", d=D)
            nc.scalar.activation(qtok[:, :, 0:3:2, :], q8.unsqueeze(2).to_broadcast([P, 2 * H, 2, D]), ACT.Copy)
            high.mark(nc.scalar.activation(ktok[:, :, 0:2, :], k8.unsqueeze(2).to_broadcast([P, H, 2, D]), ACT.Copy))
            high.latest(nc.gpsimd)
            nc.gpsimd.tensor_tensor(qtok[:, :, 1, :], q8, qtok[:, :, 0, :], ALU.subtract)
            low.mark(nc.gpsimd.tensor_tensor(ktok[:, :, 2, :], k8, ktok[:, :, 0, :], ALU.subtract))
            yield
        ctx_ready.wait_all(nc.tensor, n)
        bank = pro.claim()
        pro.filled(nc.tensor.matmul(bank[:, 0:2 * C], ctx2[p][:, :], Wctx[:, :, :].rearrange("p a c -> p (a c)"),
                                    start=True, stop=True))
        pro.drain("v")
        for a in range(2):
            half = slice(TC * a, TC * a + TC)
            nc.vector.tensor_tensor(Vc[p][half, :, a, 0:D],
                                    bank[half, C:2 * C].rearrange("p (i a d) -> p i a d", a=2, d=D)[:, :, a, :],
                                    bctx[half, 1, :].rearrange("p (i a d) -> p i a d", a=2, d=D)[:, :, a, :], ALU.add)
        pro.drained("v", nc.vector.tensor_tensor(kcf[:, :], bank[0:TC, 0:C], bctx[0:TC, 0, :], ALU.add))
        pro.out["v"].latest(nc.scalar)
        kt_ = parts(kctok[:, :, :].rearrange("p h w -> p (h w)"), TC, H)
        k8 = kcf[:, :].rearrange("p (h d) -> p h d", d=D)
        high.mark(nc.scalar.activation(kt_[:, :, 0:2, :], k8.unsqueeze(2).to_broadcast([TC, H, 2, D]), ACT.Copy))
        high.latest(nc.gpsimd)
        low.mark(nc.gpsimd.tensor_tensor(kt_[:, :, 2, :], k8, kt_[:, :, 0, :], ALU.subtract))
        yield
        low.latest(nc.tensor)
        for t in range(2):
            bank16 = pro.claim().bitcast(F16)
            for a in range(2):
                for g in range(G):
                    at = (a * G + g) * P
                    inst = nc.tensor.transpose(bank16[:, at:at + P],
                                               tok[:, t, a, 4 * g:4 * g + 4, :].rearrange("p h w -> p (h w)"),
                                               pr.ident16[:, :])
            pro.filled(inst)
            pro.drain("a")
            pro.drained("a", nc.scalar.activation(QT[p][:, :, :, t * P:t * P + P].rearrange("p a g t -> p (a g) t"),
                                                  bank16[:, :].rearrange("p (a t) -> p a t", t=P), ACT.Copy))
            yield
        bank16 = pro.claim().bitcast(F16)
        for g in range(G):
            for t in range(2):
                at = (g * 2 + t) * P
                inst = nc.tensor.transpose(bank16[:, at:at + P],
                                           tok[:, t, 2, 4 * g:4 * g + 4, :].rearrange("p h w -> p (h w)"),
                                           pr.ident16[:, :])
        pro.filled(inst)
        pro.drain("a")
        kt_masked.wait_all(nc.scalar, n - 1)
        pro.drained("a", nc.scalar.activation(KTall[:, :], bank16[:, :], ACT.Copy))
        pro.out["a"].latest(nc.vector)
        for j in range(4):
            inst = nc.vector.tensor_scalar(KT[p][:, j, :, :].rearrange("p g t -> p (g t)"), KTall[:, :],
                                           pr.quadrant[:, j:j + 1], None, ALU.mult)
        kt_masked.mark(inst)
        yield
        bank16 = pro.claim(apart=True).bitcast(F16)
        for g in range(G):
            inst = nc.tensor.transpose(bank16[:, g * TC:g * TC + TC],
                                       kctok[:, 4 * g:4 * g + 4, :].rearrange("p h w -> p (h w)"),
                                       pr.ident16[0:TC, 0:TC])
        pro.filled(inst)
        pro.drain("v")
        for j in range(4):
            inst = nc.vector.tensor_scalar(KcT[p][:, :, j, :],
                                           bank16[:, 0:G * TC].rearrange("p (g t) -> p g t", t=TC),
                                           pr.quadrant[:, j:j + 1], None, ALU.mult)
        pro.drained("v", inst)
        yield
        pro.out["a"].latest(nc.tensor), pro.out["v"].latest(nc.tensor)

        def mx_reduce(bank, out, shape):
            pro.drain("v")
            pro.drained("v", nc.vector.tensor_reduce(out, bank.rearrange("p (a b) -> p a b", a=shape), X, ALU.max,
                                                     negate=True))

        for g in range(G):
            bank = pro.claim()
            for j in range(4):
                nc.tensor.matmul(bank[:, j * P:j * P + P], QT[p][:, 0, g, 0:P], KT[p][:, j, g, 0:P],
                                 start=(j == 0), stop=False, skip_group_check=True)
            pro.filled(nc.tensor.matmul(bank, pr.identb[:, :], pr.hide_later[:, :, :].rearrange("p a k -> p (a k)"),
                                          start=False, stop=True, skip_group_check=True))
            mx_reduce(bank, nm[:, 0, :, 0, g], 4)
            yield
            for jj in range(2):
                bank = pro.claim()
                for a in range(2):
                    nc.tensor.matmul(bank[:, a * T:a * T + T], QT[p][:, 0, g, P:T], KT[p][:, 2 * jj + a, g, :],
                                     start=(a == 0), stop=False, skip_group_check=True)
                diagonal = bank.rearrange("p (a h k) -> p a h k", a=2, h=2)[:, :, 1, :]
                pro.filled(nc.tensor.matmul(diagonal, pr.identb[:, :], pr.hide_later[:, 0:2, :],
                                              start=False, stop=True, skip_group_check=True))
                mx_reduce(bank, nm[:, 1, 2 * jj:2 * jj + 2, 0, g], 2)
                yield
        for t in range(2):
            for c in range(2):
                bank = pro.claim()
                for gg in range(2):
                    g = 2 * c + gg
                    inst = nc.tensor.matmul(bank[:, gg * 256:gg * 256 + 256], QT[p][:, 1, g, t * P:t * P + P],
                                            KcT[p][:, g, :, :].rearrange("p j t -> p (j t)"), start=(gg == 0),
                                            stop=True, skip_group_check=True)
                pro.filled(inst)
                mx_reduce(bank, nm[:, t, :, 1, 2 * c:2 * c + 2].rearrange("p j g -> p g j"), 8)
                yield
        pro.out["v"].latest(nc.tensor)
        bank16 = pro.claim().bitcast(F16)
        for t in range(2):
            inst = nc.tensor.transpose(bank16[0:W, t * P:t * P + P], nm[:, t, :, :, :].rearrange("p j s g -> p (j s g)"),
                                       pr.ident16[:, :])
        pro.filled(inst)
        pro.drain("a")
        nm_placed.wait_all(nc.scalar, n - 1)
        pro.drained("a", nc.scalar.activation(nmT[:, :], bank16[0:W, 0:T], ACT.Copy))
        pro.out["a"].latest(nc.sync)
        for j in range(4):
            nm_placed.mark(nc.sync.dma_start(QT[p][W * j + NM:W * j + NM + 1, :, :, :],
                                             nmT[8 * j:8 * j + 8, :]))
        yield

    units = [("self", h) for h in range(H)] + [("cross", g) for g in range(G)]

    def scores(n, p, i):
        kind, h = units[i]
        exp_done.wait(nc.tensor, n, i - 1)
        bank = psum[:, 3 + i % 2, :]
        if kind == "self":
            g, j = h // 4, h % 4
            nc.tensor.matmul(bank[:, 0:T], KT[p][:, j, g, 0:P], QT[p][:, 0, g, :], start=True, stop=True)
            inst = nc.tensor.matmul(bank[:, T:T + P], KT[p][:, j, g, P:T], QT[p][:, 0, g, P:T], start=False, stop=True,
                                    skip_group_check=True)
        else:
            for a in range(2):
                inst = nc.tensor.matmul(bank[:, a * T:a * T + T],
                                        KcT[p][:, h, 2 * a:2 * a + 2, :].rearrange("p j t -> p (j t)"),
                                        QT[p][:, 1, h, :], start=(a == 0), stop=True, skip_group_check=True)
        st_full.mark(inst)
        width = T + P if kind == "self" else 2 * T
        st_full.latest(nc.scalar)
        av_done.wait(nc.scalar, n, i - 3)
        exp_done.mark(nc.scalar.activation(prob[i % 4][:, 0:width], bank[:, 0:width], ACT.Exp, scale=SCALE))
        if kind == "self":
            exp_done.latest(nc.gpsimd)
            d = prob[i % 4][:, 0:2 * T].rearrange("p (a q) -> p a q", a=2)[:, :, 0:P]
            sel_done.mark(nc.gpsimd.affine_select(out=d, in_=d, compare_op=ALU.is_ge, fill=0.0, base=0,
                                                  pattern=[[0, 2], [1, P]], channel_multiplier=-1))

    def values(n, p, i):
        kind, h = units[i]
        g = h // 4
        pb = prob[i % 4]
        if kind == "self":
            sel_done.wait(nc.tensor, n, i + 1)
            j, use = h % 4, g // 2
            if h % 8 == 0:
                ys_ready.wait(nc.tensor, n, (0, -1)[use])
            o = psum[32 * j:32 * j + 32, 5 + use, (g % 2) * T:(g % 2) * T + T]
            nc.tensor.matmul(o, V[p][:, 0, h, :], pb[:, 0:T], start=True, stop=False, skip_group_check=True)
            inst = nc.tensor.matmul(o[:, P:T], V[p][:, 1, h, :], pb[:, T:T + P], start=False, stop=True,
                                    skip_group_check=True)
        else:
            use = 2
            exp_done.wait(nc.tensor, n, i + 1)
            if h == 0:
                ys_ready.wait(nc.tensor, n, 1)
            for a in range(2):
                q = 2 * (h % 2) + a
                inst = nc.tensor.matmul(psum[32 * q:32 * q + 32, 5, (h // 2) * T:(h // 2) * T + T],
                                        Vc[p][:, 2 * h + a, :, :].rearrange("p a w -> p (a w)"),
                                        pb[:, a * T:a * T + T], start=True, stop=True, skip_group_check=True)
        av_done.mark(inst)
        if (kind, h) in (("self", 7), ("self", 15), ("cross", 3)):
            av_done.latest(nc.scalar)
            if use == 0:
                epi.full.wait(nc.scalar, n - 1, 1)
            ys_ready.mark(nc.scalar.activation(ysT[p][:, use, :], psum[:, 5 + use % 2, :], ACT.Copy))

    def epilogue(n, p):
        SE.begin(n)
        for t in range(2):
            ys_ready.wait(nc.tensor, n, 2)
            bank = epi.claim()
            for g in range(G):
                at = (g % 2) * T + t * P
                inst = nc.tensor.transpose(bank[:, g * P:g * P + P], ysT[p][:, g // 2, at:at + P], pr.ident[:, :])
            epi.filled(inst)
            epi.drain("v")
            heads = bank.rearrange("p (h w) -> p h w", w=W)
            chain_e(nc.vector.reciprocal(den[:, t, :], heads[:, :, D]))
            epi.drained("v", nc.vector.tensor_tensor(y[:, t, :, :], heads[:, :, 0:D],
                                                     den[:, t, :].unsqueeze(2).to_broadcast([P, H, D]), ALU.mult))
            yield
        ys_ready.wait(nc.tensor, n, 3)
        bank = epi.claim()
        for t in range(2):
            for c in range(2):
                inst = nc.tensor.transpose(bank[:, t * T + c * P:t * T + c * P + P],
                                           ysT[p][:, 2, c * T + t * P:c * T + t * P + P], pr.ident[:, :])
        epi.filled(inst)
        epi.drain("v")
        heads = bank.rearrange("p (t w) -> p t w", w=W // 2)
        denf = denc[:, :, :].rearrange("p t h -> p (t h)")
        chain_e(nc.vector.reciprocal(denf, heads[:, :, D]))
        epi.drained("v", nc.vector.tensor_tensor(yc[:, :, :, :].rearrange("p t h d -> p (t h) d"), heads[:, :, 0:D],
                                                 denf.unsqueeze(2).to_broadcast([P, 2 * H, D]), ALU.mult))
        epi.out["v"].latest(nc.vector)
        flat = lambda m: m[:, :, :, :].rearrange("p t h d -> p (t h d)")
        chain_e(nc.vector.tensor_tensor(flat(y), flat(y), flat(yc), ALU.add))
        yield
        chain_e.event.latest(nc.tensor)
        bank = epi.claim()
        for t in range(2):
            inst = nc.tensor.transpose(bank[:, t * P:t * P + P], y[:, t, :, :].rearrange("p h d -> p (h d)"), pr.ident[:, :])
        epi.filled(inst)
        epi.drain("a")
        epi.drained("a", nc.scalar.activation(yT[:, :], bank[:, 0:T], ACT.Copy))
        yield
        bank = epi.claim()
        for t in range(2):
            inst = nc.tensor.matmul(bank[:, t * P:t * P + P], yT[:, t * P:t * P + P], Wp[:, :], start=(t == 0), stop=True,
                                    skip_group_check=True)
        epi.filled(inst)
        epi.drain("v")
        epi.drained("v", nc.vector.tensor_tensor(res[:, :, :].rearrange("p t c -> p (t c)"), bank[:, 0:T],
                                                 bp[:, :, :].rearrange("p t c -> p (t c)"), ALU.add))
        epi.out["v"].latest(nc.vector)
        dst = xs[:, bass.ds(n * 2, 2), :]
        chain_e(nc.vector.tensor_tensor(dst, dst, res[:, :, :], ALU.add))
        yield

    LAG = 2

    def main(n, p):
        SM.begin(n)
        nm_placed.wait_all(nc.tensor, n)
        for i in range(len(units) + LAG):
            if i < len(units):
                scores(n, p, i)
                yield
            if i >= LAG:
                values(n, p, i - LAG)
                yield

    run_pipeline(pr, "a", B, normed, prologue, main, epilogue)


HID = 512
K4 = HID // P
N4 = 4 * P


def feed_forward(pr, mem, tag, src, dst, first, middle, last, out_scale, out_bias):
    nc, psum = pr.nc, pr.psum
    gated = len(first) == 2
    z = pr.sb(tag + "_z", [P, 4, C], F32, mem)
    zT = [pr.sb(f"{tag}_zT{i}", [P, N4], F32, mem) for i in range(2)]
    gate = [pr.sb(f"{tag}_gate{i}", [P, N4], F32, mem) for i in range(2)] if gated else None
    hT = [pr.sb(f"{tag}_hT{i}", [P, K4, N4], F32, mem) for i in range(2)]
    res = pr.sb(tag + "_res", [P, 4, C], F32, mem)
    SP, SM = Stage(pr, tag + "p"), Stage(pr, tag + "m")
    ln = LayerNorm(pr, SP, "ln", 4, mem)
    pro = Ring(SP, "pro", [psum[:, 0, :]])
    z_ready = SP.counter("z")
    full, out_a, out_v, silu_done = (SM.counter(x) for x in ("full", "out_a", "out_v", "silu"))
    y_full, y_out = SM.counter("y_full"), SM.counter("y_out")
    chain = SM.chain(nc.vector, "chain")
    RING = 4

    def prologue(n, p):
        SP.begin(n)
        tokens = src[:, bass.ds(n * 4, 4), :]
        ln(tokens)
        z_ready.mark(ln.normalise(z, tokens))
        yield
        z_ready.latest(nc.tensor)
        bank = pro.claim()
        for t in range(4):
            inst = nc.tensor.transpose(bank[:, t * P:t * P + P], z[:, t, :], pr.ident[:, :])
        pro.filled(inst)
        pro.drain("v")
        pro.drained("v", nc.vector.tensor_copy(zT[p][:, :], bank))
        yield

    def main(n, p):
        drains = []

        def bank_for():
            u = len(drains)
            if u >= RING:
                s, k = drains[u - RING]
                s.wait(nc.tensor, n, k)
            else:
                out_a.wait(nc.tensor, n, u - RING + 1)
            return psum[:, 1 + u % RING, :]

        def activate(bank, out, func, scale, bias, event):
            full.latest(nc.scalar)
            inst = nc.scalar.activation(out, bank, func, **({"scale": scale} if scale is not None else {}),
                                        **({"bias": bias} if bias is not None else {}))
            return event.mark(inst)

        pro.out["v"].wait_all(nc.tensor, n)
        ready = []
        for m in range(K4):
            if not gated:
                w, scale, bias = first[0]
                bank = bank_for()
                full.mark(nc.tensor.matmul(bank, w[:, m * P:m * P + P], zT[p][:, :], start=True, stop=True))
                k = activate(bank, hT[0][:, m, :], ACT.Gelu, scale, bias[:, m:m + 1], out_a)
                drains.append((out_a, k)), ready.append((out_a, k))
            else:
                (wa, sa, _), (wb, sb, _) = first
                bank = bank_for()
                full.mark(nc.tensor.matmul(bank, wa[:, m * P:m * P + P], zT[p][:, :], start=True, stop=True))
                out_v.latest(nc.scalar) if m >= 2 else None
                k = activate(bank, gate[m % 2][:, :], ACT.Silu, sa[:, m:m + 1], None, out_a)
                drains.append((out_a, k))
                bank = bank_for()
                full.mark(nc.tensor.matmul(bank, wb[:, m * P:m * P + P], zT[p][:, :], start=True, stop=True))
                full.latest(nc.vector), out_a.latest(nc.vector)
                k = out_v.mark(nc.vector.scalar_tensor_tensor(hT[0][:, m, :], bank, sb[:, m:m + 1], gate[m % 2][:, :],
                                                              ALU.mult, ALU.mult))
                drains.append((out_v, k)), ready.append((out_v, k))
            yield
        cur = 0
        for w, scale in middle:
            now = []
            for m in range(K4):
                bank = bank_for()
                for k in range(K4):
                    if m == 0:
                        ready[k][0].wait(nc.tensor, n, ready[k][1])
                    inst = nc.tensor.matmul(bank, w[:, k, m * P:m * P + P], hT[cur][:, k, :],
                                            start=(k == 0), stop=(k == K4 - 1))
                full.mark(inst)
                k = activate(bank, hT[1 - cur][:, m, :], ACT.Gelu, scale[:, m:m + 1], None, out_a)
                drains.append((out_a, k)), now.append((out_a, k))
                yield
            ready, cur = now, 1 - cur
        y_out.wait_all(nc.tensor, n - 1)
        bank = psum[:, 1 + RING, :]
        for t in range(4):
            for k in range(K4):
                if t == 0:
                    ready[k][0].wait(nc.tensor, n, ready[k][1])
                inst = nc.tensor.matmul(bank[:, t * P:t * P + P], hT[cur][:, k, t * P:t * P + P], last[:, k, :],
                                        start=(t == 0 and k == 0), stop=(k == K4 - 1), skip_group_check=True)
        y_full.mark(inst)
        y_full.latest(nc.vector)
        tokens, r = dst[:, bass.ds(n * 4, 4), :], res[:, :, :]
        bank = bank.rearrange("p (t c) -> p t c", t=4)
        if out_scale is not None:
            y_out.mark(nc.vector.tensor_tensor(r, bank, out_scale.unsqueeze(1).to_broadcast([P, 4, C]), ALU.mult))
        else:
            y_out.mark(nc.vector.tensor_tensor(r, bank, out_bias.unsqueeze(1).to_broadcast([P, 4, C]), ALU.add))
        y_out.latest(nc.vector)
        chain(nc.vector.tensor_tensor(tokens, tokens, r, ALU.add))
        yield

    def step(n, p, left):
        SM.begin(n)
        ahead = [(tag + "p", prologue(n + 1, 1 - p), 0.1, 0.6)] if left else []
        weave(pr, (tag, main(n, p), 0.0, 1.0), *ahead)

    finish(prologue(0, 0))
    pipeline(nc, TILES // 4, step)
    pr.fence()


def l0_ffn_weights(pr, mem):
    io, w = pr.io, {}
    sem = pr.nc.alloc_semaphore("l0f_w")
    for name, shape in (("w1_w", [P, HID]), ("w2_w", [P, HID]), ("h1_w", [P, K4, HID]), ("h2_w", [P, K4, HID]),
                        ("w3_w", [P, K4, C]), ("w1_s", [P, K4]), ("w2_s", [P, K4]), ("h1_s", [P, K4]),
                        ("h2_s", [P, K4])):
        w[name] = pr.sb("f_" + name, shape, F32, mem)
        load(pr, w[name][...], io["L0_ffn_" + name], sem)
    w["w3_s"] = pr.sb("f_w3s", [P, C], F32, mem)
    load(pr, w["w3_s"][:, :], io["L0_ffn_w3_s"].partition_broadcast(P), sem)
    return w, (sem, 160)


def l0_ffn(pr, mem):
    w, (sem, v) = l0_ffn_weights(pr, mem)
    pr.nc.sync.wait_ge(sem, v)
    pr.fence()
    feed_forward(pr, mem, "f", pr.x, pr.x, [(w["w1_w"], w["w1_s"], None), (w["w2_w"], w["w2_s"], None)],
                 [(w["h1_w"], w["h1_s"]), (w["h2_w"], w["h2_s"])], w["w3_w"], w["w3_s"][:, :], None)


def fold_weights(pr, mem, tag, weights, biases):
    nc, psum = pr.nc, pr.psum
    sv, sp = (pr.nc.alloc_semaphore(tag + x) for x in ("_fold_v", "_fold_p"))
    wide = pr.sb(tag + "_offset", [P, P], F32, mem)
    v = 0
    for n, (w, gain, offset, out, plus) in enumerate(weights):
        rows, by_token = w.shape[0], out.shape[1] == HID
        bank = psum[:, n % 8, :]
        if by_token:
            if n:
                nc.vector.wait_ge(sp, n)
            v += 1
            nc.vector.tensor_copy(wide[0:rows, :], offset.to_broadcast([rows, P])).then_inc(sv, 1)
            nc.tensor.wait_ge(sv, v)
            nc.tensor.matmul(bank, wide[0:rows, :], w, start=True, stop=True).then_inc(sp, 1)
            nc.vector.wait_ge(sp, n + 1)
            v += 1
            nc.vector.tensor_copy(out, bank).then_inc(sv, 1)
        else:
            for m in range(K4):
                inst = nc.tensor.matmul(bank[:, m:m + 1], w[:, m * P:m * P + P], offset, start=(m == 0), stop=True,
                                        skip_group_check=True)
            inst.then_inc(sp, 1)
            nc.vector.wait_ge(sp, n + 1)
            v += 1
            nc.vector.tensor_tensor(out, bank[:, 0:K4], plus, ALU.add).then_inc(sv, 1)
        v += 1
        nc.vector.tensor_scalar(w, w, gain, None, ALU.mult).then_inc(sv, 1)


def mha_weights(pr, mem, tag, pre, norm):
    io, w = pr.io, {}
    ck = C if pre == "a1" else CC
    sem = pr.nc.alloc_semaphore(tag + "_w")
    q = lambda x: io[f"L1_xattn_{x}"]
    for name, rows in (("wq", C), ("wk", ck), ("wv", ck)):
        w[name] = pr.sb(f"{tag}_{name}", [rows, HID], F32, mem)
        load(pr, w[name][:, :], q(f"{pre}_{name}"), sem)
    w["li1"] = pr.sb(tag + "_li1", [P, K4, C], F32, mem)
    load(pr, w["li1"][:, :, :], q(pre + "_li1_w"), sem)
    for name, src, rows in (("gx", "lnx_g", C), ("bx", "lnx_b", C), ("gy", "lny_g", ck), ("by", "lny_b", ck)):
        w[name] = pr.sb(f"{tag}_{name}", [rows, 1], F32, mem)
        load(pr, w[name][:, :], q(f"{pre}_{src}").unsqueeze(1), sem)
    for name, src in (("li1_b", pre + "_li1_b"), ("g", norm + "_g"), ("b", norm + "_b")):
        w[name] = pr.sb(f"{tag}_{name}_row", [P, C], F32, mem)
        load(pr, w[name][:, :], q(src).partition_broadcast(P), sem)
    for name in ("bq", "bk", "bv"):
        w[name] = pr.sb(f"{tag}_{name}", [P, HID], F32, mem)
    return w, (sem, 11 * 16)


def mha_attention(pr, mem, tag, own):
    nc, psum = pr.nc, pr.psum
    D, G = 32, 4
    R = 3 * D + 1
    NM = 3 * D
    RP = R + 1
    SCALE = float(D) ** -0.5
    w, (sem, v) = mha_weights(pr, mem, tag, "a1" if own else "a2", "ln1" if own else "ln2")
    nc.sync.wait_ge(sem, v)
    pr.fence()
    fold_weights(pr, mem, tag, [(w["wq"][:, :], w["gx"][:, :], w["bx"][:, :], w["bq"][:, :], None),
                                (w["wk"][:, :], w["gy"][:, :], w["by"][:, :], w["bk"][:, :], None),
                                (w["wv"][:, :], w["gy"][:, :], w["by"][:, :], w["bv"][:, :], None)], None)
    z = [pr.sb(f"{tag}_z{i}", [P, 2, C], F32, mem) for i in range(2)]
    zi = pr.sb(tag + "_zi", [P, 2, C], F32, mem)
    zT = pr.sb(tag + "_zT", [P, T], F32, mem)
    qf = [pr.sb(f"{tag}_qf{i}", [P, HID], F32, mem) for i in range(2)]
    qtok = pr.sb(tag + "_qtok", [P, 2, H, RP], F16, mem)
    ktok = pr.sb(tag + "_ktok", [P, 2 if own else 1, H, RP], F16, mem)
    KW = T if own else TC
    QT = [pr.sb(f"{tag}_QT{i}", [R, H, T], F16, mem) for i in range(2)]
    KT = [pr.sb(f"{tag}_KT{i}", [R, H, KW], F16, mem) for i in range(2)]
    nm = pr.sb(tag + "_nm", [P, 2, H], F16, mem)
    nmT = pr.sb(tag + "_nmT", [H, T], F16, mem)
    prob = [pr.sb(f"{tag}_prob{i}", [P, 2 * T], F32, mem) for i in range(4)]
    late = [pr.sb(f"{tag}_late{i}", [P, 2, P], F32, mem) for i in range(4)] if own else None
    ndT = [pr.sb(f"{tag}_ndT{i}", [P, G, 2 * T], F32, mem) for i in range(2)]
    rden = pr.sb(tag + "_rden", [P, 2, H], F32, mem)
    o = pr.sb(tag + "_o", [P, 2, H, D], F32, mem)
    oT = pr.sb(tag + "_oT", [P, G, T], F32, mem)
    res = pr.sb(tag + "_res", [P, 2, C], F32, mem)
    if own:
        V = [pr.sb(f"{tag}_V{i}", [P, 2, HID], F32, mem) for i in range(2)]
        zeroed = []
        sums = pr.ones[:, 0:D]
    else:
        V = [pr.sb(f"{tag}_V{i}", [P, H // 2, 2, D], F32, mem) for i in range(2)]
        pair_ones = pr.sb(tag + "_pair_ones", [P, 2, D], F32, mem)
        zeroed = [*V, pair_ones]
        sums = pair_ones[:, :, :].rearrange("p a d -> p (a d)")
        zc = [pr.sb(f"{tag}_zc{i}", [P, 1, CC], F32, mem) for i in range(2)]
        cT = pr.sb(tag + "_cT", [CC, P], F32, mem)
    s0 = pr.nc.alloc_semaphore(tag + "_init")
    for m in [*zeroed, qtok, ktok]:
        inst = nc.vector.memset(m[...], 0.0)
    inst.then_inc(s0, 1)
    nc.vector.wait_ge(s0, 1)
    if not own:
        for a in range(2):
            nc.vector.memset(pair_ones[TC * a:TC * a + TC, a, :], 1.0)
    nc.vector.memset(ktok[:, :, :, NM:NM + 1], 1.0).then_inc(s0, 1)
    nc.vector.wait_ge(s0, 2)
    pr.fence()

    SA, SP, SM, SE = (Stage(pr, tag + x) for x in "apme")
    ln_in = LayerNorm(pr, SA, "lni", 2, mem, twice=own)
    ln_x = LayerNorm(pr, SA, "lnx", 2, mem)
    ln_c = None if own else LayerNorm(pr, SA, "lnc", 1, mem)
    pro = Ring(SP, "pro", [psum[:, i, :] for i in range(3)])
    z_ready, high, low = SA.counter("z"), SP.counter("high"), SP.counter("low")
    chain_a = SA.chain(nc.vector, "chain")
    nm_placed = SP.counter("nm_placed", 16)
    st_full, exp_done, sel_done, av_done, nd_ready = (SM.counter(x) for x in ("st_full", "exp", "sel", "av", "nd"))
    epi = Ring(SE, "epi", [psum[:, 7, :]])
    chain_e = SE.chain(nc.vector, "chain")
    src, u, xo, xs = (pr.x if own else pr.u), pr.u, pr.xo, pr.x
    two = lambda m, n: m[:, bass.ds(n * 2, 2), :]
    row2 = lambda m: m[:, :].unsqueeze(1).to_broadcast([P, 2, C])

    def stack(bank, bias, dst, turn, key, rows=P):
        pro.drain("v")
        f = qf[turn][0:rows, :]
        low.wait(nc.vector, SP.n, low.k - 1)
        pro.drained("v", nc.vector.tensor_tensor(f, bank[0:rows, :], bias[0:rows, :], ALU.add))
        pro.out["v"].latest(nc.scalar)
        f3 = f.rearrange("p (h d) -> p h d", d=D)
        d3 = dst[:, :, 0:NM].rearrange("p h (k d) -> p h k d", d=D)
        twice = d3[:, :, 0:2, :] if key else d3[:, :, 0:3:2, :]
        high.mark(nc.scalar.activation(twice, f3.unsqueeze(2).to_broadcast([rows, H, 2, D]), ACT.Copy))
        high.latest(nc.gpsimd)
        low.mark(nc.gpsimd.tensor_tensor(d3[:, :, 2 if key else 1, :], f3, d3[:, :, 0, :], ALU.subtract))

    def turned(tok, out, rows, width, who):
        bank16 = pro.claim(apart=rows < P).bitcast(F16)
        for h in range(8):
            inst = nc.tensor.transpose(bank16[0:R, h * width:h * width + width], tok[:, h, 0:R],
                                       pr.ident16[0:rows, 0:rows])
        pro.filled(inst)
        pro.drain(who)
        source = bank16[0:R, 0:8 * width].rearrange("p (h t) -> p h t", h=8)
        pro.drained(who, nc.vector.tensor_copy(out, source) if who == "v" else
                    nc.scalar.activation(out, source, ACT.Copy))

    def normed(n, p):
        SA.begin(n)
        un = two(u, n)
        ln_in(two(src, n))
        yield
        chain_a(ln_in.normalise(zi, two(src, n)))
        chain_a(nc.vector.tensor_tensor(zi[:, :, :], zi[:, :, :], row2(w["g"]), ALU.mult))
        chain_a(nc.vector.tensor_tensor(un, zi[:, :, :], row2(w["b"]), ALU.add))
        yield
        ln_x(un)
        yield
        pro.full.wait(nc.vector, n - 2, 1)
        z_ready.mark(ln_x.normalise(z[p], un))
        if not own:
            cn = pr.ctx2[:, bass.ds(n, 1), :]
            ln_c(cn)
            z_ready.mark(ln_c.normalise(zc[p], cn))
        yield

    def prologue(n, p):
        SP.begin(n)
        z_ready.wait_all(nc.tensor, n)
        bank = pro.claim()
        for t in range(2):
            inst = nc.tensor.transpose(bank[:, t * P:t * P + P], z[p][:, t, :], pr.ident[:, :])
        if not own:
            inst = nc.tensor.transpose(bank[0:CC, T:T + P], zc[p][:, 0, :], pr.ident[:, :])
        pro.filled(inst)
        pro.drain("a")
        if not own:
            nc.scalar.activation(cT[:, :], bank[0:CC, T:T + P], ACT.Copy)
        pro.drained("a", nc.scalar.activation(zT[:, :], bank[:, 0:T], ACT.Copy))
        yield
        turn = 0
        pro.out["a"].latest(nc.tensor)
        for t in range(2):
            zt = zT[:, t * P:t * P + P]
            bank = pro.claim()
            pro.filled(nc.tensor.matmul(bank, zt, w["wq"][:, :], start=True, stop=True))
            stack(bank, w["bq"], qtok[:, t, :, :], turn, False)
            turn ^= 1
            yield
            if own:
                bank = pro.claim()
                pro.filled(nc.tensor.matmul(bank, zt, w["wk"][:, :], start=True, stop=True))
                stack(bank, w["bk"], ktok[:, t, :, :], turn, True)
                turn ^= 1
                yield
                bank = pro.claim()
                pro.filled(nc.tensor.matmul(bank, zt, w["wv"][:, :], start=True, stop=True))
                pro.drain("v")
                pro.drained("v", nc.vector.tensor_tensor(V[p][:, t, :], bank, w["bv"][:, :], ALU.add))
                yield
        if not own:
            bank = pro.claim()
            pro.filled(nc.tensor.matmul(bank, cT[:, :], w["wk"][:, :], start=True, stop=True))
            stack(bank, w["bk"], ktok[0:TC, 0, :, :], turn, True, TC)
            yield
            bank = pro.claim()
            pro.filled(nc.tensor.matmul(bank, cT[:, :], w["wv"][:, :], start=True, stop=True))
            pro.drain("v")
            for a in range(2):
                half = slice(TC * a, TC * a + TC)
                pick = lambda m: m[half, :].rearrange("p (i a d) -> p i a d", a=2, d=D)[:, :, a, :]
                inst = nc.vector.tensor_tensor(V[p][half, :, a, :], pick(bank), pick(w["bv"]), ALU.add)
            pro.drained("v", inst)
            yield
        low.latest(nc.tensor)
        for t in range(2):
            for e in range(2):
                turned(qtok[:, t, 8 * e:8 * e + 8, :], QT[p][:, 8 * e:8 * e + 8, t * P:t * P + P], P, P, "av"[e])
                yield
                if own:
                    turned(ktok[:, t, 8 * e:8 * e + 8, :], KT[p][:, 8 * e:8 * e + 8, t * P:t * P + P], P, P, "va"[e])
                    yield
        if not own:
            for e in range(2):
                turned(ktok[0:TC, 0, 8 * e:8 * e + 8, :], KT[p][:, 8 * e:8 * e + 8, :], TC, TC, "av"[e])
            yield
        pro.out["a"].latest(nc.tensor), pro.out["v"].latest(nc.tensor)

        def mx_use(matmuls, out, groups):
            bank = pro.claim()
            for i, (at, width, lhsT, rhs) in enumerate(matmuls):
                inst = nc.tensor.matmul(bank[:, at:at + width], lhsT, rhs, start=(i == 0), stop=True,
                                        skip_group_check=True)
            pro.filled(inst)
            pro.drain("v")
            pro.drained("v", nc.vector.tensor_reduce(out, bank.rearrange("p (a b) -> p a b", a=groups), X, ALU.max,
                                                     negate=True))

        if own:
            for h in range(H):
                mx_use([(t * T, T, QT[p][:, h, t * P:t * P + P], KT[p][:, h, :]) for t in range(2)], nm[:, :, h], 2)
                yield
        else:
            for t in range(2):
                for e in range(2):
                    mx_use([(i * TC, TC, QT[p][:, 8 * e + i, t * P:t * P + P], KT[p][:, 8 * e + i, :])
                            for i in range(8)], nm[:, t, 8 * e:8 * e + 8], 8)
                    yield
        pro.out["v"].latest(nc.tensor)
        bank16 = pro.claim().bitcast(F16)
        for t in range(2):
            inst = nc.tensor.transpose(bank16[0:H, t * P:t * P + P], nm[:, t, :], pr.ident16[:, :])
        pro.filled(inst)
        pro.drain("a")
        nm_placed.wait_all(nc.scalar, n - 1)
        pro.drained("a", nc.scalar.activation(nmT[:, :], bank16[0:H, 0:T], ACT.Copy))
        pro.out["a"].latest(nc.sync)
        nm_placed.mark(nc.sync.dma_start(QT[p][NM:NM + 1, :, :], nmT[:, :]))
        yield

    units = H if own else G

    def scores(n, p, i):
        exp_done.wait(nc.tensor, n, i - 1)
        bank = psum[:, 3 + i % 2, :]
        if own:
            for kb in range(2):
                inst = nc.tensor.matmul(bank[:, kb * T:kb * T + T], KT[p][:, i, kb * P:kb * P + P], QT[p][:, i, :],
                                        start=(kb == 0), stop=True, skip_group_check=True)
        else:
            for j in range(4):
                a, pair = j % 2, j // 2
                inst = nc.tensor.matmul(bank[TC * a:TC * a + TC, pair * T:pair * T + T], KT[p][:, 4 * i + j, :],
                                        QT[p][:, 4 * i + j, :], start=(pair == 0), stop=True, skip_group_check=True)
        st_full.mark(inst)
        st_full.latest(nc.scalar)
        av_done.wait(nc.scalar, n, i - 3)
        exp_done.mark(nc.scalar.activation(prob[i % 4][:, :], bank, ACT.Exp, scale=SCALE))
        if own:
            exp_done.latest(nc.gpsimd)
            av_done.wait(nc.gpsimd, n, i - 3)
            pm = prob[i % 4][:, :]
            for b, at in enumerate((0, T + P)):
                inst = nc.gpsimd.affine_select(out=late[i % 4][:, b, :], in_=pm[:, at:at + P], compare_op=ALU.is_gt,
                                               fill=0.0, base=0, pattern=[[-1, P]], channel_multiplier=1)
            sel_done.mark(inst)

    def values(n, p, i):
        g = i // 4 if own else i
        j = i % 4
        pb = prob[i % 4]
        bank = psum[:, 5 + g % 2, :]
        if j == 0 or not own:
            nd_ready.wait(nc.tensor, n, g - 1)
        exp_done.wait(nc.tensor, n, i + 1)
        if own:
            o_ = bank[32 * j:32 * j + 32, :]
            for kb in range(2):
                nc.tensor.matmul(o_[:, T:2 * T], sums, pb[:, kb * T:kb * T + T], start=(kb == 0), stop=(kb == 1),
                                 skip_group_check=True)
            yield
            sel_done.wait(nc.tensor, n, i + 1)
            vh = lambda kb: V[p][:, kb, i * D:i * D + D]
            nc.tensor.matmul(o_[:, 0:P], vh(1), pb[:, T:T + P], start=True, stop=False, skip_group_check=True)
            nc.tensor.matmul(o_[:, P:T], vh(1), late[i % 4][:, 1, :], start=False, stop=True, skip_group_check=True)
            inst = nc.tensor.matmul(o_[:, 0:P], vh(0), late[i % 4][:, 0, :], start=False, stop=True,
                                    skip_group_check=True)
        else:
            for pair in range(2):
                if pair:
                    yield
                o_ = bank[64 * pair:64 * pair + 64, :]
                q = pb[:, pair * T:pair * T + T]
                nc.tensor.matmul(o_[:, T:2 * T], sums, q, start=True, stop=True, skip_group_check=True)
                inst = nc.tensor.matmul(o_[:, 0:T], V[p][:, 2 * i + pair, :, :].rearrange("p a d -> p (a d)"), q,
                                        start=True, stop=True, skip_group_check=True)
        av_done.mark(inst)
        if j == 3 or not own:
            av_done.latest(nc.scalar)
            if g == 0:
                epi.full.wait(nc.scalar, n - 1, 1)
            nd_ready.mark(nc.scalar.activation(ndT[p][:, g, :], bank, ACT.Copy))
        yield

    def epilogue(n, p):
        SE.begin(n)
        nd_ready.wait(nc.tensor, n, G)
        for t in range(2):
            bank = epi.claim()
            for g in range(G):
                inst = nc.tensor.transpose(bank[:, g * P:g * P + P], ndT[p][:, g, T + t * P:T + t * P + P], pr.ident[:, :])
            epi.filled(inst)
            epi.drain("v")
            epi.drained("v", nc.vector.reciprocal(rden[:, t, :], bank.rearrange("p (h d) -> p h d", d=D)[:, :, 0]))
            yield
            bank = epi.claim()
            for g in range(G):
                inst = nc.tensor.transpose(bank[:, g * P:g * P + P], ndT[p][:, g, t * P:t * P + P], pr.ident[:, :])
            epi.filled(inst)
            epi.drain("v")
            epi.out["v"].latest(nc.vector)
            epi.drained("v", nc.vector.tensor_tensor(o[:, t, :, :], bank.rearrange("p (h d) -> p h d", d=D),
                                                     rden[:, t, :].unsqueeze(2).to_broadcast([P, H, D]), ALU.mult))
            yield
            bank = epi.claim()
            flat = o[:, t, :, :].rearrange("p h d -> p (h d)")
            for g in range(G):
                inst = nc.tensor.transpose(bank[:, g * P:g * P + P], flat[:, g * P:g * P + P], pr.ident[:, :])
            epi.filled(inst)
            epi.drain("a")
            epi.drained("a", nc.scalar.activation(oT[:, :, t * P:t * P + P], bank.rearrange("p (g t) -> p g t", g=G),
                                                  ACT.Copy))
            yield
        bank = epi.claim()
        for t in range(2):
            for g in range(G):
                inst = nc.tensor.matmul(bank[:, t * P:t * P + P], oT[:, g, t * P:t * P + P], w["li1"][:, g, :],
                                        start=(t == 0 and g == 0), stop=(g == G - 1), skip_group_check=True)
        epi.filled(inst)
        epi.drain("v")
        un, xon, xn, r = two(u, n), two(xo, n), two(xs, n), res[:, :, :]
        epi.drained("v", nc.vector.tensor_tensor(r, bank[:, 0:T].rearrange("p (t c) -> p t c", t=2), row2(w["li1_b"]),
                                                 ALU.add))
        epi.out["v"].latest(nc.vector)
        chain_e(nc.vector.tensor_tensor(xon, un, r, ALU.add))
        if own:
            chain_e(nc.vector.tensor_tensor(un, un, xon, ALU.add))
        else:
            chain_e(nc.vector.tensor_tensor(r, un, xon, ALU.add))
            chain_e(nc.vector.tensor_tensor(xn, xn, r, ALU.add))
        yield

    LAG = 2 if own else 1

    def main(n, p):
        SM.begin(n)
        nm_placed.wait_all(nc.tensor, n)
        for i in range(units + LAG):
            if i < units:
                scores(n, p, i)
                yield
            if i >= LAG:
                yield from values(n, p, i - LAG)

    run_pipeline(pr, tag, B, normed, prologue, main, epilogue)


def mha_ffn(pr, mem, tag, pre, dst):
    nc, io = pr.nc, pr.io
    q = lambda x: io[f"L1_xattn_{pre}_{x}"]
    sem = pr.nc.alloc_semaphore(tag + "_w")
    li2 = pr.sb(tag + "_li2", [P, HID], F32, mem)
    li3 = pr.sb(tag + "_li3", [P, K4, C], F32, mem)
    cols = pr.sb(tag + "_cols", [P, 2, 1], F32, mem)
    b2 = pr.sb(tag + "_b2", [P, K4], F32, mem)
    bias = pr.sb(tag + "_bias", [P, K4], F32, mem)
    b3 = pr.sb(tag + "_b3", [P, C], F32, mem)
    load(pr, li2[:, :], q("li2_w"), sem)
    load(pr, li3[:, :, :], q("li3_w"), sem)
    load(pr, cols[:, 0, :], q("ln3_g").unsqueeze(1), sem)
    load(pr, cols[:, 1, :], q("ln3_b").unsqueeze(1), sem)
    load(pr, b2[:, :], q("li2_b"), sem)
    load(pr, b3[:, :], q("li3_b").partition_broadcast(P), sem)
    nc.sync.wait_ge(sem, 96)
    pr.fence()
    fold_weights(pr, mem, tag, [(li2[:, :], cols[:, 0, :], cols[:, 1, :], bias[:, :], b2[:, :])], None)
    pr.fence()
    feed_forward(pr, mem, tag, pr.xo, dst, [(li2, None, bias)], [], li3, None, b3[:, :])


E = 8
CAP = 640
CT = CAP // P


def moe(pr, mem):
    nc, io, psum, xn = pr.nc, pr.io, pr.psum, pr.u
    tokens_in = nc.dram_tensor("expert_in", [E * CAP + TILES * P, C], F32).ap()
    tokens_out = nc.dram_tensor("expert_out", [E * CAP, C], F32).ap()
    sem = pr.nc.alloc_semaphore("m_w")
    gate_w = pr.sb("m_gate_w", [P, E], F32, mem)
    gate_b = pr.sb("m_gate_b", [P, E], F32, mem)
    logits = pr.sb("m_logits", [P, TILES, E], F32, mem)
    load(pr, gate_w[:, :], io["gate_wT"], sem)
    load(pr, gate_b[:, :], io["L1_ffn_gate_b"].partition_broadcast(P), sem)
    nc.sync.wait_ge(sem, 32)

    zero = pr.sb("m_zero", [P, CT, C], F32, mem)
    s_zero, s_zeroed = pr.nc.alloc_semaphore("m_z0"), pr.nc.alloc_semaphore("m_z1")
    nc.vector.memset(zero[:, :, :], 0.0).then_inc(s_zero, 1)
    nc.sync.wait_ge(s_zero, 1)
    by_tile = lambda m, e: m[bass.ds(e * CAP, CAP), :].rearrange("(t p) c -> p t c", p=P)
    with nc.sync.Fori(0, E) as e:
        nc.sync.dma_start(by_tile(tokens_in, e), zero[:, :, :]).then_inc(s_zeroed, 16)
    pr.fence()

    SP, SM = Stage(pr, "mp"), Stage(pr, "mm")
    ln = LayerNorm(pr, SP, "ln", 4, mem)
    z = pr.sb("m_z", [P, 4, C], F32, mem)
    zT = pr.sb("m_zT", [P, N4], F32, mem)
    pro, out = Ring(SP, "pro", [psum[:, 0, :]]), Ring(SP, "out", [psum[:, 1, :]])
    z_ready, copied = SP.counter("z"), SP.counter("copied")

    def route(n, p, left):
        SP.begin(n)
        tokens = pr.x[:, bass.ds(n * 4, 4), :]
        ln(tokens)
        copied.wait_all(nc.vector, n - 1)
        z_ready.mark(ln.normalise(z, tokens))
        z_ready.latest(nc.scalar)
        copied.mark(nc.scalar.activation(xn[:, bass.ds(n * 4, 4), :], z[:, :, :], ACT.Copy))
        z_ready.latest(nc.tensor)
        bank = pro.claim()
        for t in range(4):
            inst = nc.tensor.transpose(bank[:, t * P:t * P + P], z[:, t, :], pr.ident[:, :])
        pro.filled(inst)
        pro.drain("v")
        pro.drained("v", nc.vector.tensor_copy(zT[:, :], bank))
        pro.out["v"].latest(nc.tensor)
        bank = out.claim()
        for t in range(4):
            inst = nc.tensor.matmul(bank[:, t * E:t * E + E], zT[:, t * P:t * P + P], gate_w[:, :], start=(t == 0),
                                    stop=True, skip_group_check=True)
        out.filled(inst)
        out.drain("v")
        out.drained("v", nc.vector.tensor_tensor(logits[:, bass.ds(n * 4, 4), :],
                                                 bank[:, 0:4 * E].rearrange("p (t e) -> p t e", e=E),
                                                 gate_b[:, :].unsqueeze(1).to_broadcast([P, 4, E]), ALU.add))

    pipeline(nc, TILES // 4, route)
    pr.fence()

    small = lambda name, *shape: pr.sb("m_" + name, [P, *shape], F32, mem)
    d, pe_, pick, hot, count, scan = (small(x, TILES, E) for x in ("d", "pe", "pick", "hot", "count", "scan"))
    iota_e, tri, token = small("iota_e", TILES, E), small("tri", P), small("token", TILES)
    top, total, idx, place, keep, gate, row, back, tmp = (
        small(x, TILES) for x in ("top", "total", "idx", "place", "keep", "gate", "row", "back", "tmp"))
    iota_i = pr.sb("m_iota_i", [P, TILES, E], mybir.dt.int32, mem)
    token_i = pr.sb("m_token_i", [P, TILES], mybir.dt.int32, mem)
    row_u, back_u = pr.sb("m_row_u", [P, TILES], U32, mem), pr.sb("m_back_u", [P, TILES], U32, mem)
    sv, sg, st_, sa = (pr.nc.alloc_semaphore("m_" + x) for x in ("v", "g", "t", "a"))
    nv = [0]

    def v(inst):
        nv[0] += 1
        inst.then_inc(sv, 1)
        nc.vector.wait_ge(sv, nv[0])

    wide = lambda m: m[:, :].unsqueeze(2).to_broadcast([P, TILES, E])
    flat = lambda m: m[:, :, :].rearrange("p t e -> p (t e)")
    nc.gpsimd.iota(iota_i[:, :, :], [[0, TILES], [1, E]], base=0, channel_multiplier=0).then_inc(sg, 1)
    nc.gpsimd.iota(token_i[:, :], [[P, TILES]], base=0, channel_multiplier=1).then_inc(sg, 1)
    nc.gpsimd.affine_select(out=tri[:, :], in_=pr.ones[:, :], compare_op=ALU.is_ge, fill=0.0, base=0,
                            pattern=[[1, P]], channel_multiplier=-1).then_inc(sg, 1)
    v(nc.vector.tensor_reduce(tmp[:, :], logits[:, :, :], X, ALU.max))
    v(nc.vector.tensor_tensor(d[:, :, :], logits[:, :, :], wide(tmp), ALU.subtract))
    nc.scalar.wait_ge(sv, nv[0])
    nc.scalar.activation(pe_[:, :, :], d[:, :, :], ACT.Exp).then_inc(sa, 1)
    nc.vector.wait_ge(sg, 3)
    v(nc.vector.tensor_copy(iota_e[:, :, :], iota_i[:, :, :]))
    v(nc.vector.tensor_copy(token[:, :], token_i[:, :]))
    v(nc.vector.tensor_scalar(pick[:, :, :], d[:, :, :], 0.0, float(E), ALU.is_ge, ALU.mult))
    v(nc.vector.tensor_tensor(pick[:, :, :], iota_e[:, :, :], pick[:, :, :], ALU.subtract))
    v(nc.vector.tensor_reduce(idx[:, :], pick[:, :, :], X, ALU.min))
    v(nc.vector.tensor_tensor(hot[:, :, :], pick[:, :, :], wide(idx), ALU.is_equal))
    nc.tensor.wait_ge(sv, nv[0])
    nc.tensor.wait_ge(sg, 3)
    nc.tensor.matmul(psum[:, 0, 0:TILES * E], tri[:, :], flat(hot), start=True, stop=True)
    nc.tensor.matmul(psum[:, 1, 0:TILES * E], pr.ones[:, :], flat(hot), start=True, stop=True).then_inc(st_, 1)
    nc.vector.wait_ge(sa, 1)
    v(nc.vector.tensor_reduce(total[:, :], pe_[:, :, :], X, ALU.add))
    v(nc.vector.reciprocal(top[:, :], total[:, :]))
    nc.vector.wait_ge(st_, 1)
    v(nc.vector.tensor_copy(flat(count), psum[:, 1, 0:TILES * E]))
    for e in range(E):
        inst = nc.vector.tensor_tensor_scan(scan[:, :, e], pr.ones[:, 0:TILES], count[:, :, e], 0.0, ALU.mult, ALU.add)
    v(inst)
    v(nc.vector.tensor_tensor(scan[:, :, :], scan[:, :, :], count[:, :, :], ALU.subtract))
    v(nc.vector.tensor_tensor(flat(count), psum[:, 0, 0:TILES * E], flat(scan), ALU.add))
    v(nc.vector.tensor_tensor(count[:, :, :], count[:, :, :], hot[:, :, :], ALU.mult))
    v(nc.vector.tensor_reduce(place[:, :], count[:, :, :], X, ALU.add))
    v(nc.vector.tensor_scalar(place[:, :], place[:, :], -1.0, None, ALU.add))
    v(nc.vector.tensor_scalar(keep[:, :], place[:, :], float(CAP), None, ALU.is_lt))
    v(nc.vector.tensor_tensor(gate[:, :], top[:, :], keep[:, :], ALU.mult))
    v(nc.vector.tensor_scalar(idx[:, :], idx[:, :], float(E), float(CAP), ALU.add, ALU.mult))
    v(nc.vector.tensor_tensor(tmp[:, :], place[:, :], keep[:, :], ALU.mult))
    v(nc.vector.tensor_tensor(back[:, :], idx[:, :], tmp[:, :], ALU.add))
    v(nc.vector.tensor_scalar(token[:, :], token[:, :], float(E * CAP), None, ALU.add))
    v(nc.vector.tensor_tensor(tmp[:, :], back[:, :], token[:, :], ALU.subtract))
    v(nc.vector.tensor_tensor(tmp[:, :], tmp[:, :], keep[:, :], ALU.mult))
    v(nc.vector.tensor_tensor(row[:, :], tmp[:, :], token[:, :], ALU.add))
    v(nc.vector.tensor_copy(row_u[:, :], row[:, :]))
    v(nc.vector.tensor_copy(back_u[:, :], back[:, :]))

    s_there = pr.nc.alloc_semaphore("m_there")
    nc.gpsimd.wait_ge(sv, nv[0])
    nc.gpsimd.wait_ge(s_zeroed, 16 * E)
    for t in range(TILES):
        nc.gpsimd.indirect_dma_start(out=tokens_in, out_offset=bass.IndirectOffsetOnAxis(ap=row_u[:, t:t + 1], axis=0),
                                     in_=xn[:, t, :], in_offset=None).then_inc(s_there, 16)
    nc.sync.wait_ge(s_there, 16 * TILES)

    w1 = [pr.sb(f"m_w1_{i}", [P, HID], F32, mem) for i in range(2)]
    w2 = [pr.sb(f"m_w2_{i}", [P, K4, C], F32, mem) for i in range(2)]
    b1 = [pr.sb(f"m_b1_{i}", [P, K4], F32, mem) for i in range(2)]
    b2 = [pr.sb(f"m_b2_{i}", [P, C], F32, mem) for i in range(2)]
    xt = [pr.sb(f"m_xt{i}", [P, CT, C], F32, mem) for i in range(2)]
    xT = [pr.sb(f"m_xT{i}", [P, CAP], F32, mem) for i in range(2)]
    hT = pr.sb("m_hT", [P, K4, CAP], F32, mem)
    ys = pr.sb("m_ys", [P, CT, C], F32, mem)
    SL, SX = Stage(pr, "el"), Stage(pr, "ex")
    loaded = SL.counter("loaded", 16)
    xT_full, xT_out = SL.counter("xT_full"), SL.counter("xT_out")
    h_full, h_out, y_full, y_out = (SX.counter(x) for x in ("h_full", "h_out", "y_full", "y_out"))
    stored = SX.counter("stored", 16)
    HALF = CAP // 2

    def fetch(n, p):
        SL.begin(n)
        y_out.wait_all(nc.sync, n - 2)
        loaded.wait_all(nc.sync, n - 1)
        one = lambda name: io["L1_ffn_" + name][bass.ds(n, 1), :, :].rearrange("e p f -> (e p) f")
        loaded.mark(nc.sync.dma_start(xt[p][:, :, :], by_tile(tokens_in, n)))
        loaded.mark(nc.sync.dma_start(w1[p][:, :], one("w1")))
        loaded.mark(nc.sync.dma_start(b1[p][:, :], one("b1")))
        loaded.mark(nc.sync.dma_start(w2[p][:, :, :].rearrange("p k c -> p (k c)"), one("w2")))
        loaded.mark(nc.sync.dma_start(b2[p][:, :], one("b2").partition_broadcast(P).rearrange("q e c -> q (e c)")))
        yield
        loaded.wait_all(nc.tensor, n)
        xT_out.wait_all(nc.tensor, n - 1)
        for t in range(CT):
            inst = nc.tensor.transpose(psum[:, t // 4, (t % 4) * P:(t % 4) * P + P], xt[p][:, t, :], pr.ident[:, :])
        xT_full.mark(inst)
        xT_full.latest(nc.vector)
        nc.vector.tensor_copy(xT[p][:, 0:N4], psum[:, 0, :])
        xT_out.mark(nc.vector.tensor_copy(xT[p][:, N4:CAP], psum[:, 1, 0:CAP - N4]))
        yield

    def expert(n, p):
        SX.begin(n)
        xT_out.wait_all(nc.tensor, n)
        for m in range(K4):
            h_out.wait(nc.tensor, n, m - 1)
            b = 2 + 2 * (m % 2)
            for half in range(2):
                inst = nc.tensor.matmul(psum[:, b + half, 0:HALF], w1[p][:, m * P:m * P + P],
                                        xT[p][:, half * HALF:half * HALF + HALF], start=True, stop=True)
            h_full.mark(inst)
            h_full.latest(nc.scalar)
            loaded.wait_all(nc.scalar, n)
            h_out.mark(nc.scalar.activation(hT[:, m, :].rearrange("p (a f) -> p a f", a=2), psum[:, b:b + 2, 0:HALF],
                                            ACT.Relu, bias=b1[p][:, m:m + 1]))
            yield
        y_out.wait_all(nc.tensor, n - 1)
        for t in range(CT):
            for k in range(K4):
                if t == 0:
                    h_out.wait(nc.tensor, n, k + 1)
                inst = nc.tensor.matmul(psum[:, 6 + t // 4, (t % 4) * P:(t % 4) * P + P], hT[:, k, t * P:t * P + P],
                                        w2[p][:, k, :], start=(t % 4 == 0 and k == 0), stop=(k == K4 - 1),
                                        skip_group_check=True)
        y_full.mark(inst)
        y_full.latest(nc.vector)
        loaded.wait_all(nc.vector, n)
        stored.wait(nc.vector, n - 1, 1)
        b2w = lambda t: b2[p][:, :].unsqueeze(1).to_broadcast([P, t, C])
        nc.vector.tensor_tensor(ys[:, 0:4, :], psum[:, 6, :].rearrange("p (t c) -> p t c", c=C), b2w(4), ALU.add)
        y_out.mark(nc.vector.tensor_tensor(ys[:, 4, :], psum[:, 7, 0:C], b2[p][:, :], ALU.add))
        y_out.latest(nc.sync)
        stored.mark(nc.sync.dma_start(by_tile(tokens_out, n), ys[:, :, :]))
        yield

    def step(n, p, left):
        ahead = [("fetch", fetch(n + 1, 1 - p), 0.1, 0.6)] if left else []
        weave(pr, ("expert", expert(n, p), 0.0, 1.0), *ahead)

    finish(fetch(0, 0))
    pipeline(nc, E, step)
    stored.wait_all(nc.gpsimd, E - 1)

    s_back = pr.nc.alloc_semaphore("m_back")
    for t in range(TILES):
        nc.gpsimd.indirect_dma_start(out=xn[:, t, :], out_offset=None, in_=tokens_out,
                                     in_offset=bass.IndirectOffsetOnAxis(ap=back_u[:, t:t + 1], axis=0))\
            .then_inc(s_back, 16)
    nc.vector.wait_ge(s_back, 16 * TILES)
    for t in range(TILES):
        inst = nc.vector.scalar_tensor_tensor(out=pr.x[:, t, :], in0=xn[:, t, :], scalar=gate[:, t:t + 1],
                                              in1=pr.x[:, t, :], op0=ALU.mult, op1=ALU.add)
    inst.then_inc(sv, 1)
    pr.fence()


def program(nc, io, out, per, upto=4):
    with ExitStack() as ctx:
        pr = Prog(nc, ctx, per, io)
        pr.psum = ctx.enter_context(nc.psum_tensor("psum", [P, 8, 512], F32))
        constants(pr)
        pr.x = pr.sb("x_sb", [P, TILES, C])
        io_in = ctx.enter_context(nc.semaphore("io_in"))
        io_out = ctx.enter_context(nc.semaphore("io_out"))
        nc.sync.dma_start(pr.x[:, :, :], io["x"].rearrange("b (t p) c -> p (b t) c", p=P)).then_inc(io_in, 16)
        pr.ctxT = pr.sb("ctxT", [CC, B, TC])
        nc.sync.dma_start(pr.ctxT[:, :, :], io["ctxT"]).then_inc(io_in, 16)
        nc.sync.wait_ge(io_in, 32)
        pr.fence()
        with pr.phase() as mem:
            l0_attention(pr, mem)
        if upto >= 2:
            with pr.phase() as mem:
                l0_ffn(pr, mem)
        if upto >= 3:
            pr.u = pr.sb("u_sb", [P, TILES, C])
            pr.xo = pr.sb("xo_sb", [P, TILES, C])
            pr.ctx2 = pr.sb("ctx2", [P, B, CC])
            for a in range(2):
                nc.sync.dma_start(pr.ctx2[TC * a:TC * a + TC, :, :], io["ctx"]).then_inc(io_in, 16)
            nc.sync.wait_ge(io_in, 64)
            pr.fence()
            for tag, own, dst in (("b", True, pr.u), ("c", False, pr.x)):
                with pr.phase() as mem:
                    mha_attention(pr, mem, tag, own)
                with pr.phase() as mem:
                    mha_ffn(pr, mem, tag + "f", "a1" if own else "a2", dst)
        if upto >= 4:
            with pr.phase() as mem:
                moe(pr, mem)
        nc.sync.dma_start(out.rearrange("b (t p) c -> p (b t) c", p=P), pr.x[:, :, :]).then_inc(io_out, 16)
        nc.sync.wait_ge(io_out, 16)
        return pr.seen


def by_chunk(v):
    return np.ascontiguousarray(v.reshape(-1, P, *v.shape[1:]).swapaxes(0, 1))


def ffn_layout(k, v):
    if k.endswith("_w"):
        v = by_chunk(v.T)
        return np.ascontiguousarray(v[:, 0]) if v.shape[1] == 1 else v
    return v if k.endswith("w3_s") else by_chunk(v)


def layout(inputs):
    a = {k: np.ascontiguousarray(v) for k, v in inputs.items()}
    for k, v in list(a.items()):
        if k.startswith("L0_ffn_"):
            a[k] = ffn_layout(k, v)
        elif k[-3:] in ("_wq", "_wk", "_wv"):
            a[k] = np.ascontiguousarray(v.transpose(1, 0, 2).reshape(v.shape[1], -1))
        elif k.endswith(("li1_w", "li3_w", "li2_b")):
            a[k] = by_chunk(v)
    for k in ("w2", "b1", "b2"):
        v = a["L1_ffn_" + k].reshape(E, -1, P if k == "b1" else C)
        a["L1_ffn_" + k] = np.ascontiguousarray(
            v if k == "b2" else v.transpose(0, 2, 1) if k == "b1" else
            v.reshape(E, K4, P, C).transpose(0, 2, 1, 3).reshape(E, P, K4 * C))
    a["gate_wT"] = np.ascontiguousarray(a.pop("L1_ffn_gate_w").T)
    a["ctx"] = np.ascontiguousarray(a["ctx_512"].transpose(1, 0, 2))
    a["ctxT"] = np.ascontiguousarray(a.pop("ctx_512").transpose(2, 0, 1))
    return a


def kernel(**inputs):
    import concourse.bacc as bacc
    from concourse.bass_utils import run_bass_kernel_spmd

    arrays = layout({k: np.asarray(v) for k, v in inputs.items()})
    per = {}
    for _ in range(2):
        nc = bacc.Bacc("TRN2", target_bir_lowering=False, num_devices=1)
        io = {k: nc.dram_tensor(f"in_{k}_dram", v.shape, mybir.dt.from_np(v.dtype), kind="ExternalInput").ap()
              for k, v in arrays.items()}
        out = nc.dram_tensor("out_0_dram", (B, T, C), F32, kind="ExternalOutput").ap()
        per = program(nc, io, out, per)
    r = run_bass_kernel_spmd(nc, [{f"in_{k}_dram": v for k, v in arrays.items()}], core_ids=[0])
    return r.results[0]["out_0_dram"]
```

```python
from contextlib import ExitStack, contextmanager

import numpy as np

import concourse.bass as bass
from concourse import mybir
from concourse.alu_op_type import AluOpType as ALU

F32 = mybir.dt.float32
F16 = mybir.dt.float16
BF16 = mybir.dt.bfloat16
U32 = mybir.dt.uint32
ACT = mybir.ActivationFunctionType
X = mybir.AxisListType.X

P = 128
B, T, C, CC, TC = 16, 256, 128, 64, 64
TILES = B * T // P
H = 16
EPS = 1e-5
NEG = -1e30


class Counter:

    def __init__(self, stage, name, unit=1, base=1):
        prog = stage.prog
        self.name, self.unit, self.prog, self.stage = name, unit, prog, stage
        self.sem = prog.nc.alloc_semaphore(name)
        self.per = prog.per.get(name, 0)
        self.k = 0
        self.base = base
        if base:
            prog.nc.gpsimd.sem_inc(self.sem, unit)

    def mark(self, instruction):
        instruction.then_inc(self.sem, self.unit)
        self.k += 1
        self.prog.seen[self.name] = max(self.prog.seen.get(self.name, 0), self.k)
        return self.k

    def latest(self, engine, apart=False):
        self.wait(engine, self.stage.n, self.k, apart)

    def wait(self, engine, n, k, apart=False):
        if self.per == 0:
            return
        value = n * self.per + k
        if not (isinstance(value, int) and value <= 0):
            value = (value + self.base) * self.unit
            engine.wait_ge(self.sem, value)
            if (apart or engine in (self.prog.nc.gpsimd, self.prog.nc.sync)) and not isinstance(value, int):
                engine.nop(nofuse=True)

    def wait_all(self, engine, n):
        self.wait(engine, n, self.per)


class Chain:

    def __init__(self, stage, engine, name):
        self.stage, self.engine = stage, engine
        self.event = stage.counter(name)

    def __call__(self, instruction):
        k = self.event.mark(instruction)
        self.event.wait(self.engine, self.stage.n, k, apart=True)


class Stage:

    def __init__(self, prog, name):
        self.prog, self.name, self.n, self.mine, self.rings = prog, name, 0, [], []

    def counter(self, name, unit=1, base=1):
        s = Counter(self, f"{self.name}_{name}", unit, base)
        self.mine.append(s)
        return s

    def chain(self, engine, name):
        return Chain(self, engine, name)

    def begin(self, n):
        self.n = n
        for s in self.mine:
            s.k = 0
        for r in self.rings:
            r.drains = []


class Prog:
    def __init__(self, nc, ctx, per, io):
        self.nc, self.ctx, self.per, self.io = nc, ctx, per, io
        self.seen, self.turn = {}, 0

    def sb(self, name, shape, dt=F32, ctx=None):
        return (ctx or self.ctx).enter_context(self.nc.sbuf_tensor(name, shape, dt))

    def fence(self):
        self.nc.all_engine_barrier()

    @contextmanager
    def phase(self):
        before = self.nc.snapshot_sems()
        with ExitStack() as mem:
            yield mem
        self.fence()
        self.nc.clear_and_free_semaphores(self.nc.allocated_since(before))
        self.fence()


def finish(gen):
    for _ in gen:
        pass


def weave(prog, *parts):
    left = []
    for name, gen, start, end in parts:
        left.append([start, name, gen, (end - start) / prog.per.get("pieces of " + name, 20), 0])
    while left:
        part = min(left, key=lambda x: x[0])
        try:
            next(part[2])
            part[0] += part[3]
            part[4] += 1
        except StopIteration:
            prog.seen["pieces of " + part[1]] = part[4]
            left.remove(part)


def pipeline(nc, nb, step, tail=1):
    pairs = (nb - 1 - tail) // 2
    step(0, 0, nb - 1)
    with nc.Fori(0, pairs) as j:
        step(j * 2 + 1, 1, nb)
        step(j * 2 + 2, 0, nb)
    for n in range(2 * pairs + 1, nb):
        step(n, n % 2, nb - 1 - n)


class Ring:

    def __init__(self, stage, name, banks):
        self.stage, self.banks, self.nc = stage, banks, stage.prog.nc
        self.full = stage.counter(name + "_full")
        self.out = {e: stage.counter(f"{name}_out_{e}") for e in "va"}
        self.engine = {"v": self.nc.vector, "a": self.nc.scalar}
        self.drains = []
        stage.rings.append(self)

    def claim(self, apart=False):
        turn = len(self.drains)
        if turn < len(self.banks):
            for s in self.out.values():
                s.wait(self.nc.tensor, self.stage.n, 0, apart)
        else:
            s, k = self.drains[turn - len(self.banks)]
            s.wait(self.nc.tensor, self.stage.n, k, apart)
        return self.banks[turn % len(self.banks)]

    def filled(self, inst):
        self.full.mark(inst)

    def drain(self, who):
        self.full.latest(self.engine[who])
        return self.engine[who]

    def drained(self, who, inst):
        self.drains.append((self.out[who], self.out[who].mark(inst)))


STRETCH = {
    "a": ((0.13, 0.63), (0.0, 1.0), (0.36, 0.63), (0.02, 0.82), (0.18, 0.96)),
    "b": ((0.08, 0.62), (0.05, 0.91), (0.11, 0.71), (0.0, 1.0), (0.28, 0.89)),
    "c": ((0.05, 0.8), (0.0, 0.77), (0.08, 0.8), (0.1, 1.0), (0.02, 1.0)),
    "f": ((0.27, 0.6), (0.5, 0.69), (0.18, 0.99)),
    "g": ((0.64, 1.0), (0.39, 0.7), (0.25, 0.66)),
    "r": ((0.02, 0.81), (0.3, 0.9), (0.2, 1.0)),
    "x": ((0.05, 1.0), (0.1, 0.9), (0.5, 1.0)),
}


def run_pipeline(pr, tag, nb, normed, project, prepare, main, epilogue):

    e_, q_, p_, a_, m_ = STRETCH[tag]

    def step(n, p, left):
        parts = []
        if not isinstance(n, int) or n > 0:
            e = epilogue(n - 1, 1 - p)
            next(e)
            parts.append((tag + "e", e, *e_))
        if left >= 1:
            parts.append((tag + "q", prepare(n + 1, 1 - p), *q_))
        if left >= 2:
            parts.append((tag + "p", project(n + 2, p), *p_))
        if left >= 3:
            parts.append((tag + "a", normed(n + 3, 1 - p), *a_))
        weave(pr, *parts, (tag + "m", main(n, p), *m_))

    pr.fence()
    finish(normed(0, 0))
    finish(project(0, 0))
    finish(normed(1, 1))
    weave(pr, (tag + "q", prepare(0, 0), 0.0, 1.0), (tag + "p", project(1, 1), 0.05, 0.9),
          (tag + "a", normed(2, 0), 0.1, 0.9))
    pipeline(pr.nc, nb, step, tail=3)
    finish(epilogue(nb - 1, (nb - 1) % 2))
    pr.fence()


class LayerNorm:

    def __init__(self, pr, stage, name, tiles, mem, width=C, twice=False):
        nc = pr.nc
        self.pr, self.stage, self.tiles, self.twice = pr, stage, tiles, twice
        name = stage.name + name
        self.stat = pr.sb(name + "_stat", [P, tiles, 6], F32, mem)
        self.mv = pr.sb(name + "_mv", [P, tiles, 2], F32, mem)
        self.tmp = pr.sb(name + "_tmp", [P, 3, tiles], F32, mem)
        self.rstd = pr.sb(name + "_rstd", [P, tiles], F32, mem)
        self.var_ready = stage.counter(name + "_var")
        self.rstd_ready = stage.counter(name + "_rstd")
        self.chain_p = stage.chain(nc.gpsimd, name + "_pow")
        self.chain_v = stage.chain(nc.vector, name + "_stats")

    def __call__(self, src, rows=P):
        nc, n = self.pr.nc, self.stage.n
        mv, tmp = self.mv[0:rows], self.tmp[0:rows]
        for t in range(self.tiles):
            inst = nc.vector.bn_stats(self.stat[0:rows, t, :], src[:, t, :])
        self.chain_v(inst)
        for t in range(self.tiles):
            inst = nc.vector.bn_aggr(mv[:, t, :], self.stat[0:rows, t, :])
        self.chain_v(inst)
        k = self.var_ready.mark(nc.vector.tensor_scalar(tmp[:, 0, :], mv[:, :, 1], EPS, None, ALU.add))
        self.var_ready.wait(nc.gpsimd, n, k)
        half, minus = self.pr.pow_half[0:rows, 0:self.tiles], self.pr.pow_one[0:rows, 0:self.tiles]
        r = self.rstd[0:rows, :]
        if not self.twice:
            k = self.rstd_ready.mark(nc.gpsimd.tensor_tensor(r, tmp[:, 0, :], half, ALU.pow))
        else:
            nc.gpsimd.tensor_tensor(tmp[:, 1, :], tmp[:, 0, :], minus, ALU.pow)
            self.chain_p(nc.gpsimd.tensor_tensor(r, tmp[:, 0, :], half, ALU.pow))
            self.chain_p(nc.gpsimd.tensor_tensor(tmp[:, 2, :], mv[:, :, 1], tmp[:, 1, :], ALU.mult))
            self.chain_p(nc.gpsimd.tensor_scalar(tmp[:, 2, :], tmp[:, 2, :], EPS, None, ALU.add))
            self.chain_p(nc.gpsimd.tensor_tensor(tmp[:, 1, :], tmp[:, 2, :], half, ALU.pow))
            k = self.rstd_ready.mark(nc.gpsimd.tensor_tensor(r, r, tmp[:, 1, :], ALU.mult))

    def normalise(self, out, src, rows=P):
        nc = self.pr.nc
        self.rstd_ready.latest(nc.vector)
        for t in range(self.tiles):
            inst = nc.vector.tensor_scalar(out[:, t, :], src[:, t, :], self.mv[0:rows, t, 0:1],
                                           self.rstd[0:rows, t:t + 1], ALU.subtract, ALU.mult)
        return inst


def constants(pr):
    nc = pr.nc
    pr.ident = pr.sb("ident", [P, P])
    pr.ident16 = pr.sb("ident16", [P, P], F16)
    pr.identb = pr.sb("identb", [P, P], BF16)
    pr.hide_later = pr.sb("hide_later", [P, 4, P], BF16)
    pr.quadrant = pr.sb("quadrant", [P, 4])
    pr.pow_half = pr.sb("pow_half", [P, 8])
    pr.pow_one = pr.sb("pow_one", [P, 8])
    pr.ones = pr.sb("ones", [P, P])
    s = pr.ctx.enter_context(nc.semaphore("const"))
    for m in (pr.ident, pr.ident16, pr.identb):
        nc.gpsimd.memset(m[:, :], 0.0).then_inc(s, 1)
    nc.gpsimd.memset(pr.hide_later[:, :, :], 0.0).then_inc(s, 1)
    nc.gpsimd.memset(pr.pow_half[:, :], -0.5).then_inc(s, 1)
    nc.gpsimd.memset(pr.pow_one[:, :], -1.0).then_inc(s, 1)
    nc.gpsimd.memset(pr.ones[:, :], 1.0).then_inc(s, 1)
    nc.gpsimd.wait_ge(s, 7)
    for m in (pr.ident, pr.ident16, pr.identb):
        nc.gpsimd.affine_select(out=m[:, :], in_=m[:, :], compare_op=ALU.not_equal, fill=1.0, base=0,
                                pattern=[[-1, P]], channel_multiplier=1).then_inc(s, 1)
    nc.gpsimd.affine_select(out=pr.hide_later[:, :, :], in_=pr.hide_later[:, :, :], compare_op=ALU.is_ge,
                            fill=NEG, base=0, pattern=[[0, 4], [-1, P]], channel_multiplier=1).then_inc(s, 1)
    nc.gpsimd.wait_ge(s, 11)
    sq = pr.ctx.enter_context(nc.semaphore("const_q"))
    nc.vector.memset(pr.quadrant[:, :], 0.0).then_inc(sq, 1)
    nc.vector.wait_ge(sq, 1)
    for j in range(4):
        nc.vector.memset(pr.quadrant[32 * j:32 * j + 32, j:j + 1], 1.0).then_inc(sq, 1)
    nc.vector.wait_ge(sq, 5)


def load(pr, dst, src, sem):
    pr.turn ^= 1
    (pr.nc.sync if pr.turn else pr.nc.scalar).dma_start(dst, src).then_inc(sem, 16)


def l0_attention(pr, mem):
    nc, io = pr.nc, pr.io
    D, G, W = 8, 4, 32
    NM = 3 * D
    SCALE = 1.0 / float(np.sqrt(D))
    wload = pr.nc.alloc_semaphore("l0a_w")
    Wcat = pr.sb("a_wcat", [P, 4, C], F32, mem)
    bcat = pr.sb("a_bcat", [P, 4, C], F32, mem)
    Wctx = pr.sb("a_wctx", [CC, 2, C], F32, mem)
    bctx = pr.sb("a_bctx", [P, 2, C], F32, mem)
    Wp = pr.sb("a_wp", [P, C], F32, mem)
    bp = pr.sb("a_bp", [P, 2, C], F32, mem)
    for i, x in enumerate("q cq k v".split()):
        load(pr, Wcat[:, i, :], io["L0_xattn_W" + x], wload)
        load(pr, bcat[:, i, :], io["L0_xattn_b" + x].partition_broadcast(P), wload)
    for i, x in enumerate("ck cv".split()):
        load(pr, Wctx[:, i, :], io["L0_xattn_W" + x], wload)
        load(pr, bctx[:, i, :], io["L0_xattn_b" + x].partition_broadcast(P), wload)
        load(pr, bp[:, i, :], io["L0_xattn_bp"].partition_broadcast(P), wload)
    load(pr, Wp[:, :], io["L0_xattn_Wp"], wload)

    z = [pr.sb(f"a_z{i}", [P, 2, C], F32, mem) for i in range(2)]
    zT = [pr.sb(f"a_zT{i}", [P, T], F32, mem) for i in range(2)]
    ctx2 = [pr.sb(f"a_ctx2{i}", [CC, P], F32, mem) for i in range(2)]
    qf = [pr.sb(f"a_qf{i}", [P, 3, C], F32, mem) for i in range(2)]
    kcf = pr.sb("a_kcf", [CC, C], F32, mem)
    tok = [pr.sb(f"a_tok{i}", [P, 2, 3, H, W], F16, mem) for i in range(2)]
    kctok = [pr.sb(f"a_kctok{i}", [CC, H, W], F16, mem) for i in range(2)]
    QT = [pr.sb(f"a_QT{i}", [P, 2, G, T], F16, mem) for i in range(2)]
    KT = [pr.sb(f"a_KT{i}", [P, 4, G, T], F16, mem) for i in range(2)]
    KcT = [pr.sb(f"a_KcT{i}", [P, G, 4, TC], F16, mem) for i in range(2)]
    V = [pr.sb(f"a_V{i}", [P, 2, H, W], F32, mem) for i in range(2)]
    Vc = [pr.sb(f"a_Vc{i}", [P, H // 2, 2, W // 2], F32, mem) for i in range(2)]
    KTall = pr.sb("a_KTall", [P, G * T], F16, mem)
    nm = pr.sb("a_nm", [P, 2, 4, 2, G], F16, mem)
    nmT = pr.sb("a_nmT", [W, T], F16, mem)
    prob = [pr.sb(f"a_prob{i}", [P, 512], F32, mem) for i in range(4)]
    ysT = [pr.sb(f"a_ysT{i}", [P, 3, 512], F32, mem) for i in range(2)]
    den = pr.sb("a_den", [P, 2, H], F32, mem)
    denc = pr.sb("a_denc", [P, 2, H], F32, mem)
    y = pr.sb("a_y", [P, 2, H, D], F32, mem)
    yc = pr.sb("a_yc", [P, 2, H, D], F32, mem)
    yT = pr.sb("a_yT", [P, T], F32, mem)
    res = pr.sb("a_res", [P, 2, C], F32, mem)
    psum = pr.psum
    s0 = pr.nc.alloc_semaphore("a_init")
    cnt = 0
    for m in [*(m[...] for m in V + Vc), *(m[:, :, :, :, NM:] for m in tok), *(m[:, :, NM:] for m in kctok)]:
        (nc.gpsimd if cnt < 2 else nc.vector).memset(m, 0.0).then_inc(s0, 1)
        cnt += 1
    nc.vector.wait_ge(s0, cnt)
    for i in range(2):
        nc.vector.memset(V[i][:, :, :, D:D + 1], 1.0)
        for a in range(2):
            nc.vector.memset(Vc[i][TC * a:TC * a + TC, :, a, D:D + 1], 1.0)
        nc.vector.memset(tok[i][:, :, 2, :, NM:NM + 1], 1.0)
        inst = nc.vector.memset(kctok[i][:, :, NM:NM + 1], 1.0)
    inst.then_inc(s0, 1)
    nc.vector.wait_ge(s0, cnt + 1)
    nc.sync.wait_ge(wload, 16 * 15)
    pr.fence()

    SA, SP, SQ, SM, SE = (Stage(pr, "a" + x) for x in "apqme")
    ln = LayerNorm(pr, SA, "ln", 2, mem)
    pro = Ring(SP, "pro", [psum[:, 0, :]])
    pre = Ring(SQ, "pre", [psum[:, i, :] for i in (1, 2)])
    z_ready = SA.counter("z")
    ctx_ready, high, low = SP.counter("ctx"), SP.counter("high"), SP.counter("low")
    kt_masked = SQ.counter("kt_masked")
    nm_placed = SQ.counter("nm_placed", 16)
    st_full, exp_done, sel_done, av_done, ys_ready = (SM.counter(x) for x in ("st_full", "exp", "sel", "av", "ys"))
    epi = Ring(SE, "epi", [psum[:, 7, :]])
    chain_e = SE.chain(nc.vector, "chain")
    xs = pr.x

    def parts(ap):
        return ap.rearrange("p (h k d) -> p h k d", k=4, d=D)

    def normed(n, p):
        SA.begin(n)
        src = xs[:, bass.ds(n * 2, 2), :]
        ln(src)
        yield
        pro.full.wait(nc.vector, n - 2, 1)
        z_ready.mark(ln.normalise(z[p], src))
        yield

    def project(n, p):
        SP.begin(n)
        pre.full.wait(nc.gpsimd, n - 2, 3)
        ctx_ready.mark(nc.gpsimd.tensor_copy(ctx2[p][:, :].rearrange("c (a t) -> c a t", a=2),
                       pr.ctxT[:, bass.ds(n, 1), :].to_broadcast([CC, 2, TC])))
        z_ready.wait_all(nc.tensor, n)
        bank = pro.claim()
        for t in range(2):
            inst = nc.tensor.transpose(bank[:, t * P:t * P + P], z[p][:, t, :], pr.ident[:, :])
        pro.filled(inst)
        pro.drain("a")
        pro.drained("a", nc.scalar.activation(zT[p][:, :], bank[:, 0:T], ACT.Copy))
        yield
        for t in range(2):
            bank = pro.claim()
            pro.filled(nc.tensor.matmul(bank[:, 0:3 * C], zT[p][:, t * P:t * P + P],
                                        Wcat[:, 0:3, :].rearrange("p a c -> p (a c)"), start=True, stop=True))
            pro.drain("v")
            low.wait(nc.vector, n - 1, t + 1)
            pro.drained("v", nc.vector.tensor_tensor(qf[t][:, :, :].rearrange("p a c -> p (a c)"), bank[:, 0:3 * C],
                                                     bcat[:, 0:3, :].rearrange("p a c -> p (a c)"), ALU.add))
            pro.out["v"].latest(nc.scalar)
            qtok = parts(tok[p][:, t, 0:2, :, :].rearrange("p a h w -> p (a h w)"))
            ktok = parts(tok[p][:, t, 2, :, :].rearrange("p h w -> p (h w)"))
            q8 = qf[t][:, 0:2, :].rearrange("p a (h d) -> p (a h) d", d=D)
            k8 = qf[t][:, 2, :].rearrange("p (h d) -> p h d", d=D)
            nc.scalar.activation(qtok[:, :, 0:3:2, :], q8.unsqueeze(2).to_broadcast([P, 2 * H, 2, D]), ACT.Copy)
            high.mark(nc.scalar.activation(ktok[:, :, 0:2, :], k8.unsqueeze(2).to_broadcast([P, H, 2, D]), ACT.Copy))
            high.latest(nc.gpsimd)
            nc.gpsimd.tensor_tensor(qtok[:, :, 1, :], q8, qtok[:, :, 0, :], ALU.subtract)
            low.mark(nc.gpsimd.tensor_tensor(ktok[:, :, 2, :], k8, ktok[:, :, 0, :], ALU.subtract))
            yield
        ctx_ready.latest(nc.tensor)
        bank = pro.claim()
        pro.filled(nc.tensor.matmul(bank[:, 0:C], ctx2[p][:, :], Wctx[:, 0, :], start=True, stop=True))
        pro.drain("v")
        pro.drained("v", nc.vector.tensor_tensor(kcf[:, :], bank[0:TC, 0:C], bctx[0:TC, 0, :], ALU.add))
        pro.out["v"].latest(nc.scalar)
        kt_ = parts(kctok[p][:, :, :].rearrange("p h w -> p (h w)"))
        k8 = kcf[:, :].rearrange("p (h d) -> p h d", d=D)
        high.mark(nc.scalar.activation(kt_[:, :, 0:2, :], k8.unsqueeze(2).to_broadcast([TC, H, 2, D]), ACT.Copy))
        high.latest(nc.gpsimd)
        low.mark(nc.gpsimd.tensor_tensor(kt_[:, :, 2, :], k8, kt_[:, :, 0, :], ALU.subtract))
        yield

    def prepare(n, p):
        SQ.begin(n)
        for t in range(2):
            bank = pre.claim()
            pre.filled(nc.tensor.matmul(bank[:, 0:C], zT[p][:, t * P:t * P + P], Wcat[:, 3, :], start=True, stop=True))
            pre.drain("v")
            pre.drained("v", nc.vector.tensor_tensor(V[p][:, t, :, 0:D], bank[:, 0:C].rearrange("p (h d) -> p h d", d=D),
                                                     bcat[:, 3, :].rearrange("p (h d) -> p h d", d=D), ALU.add))
        yield
        bank = pre.claim()
        pre.filled(nc.tensor.matmul(bank[:, 0:C], ctx2[p][:, :], Wctx[:, 1, :], start=True, stop=True))
        pre.drain("v")
        for a in range(2):
            half = slice(TC * a, TC * a + TC)
            inst = nc.vector.tensor_tensor(Vc[p][half, :, a, 0:D],
                                           bank[half, 0:C].rearrange("p (i a d) -> p i a d", a=2, d=D)[:, :, a, :],
                                           bctx[half, 1, :].rearrange("p (i a d) -> p i a d", a=2, d=D)[:, :, a, :],
                                           ALU.add)
        pre.drained("v", inst)
        yield
        low.wait_all(nc.tensor, n)
        for t in range(2):
            bank16 = pre.claim().bitcast(F16)
            for a in range(2):
                for g in range(G):
                    at = (a * G + g) * P
                    inst = nc.tensor.transpose(bank16[:, at:at + P],
                                               tok[p][:, t, a, 4 * g:4 * g + 4, :].rearrange("p h w -> p (h w)"),
                                               pr.ident16[:, :])
            pre.filled(inst)
            pre.drain("a")
            pre.drained("a", nc.scalar.activation(QT[p][:, :, :, t * P:t * P + P].rearrange("p a g t -> p (a g) t"),
                                                  bank16[:, :].rearrange("p (a t) -> p a t", t=P), ACT.Copy))
            yield
        bank16 = pre.claim().bitcast(F16)
        for g in range(G):
            for t in range(2):
                at = (g * 2 + t) * P
                inst = nc.tensor.transpose(bank16[:, at:at + P],
                                           tok[p][:, t, 2, 4 * g:4 * g + 4, :].rearrange("p h w -> p (h w)"),
                                           pr.ident16[:, :])
        pre.filled(inst)
        pre.drain("a")
        kt_masked.wait_all(nc.scalar, n - 1)
        pre.drained("a", nc.scalar.activation(KTall[:, :], bank16[:, :], ACT.Copy))
        pre.out["a"].latest(nc.vector)
        for j in range(4):
            inst = nc.vector.tensor_scalar(KT[p][:, j, :, :].rearrange("p g t -> p (g t)"), KTall[:, :],
                                           pr.quadrant[:, j:j + 1], None, ALU.mult)
        kt_masked.mark(inst)
        yield
        bank16 = pre.claim(apart=True).bitcast(F16)
        for g in range(G):
            inst = nc.tensor.transpose(bank16[:, g * TC:g * TC + TC],
                                       kctok[p][:, 4 * g:4 * g + 4, :].rearrange("p h w -> p (h w)"),
                                       pr.ident16[0:TC, 0:TC])
        pre.filled(inst)
        pre.drain("v")
        for j in range(4):
            inst = nc.vector.tensor_scalar(KcT[p][:, :, j, :],
                                           bank16[:, 0:G * TC].rearrange("p (g t) -> p g t", t=TC),
                                           pr.quadrant[:, j:j + 1], None, ALU.mult)
        pre.drained("v", inst)
        yield
        pre.out["a"].latest(nc.tensor), pre.out["v"].latest(nc.tensor)

        def mx_reduce(bank, out, shape):
            pre.drain("v")
            pre.drained("v", nc.vector.tensor_reduce(out, bank.rearrange("p (a b) -> p a b", a=shape), X, ALU.max,
                                                     negate=True))

        for g in range(G):
            bank = pre.claim()
            for j in range(4):
                nc.tensor.matmul(bank[:, j * P:j * P + P], QT[p][:, 0, g, 0:P], KT[p][:, j, g, 0:P],
                                 start=(j == 0), stop=False, skip_group_check=True)
            pre.filled(nc.tensor.matmul(bank, pr.identb[:, :], pr.hide_later[:, :, :].rearrange("p a k -> p (a k)"),
                                          start=False, stop=True, skip_group_check=True))
            mx_reduce(bank, nm[:, 0, :, 0, g], 4)
            yield
            for jj in range(2):
                bank = pre.claim()
                for a in range(2):
                    nc.tensor.matmul(bank[:, a * T:a * T + T], QT[p][:, 0, g, P:T], KT[p][:, 2 * jj + a, g, :],
                                     start=(a == 0), stop=False, skip_group_check=True)
                diagonal = bank.rearrange("p (a h k) -> p a h k", a=2, h=2)[:, :, 1, :]
                pre.filled(nc.tensor.matmul(diagonal, pr.identb[:, :], pr.hide_later[:, 0:2, :],
                                              start=False, stop=True, skip_group_check=True))
                mx_reduce(bank, nm[:, 1, 2 * jj:2 * jj + 2, 0, g], 2)
                yield
        for t in range(2):
            for c in range(2):
                bank = pre.claim()
                for gg in range(2):
                    g = 2 * c + gg
                    inst = nc.tensor.matmul(bank[:, gg * 256:gg * 256 + 256], QT[p][:, 1, g, t * P:t * P + P],
                                            KcT[p][:, g, :, :].rearrange("p j t -> p (j t)"), start=(gg == 0),
                                            stop=True, skip_group_check=True)
                pre.filled(inst)
                mx_reduce(bank, nm[:, t, :, 1, 2 * c:2 * c + 2].rearrange("p j g -> p g j"), 8)
                yield
        pre.out["v"].latest(nc.tensor)
        bank16 = pre.claim().bitcast(F16)
        for t in range(2):
            inst = nc.tensor.transpose(bank16[0:W, t * P:t * P + P], nm[:, t, :, :, :].rearrange("p j s g -> p (j s g)"),
                                       pr.ident16[:, :])
        pre.filled(inst)
        pre.drain("a")
        nm_placed.wait_all(nc.scalar, n - 1)
        pre.drained("a", nc.scalar.activation(nmT[:, :], bank16[0:W, 0:T], ACT.Copy))
        pre.out["a"].latest(nc.sync)
        for j in range(4):
            nm_placed.mark(nc.sync.dma_start(QT[p][W * j + NM:W * j + NM + 1, :, :, :],
                                             nmT[8 * j:8 * j + 8, :]))
        yield

    units = [("self", h) for h in range(H)] + [("cross", g) for g in range(G)]

    def scores(n, p, i):
        kind, h = units[i]
        exp_done.wait(nc.tensor, n, i - 1)
        bank = psum[:, 3 + i % 2, :]
        if kind == "self":
            g, j = h // 4, h % 4
            nc.tensor.matmul(bank[:, 0:T], KT[p][:, j, g, 0:P], QT[p][:, 0, g, :], start=True, stop=True)
            inst = nc.tensor.matmul(bank[:, T:T + P], KT[p][:, j, g, P:T], QT[p][:, 0, g, P:T], start=False, stop=True,
                                    skip_group_check=True)
        else:
            for a in range(2):
                inst = nc.tensor.matmul(bank[:, a * T:a * T + T],
                                        KcT[p][:, h, 2 * a:2 * a + 2, :].rearrange("p j t -> p (j t)"),
                                        QT[p][:, 1, h, :], start=(a == 0), stop=True, skip_group_check=True)
        st_full.mark(inst)
        width = T + P if kind == "self" else 2 * T
        st_full.latest(nc.scalar)
        av_done.wait(nc.scalar, n, i - 3)
        exp_done.mark(nc.scalar.activation(prob[i % 4][:, 0:width], bank[:, 0:width], ACT.Exp, scale=SCALE))
        if kind == "self":
            exp_done.latest(nc.gpsimd)
            d = prob[i % 4][:, 0:2 * T].rearrange("p (a q) -> p a q", a=2)[:, :, 0:P]
            sel_done.mark(nc.gpsimd.affine_select(out=d, in_=d, compare_op=ALU.is_ge, fill=0.0, base=0,
                                                  pattern=[[0, 2], [1, P]], channel_multiplier=-1))

    def values(n, p, i):
        kind, h = units[i]
        g = h // 4
        pb = prob[i % 4]
        if kind == "self":
            sel_done.wait(nc.tensor, n, i + 1)
            j, use = h % 4, g // 2
            if h % 8 == 0:
                ys_ready.wait(nc.tensor, n, (0, -1)[use])
            o = psum[32 * j:32 * j + 32, 5 + use, (g % 2) * T:(g % 2) * T + T]
            nc.tensor.matmul(o, V[p][:, 0, h, :], pb[:, 0:T], start=True, stop=False, skip_group_check=True)
            inst = nc.tensor.matmul(o[:, P:T], V[p][:, 1, h, :], pb[:, T:T + P], start=False, stop=True,
                                    skip_group_check=True)
        else:
            use = 2
            exp_done.wait(nc.tensor, n, i + 1)
            if h == 0:
                ys_ready.wait(nc.tensor, n, 1)
            for a in range(2):
                q = 2 * (h % 2) + a
                inst = nc.tensor.matmul(psum[32 * q:32 * q + 32, 5, (h // 2) * T:(h // 2) * T + T],
                                        Vc[p][:, 2 * h + a, :, :].rearrange("p a w -> p (a w)"),
                                        pb[:, a * T:a * T + T], start=True, stop=True, skip_group_check=True)
        av_done.mark(inst)
        if (kind, h) in (("self", 7), ("self", 15), ("cross", 3)):
            av_done.latest(nc.scalar)
            if use == 0:
                epi.full.wait(nc.scalar, n - 1, 1)
            ys_ready.mark(nc.scalar.activation(ysT[p][:, use, :], psum[:, 5 + use % 2, :], ACT.Copy))

    def epilogue(n, p):
        SE.begin(n)
        for t in range(2):
            ys_ready.wait(nc.tensor, n, 2)
            bank = epi.claim()
            for g in range(G):
                at = (g % 2) * T + t * P
                inst = nc.tensor.transpose(bank[:, g * P:g * P + P], ysT[p][:, g // 2, at:at + P], pr.ident[:, :])
            epi.filled(inst)
            epi.drain("v")
            heads = bank.rearrange("p (h w) -> p h w", w=W)
            chain_e(nc.vector.reciprocal(den[:, t, :], heads[:, :, D]))
            epi.drained("v", nc.vector.tensor_tensor(y[:, t, :, :], heads[:, :, 0:D],
                                                     den[:, t, :].unsqueeze(2).to_broadcast([P, H, D]), ALU.mult))
            yield
        ys_ready.wait(nc.tensor, n, 3)
        bank = epi.claim()
        for t in range(2):
            for c in range(2):
                inst = nc.tensor.transpose(bank[:, t * T + c * P:t * T + c * P + P],
                                           ysT[p][:, 2, c * T + t * P:c * T + t * P + P], pr.ident[:, :])
        epi.filled(inst)
        epi.drain("v")
        heads = bank.rearrange("p (t w) -> p t w", w=W // 2)
        denf = denc[:, :, :].rearrange("p t h -> p (t h)")
        chain_e(nc.vector.reciprocal(denf, heads[:, :, D]))
        epi.drained("v", nc.vector.tensor_tensor(yc[:, :, :, :].rearrange("p t h d -> p (t h) d"), heads[:, :, 0:D],
                                                 denf.unsqueeze(2).to_broadcast([P, 2 * H, D]), ALU.mult))
        epi.out["v"].latest(nc.vector)
        flat = lambda m: m[:, :, :, :].rearrange("p t h d -> p (t h d)")
        chain_e(nc.vector.tensor_tensor(flat(y), flat(y), flat(yc), ALU.add))
        yield
        chain_e.event.latest(nc.tensor)
        bank = epi.claim()
        for t in range(2):
            inst = nc.tensor.transpose(bank[:, t * P:t * P + P], y[:, t, :, :].rearrange("p h d -> p (h d)"), pr.ident[:, :])
        epi.filled(inst)
        epi.drain("a")
        epi.drained("a", nc.scalar.activation(yT[:, :], bank[:, 0:T], ACT.Copy))
        yield
        bank = epi.claim()
        for t in range(2):
            inst = nc.tensor.matmul(bank[:, t * P:t * P + P], yT[:, t * P:t * P + P], Wp[:, :], start=(t == 0), stop=True,
                                    skip_group_check=True)
        epi.filled(inst)
        epi.drain("v")
        epi.drained("v", nc.vector.tensor_tensor(res[:, :, :].rearrange("p t c -> p (t c)"), bank[:, 0:T],
                                                 bp[:, :, :].rearrange("p t c -> p (t c)"), ALU.add))
        epi.out["v"].latest(nc.vector)
        dst = xs[:, bass.ds(n * 2, 2), :]
        chain_e(nc.vector.tensor_tensor(dst, dst, res[:, :, :], ALU.add))
        yield

    LAG = 3

    def main(n, p):
        SM.begin(n)
        nm_placed.wait_all(nc.tensor, n)
        for i in range(len(units) + LAG):
            if i < len(units):
                scores(n, p, i)
                yield
            if i >= LAG:
                values(n, p, i - LAG)
                yield

    run_pipeline(pr, "a", B, normed, project, prepare, main, epilogue)


HID = 512
K4 = HID // P
N4 = 4 * P


def passes(w, x):
    return [(w[0], x[0])] if len(w) == 1 else [(w[0], x[0]), (w[0], x[1]), (w[1], x[0])]


def feed_forward(pr, mem, tag, src, dst, first, middle, last, out_scale, out_bias, meanwhile=None):
    nc, psum = pr.nc, pr.psum
    gated, split = len(first) == 2, len(last) == 2

    def buffers(name, shape):
        return [pr.sb(f"{tag}_{name}{x}", shape, F16 if split else F32, mem) for x in ("h", "l")[:len(last)]]

    z = [pr.sb(f"{tag}_z{i}", [P, 4, C], F32, mem) for i in range(2)]
    zT = [buffers(f"zT{i}", [P, N4]) for i in range(2)]
    gate = [pr.sb(f"{tag}_gate{i}", [P, N4], F32, mem) for i in range(2)] if gated else None
    whole = [pr.sb(f"{tag}_whole{i}", [P, N4], F32, mem) for i in range(2)] if split else None
    hT = [buffers(f"hT{i}", [P, K4, N4]) for i in range(2)] if middle else None
    hlast = [buffers(f"hlast{i}", [P, K4, N4]) for i in range(2)]
    res = pr.sb(tag + "_res", [P, 4, C], F32, mem)
    SA, SP, SM, SE = (Stage(pr, tag + x) for x in "apme")
    ln = LayerNorm(pr, SA, "ln", 4, mem)
    pro = Ring(SP, "pro", [psum[:, 0, :]])
    z_ready, zT_high = SA.counter("z"), SP.counter("zT_high")
    full, out_a, out_v, low = (SM.counter(x) for x in ("full", "out_a", "out_v", "low"))
    y_full, y_out = SE.counter("y_full"), SE.counter("y_out")
    chain = SE.chain(nc.vector, "chain")
    RING = 4

    def normed(n, p):
        SA.begin(n)
        tokens = src[:, bass.ds(n * 4, 4), :]
        ln(tokens)
        yield
        pro.full.wait(nc.vector, n - 2, 1)
        z_ready.mark(ln.normalise(z[p], tokens))
        yield

    def prologue(n, p):
        SP.begin(n)
        z_ready.wait_all(nc.tensor, n)
        bank = pro.claim()
        for t in range(4):
            inst = nc.tensor.transpose(bank[:, t * P:t * P + P], z[p][:, t, :], pr.ident[:, :])
        pro.filled(inst)
        if split:
            pro.drain("a")
            zT_high.mark(nc.scalar.activation(zT[p][0][:, :], bank, ACT.Copy))
            zT_high.latest(nc.vector)
            pro.drained("v", nc.vector.tensor_tensor(zT[p][1][:, :], bank, zT[p][0][:, :], ALU.subtract))
        else:
            pro.drain("v")
            pro.drained("v", nc.vector.tensor_copy(zT[p][0][:, :], bank))
        yield

    def main(n, p):
        SM.begin(n)
        drains = []

        def product(w, x, at, chunks=1):
            u = len(drains)
            if u >= RING:
                s, k = drains[u - RING]
                s.wait(nc.tensor, n, k)
            else:
                out_a.wait(nc.tensor, n, 0), out_v.wait(nc.tensor, n, 0)
            bank = psum[:, 1 + u % RING, :]
            for k in range(chunks):
                if chunks > 1 and at == 0:
                    ready[k][0].wait(nc.tensor, n, ready[k][1])
                pairs = passes(w, x)
                for i, (wi, xi) in enumerate(pairs):
                    lhsT = wi[:, at:at + P] if chunks == 1 else wi[:, k, at:at + P]
                    inst = nc.tensor.matmul(bank, lhsT, xi[:, :] if chunks == 1 else xi[:, k, :],
                                            start=(k == 0 and i == 0), stop=(k == chunks - 1 and i == len(pairs) - 1))
            full.mark(inst)
            return bank

        def activate(bank, out, m, func, **how):
            full.latest(nc.scalar)
            if not split:
                k = out_a.mark(nc.scalar.activation(out[0][:, m, :], bank, func, **how))
                drains.append((out_a, k))
                return out_a, k
            low.wait(nc.scalar, n, low.k - 1)
            nc.scalar.activation(whole[m % 2][:, :], bank, func, **how)
            drains.append((out_a, out_a.mark(nc.scalar.activation(out[0][:, m, :], bank, func, **how))))
            out_a.latest(nc.vector)
            return low, low.mark(nc.vector.tensor_tensor(out[1][:, m, :], whole[m % 2][:, :], out[0][:, m, :],
                                                         ALU.subtract))

        pro.out["v"].wait_all(nc.tensor, n)
        ready = []
        out = hT[0] if middle else hlast[p]
        late = None
        for m in range(K4):
            if not gated:
                w, scale, bias = first[0]
                ready.append(activate(product(w, zT[p], m * P), out, m, ACT.Gelu, bias=bias[:, m:m + 1]))
                yield
                continue
            (wa, sa, _), (wb, sb, _) = first
            bank = product(wa, zT[p], m * P)
            full.latest(nc.scalar)
            if m >= 2:
                out_v.latest(nc.scalar)
            drains.append((out_a, out_a.mark(nc.scalar.activation(gate[m % 2][:, :], bank, ACT.Silu,
                                                                  scale=sa[:, m:m + 1]))))
            gate_done = out_a.k
            yield
            bank = product(wb, zT[p], m * P)
            full.latest(nc.vector)
            out_a.wait(nc.vector, n, gate_done)
            low.latest(nc.vector)
            k = out_v.mark(nc.vector.scalar_tensor_tensor(whole[m % 2][:, :], bank, sb[:, m:m + 1], gate[m % 2][:, :],
                                                          ALU.mult, ALU.mult))
            drains.append((out_v, k))
            out_v.wait(nc.scalar, n, k)
            high = out_a.mark(nc.scalar.activation(out[0][:, m, :], whole[m % 2][:, :], ACT.Copy))
            if late:
                late()

            def late(m=m, high=high):
                out_a.wait(nc.vector, n, high)
                ready.append((low, low.mark(nc.vector.tensor_tensor(out[1][:, m, :], whole[m % 2][:, :],
                                                                    out[0][:, m, :], ALU.subtract))))
            yield
        if late:
            late()
        for layer, (w, scale) in enumerate(middle):
            x, out = out, hlast[p] if layer == len(middle) - 1 else hT[1 - layer]
            now = []
            for m in range(K4):
                now.append(activate(product(w, x, m * P, K4), out, m, ACT.Gelu, scale=scale[:, m:m + 1]))
                yield
            ready[:] = now

    def closing(n, p):
        SE.begin(n)
        out_a.wait_all(nc.tensor, n), low.wait_all(nc.tensor, n)
        bank = psum[:, 5 + p, :]
        y_out.wait(nc.tensor, n, 0)
        for t in range(4):
            for k in range(K4):
                for i, (wi, xi) in enumerate(passes(last, hlast[p])):
                    inst = nc.tensor.matmul(bank[:, t * P:t * P + P], xi[:, k, t * P:t * P + P], wi[:, k, :],
                                            start=(t == 0 and k == 0 and i == 0), stop=True, skip_group_check=True)
            if t == 3:
                y_full.mark(inst)
            yield
        y_full.latest(nc.vector)
        tokens, r = dst[:, bass.ds(n * 4, 4), :], res[:, :, :]
        bank = bank.rearrange("p (t c) -> p t c", t=4)
        row, op = (out_scale, ALU.mult) if out_scale is not None else (out_bias, ALU.add)
        y_out.mark(nc.vector.tensor_tensor(r, bank, row.unsqueeze(1).to_broadcast([P, 4, C]), op))
        y_out.latest(nc.vector)
        chain(nc.vector.tensor_tensor(tokens, tokens, r, ALU.add))
        yield

    stretch = STRETCH["f" if gated else "g"]

    def step(n, p, left):
        parts = []
        if not isinstance(n, int) or n > 0:
            parts.append((tag + "e", closing(n - 1, 1 - p), *stretch[0]))
        if left >= 1:
            parts.append((tag + "p", prologue(n + 1, 1 - p), *stretch[1]))
        if left >= 2:
            parts.append((tag + "a", normed(n + 2, p), *stretch[2]))
        weave(pr, (tag, main(n, p), 0.0, 1.0), *parts)

    nb = TILES // 4
    pr.fence()
    if meanwhile:
        meanwhile()
    finish(normed(0, 0))
    finish(prologue(0, 0))
    finish(normed(1, 1))
    pipeline(nc, nb, step, tail=2)
    finish(closing(nb - 1, (nb - 1) % 2))
    pr.fence()


def l0_ffn_weights(pr, mem):
    io, w = pr.io, {}
    sem = pr.nc.alloc_semaphore("l0f_w")
    for name, shape in (("w1_w", [P, HID]), ("w2_w", [P, HID]), ("h1_w", [P, K4, HID]), ("h2_w", [P, K4, HID]),
                        ("w3_w", [P, K4, C]), ("w1_s", [P, K4]), ("w2_s", [P, K4]), ("h1_s", [P, K4]),
                        ("h2_s", [P, K4])):
        w[name] = pr.sb("f_" + name, shape, F32, mem)
        load(pr, w[name][...], io["L0_ffn_" + name], sem)
    w["w3_s"] = pr.sb("f_w3s", [P, C], F32, mem)
    load(pr, w["w3_s"][:, :], io["L0_ffn_w3_s"].partition_broadcast(P), sem)
    return w, (sem, 160)


def l0_ffn(pr, mem):
    nc = pr.nc
    w, (sem, v) = l0_ffn_weights(pr, mem)
    nc.sync.wait_ge(sem, v)
    pr.fence()
    high, low = nc.alloc_semaphore("f_high"), nc.alloc_semaphore("f_low")
    parts = {}
    for i, name in enumerate(("w1_w", "w2_w", "h1_w", "h2_w", "w3_w")):
        m = w[name]
        parts[name] = [pr.sb(f"f_{name}{x}", list(m.shape), F16, mem) for x in "hl"]
        nc.scalar.activation(parts[name][0][...], m[...], ACT.Copy).then_inc(high, 1)
        nc.vector.wait_ge(high, i + 1)
        nc.vector.tensor_tensor(parts[name][1][...], m[...], parts[name][0][...], ALU.subtract).then_inc(low, 1)
    nc.tensor.wait_ge(low, len(parts))
    feed_forward(pr, mem, "f", pr.x, pr.x, [(parts["w1_w"], w["w1_s"], None), (parts["w2_w"], w["w2_s"], None)],
                 [(parts["h1_w"], w["h1_s"]), (parts["h2_w"], w["h2_s"])], parts["w3_w"], w["w3_s"][:, :], None,
                 meanwhile=lambda: clear_rows(pr))


def fold_weights(pr, mem, tag, weights):
    nc, psum = pr.nc, pr.psum
    copied, multiplied, done = (nc.alloc_semaphore(tag + x) for x in ("_copied", "_multiplied", "_folded"))
    wide = [pr.sb(f"{tag}_offset{n}", [P, P], F32, mem) for n in range(len(weights))]
    for n, (w, gain, offset, out, plus) in enumerate(weights):
        nc.vector.tensor_copy(wide[n][0:w.shape[0], :], offset.to_broadcast([w.shape[0], P])).then_inc(copied, 1)
    for n, (w, gain, offset, out, plus) in enumerate(weights):
        bank = psum[:, n, :]
        nc.tensor.wait_ge(copied, n + 1)
        if out.shape[1] == HID:
            inst = nc.tensor.matmul(bank, wide[n][0:w.shape[0], :], w, start=True, stop=True)
        else:
            for m in range(K4):
                inst = nc.tensor.matmul(bank[:, m:m + 1], w[:, m * P:m * P + P], offset, start=(m == 0), stop=True,
                                        skip_group_check=True)
        inst.then_inc(multiplied, 1)
    for n, (w, gain, offset, out, plus) in enumerate(weights):
        nc.vector.wait_ge(multiplied, n + 1)
        if plus is None:
            nc.vector.tensor_copy(out, psum[:, n, :]).then_inc(done, 1)
        else:
            nc.vector.tensor_tensor(out, psum[:, n, 0:K4], plus, ALU.add).then_inc(done, 1)
        nc.vector.tensor_scalar(w, w, gain, None, ALU.mult).then_inc(done, 1)
    nc.vector.wait_ge(done, 2 * len(weights))


def mha_weights(pr, mem, tag, pre, norm):
    io, w = pr.io, {}
    ck = C if pre == "a1" else CC
    sem = pr.nc.alloc_semaphore(tag + "_w")
    q = lambda x: io[f"L1_xattn_{x}"]
    for name, rows in (("wq", C), ("wk", ck), ("wv", ck)):
        w[name] = pr.sb(f"{tag}_{name}", [rows, HID], F32, mem)
        load(pr, w[name][:, :], q(f"{pre}_{name}"), sem)
    w["li1"] = pr.sb(tag + "_li1", [P, K4, C], F32, mem)
    load(pr, w["li1"][:, :, :], q(pre + "_li1_w"), sem)
    for name, src, rows in (("gx", "lnx_g", C), ("bx", "lnx_b", C), ("gy", "lny_g", ck), ("by", "lny_b", ck)):
        w[name] = pr.sb(f"{tag}_{name}", [rows, 1], F32, mem)
        load(pr, w[name][:, :], q(f"{pre}_{src}").unsqueeze(1), sem)
    for name, src in (("li1_b", pre + "_li1_b"), ("g", norm + "_g"), ("b", norm + "_b")):
        w[name] = pr.sb(f"{tag}_{name}_row", [P, C], F32, mem)
        load(pr, w[name][:, :], q(src).partition_broadcast(P), sem)
    for name in ("bq", "bk", "bv"):
        w[name] = pr.sb(f"{tag}_{name}", [P, HID], F32, mem)
    return w, (sem, 11 * 16)


def mha_attention(pr, mem, tag, own):
    nc, psum = pr.nc, pr.psum
    D, G = 32, 4
    R = 3 * D + 1
    NM = 3 * D
    RP = R + 1
    SCALE = float(D) ** -0.5
    w, (sem, v) = mha_weights(pr, mem, tag, "a1" if own else "a2", "ln1" if own else "ln2")
    z = [pr.sb(f"{tag}_z{i}", [P, 2, C], F32, mem) for i in range(2)]
    zi = pr.sb(tag + "_zi", [P, 2, C], F32, mem)
    zT = [pr.sb(f"{tag}_zT{i}", [P, T], F32, mem) for i in range(2)]
    qf = [pr.sb(f"{tag}_qf{i}", [P, HID], F32, mem) for i in range(4)]
    qtok = [pr.sb(f"{tag}_qtok{i}", [P, 2, H, RP], F16, mem) for i in range(2)]
    ktok = [pr.sb(f"{tag}_ktok{i}", [P, 2 if own else 1, H, RP], F16, mem) for i in range(2)]
    KW = T if own else TC
    QT = [pr.sb(f"{tag}_QT{i}", [R, H, T], F16, mem) for i in range(2)]
    KT = [pr.sb(f"{tag}_KT{i}", [R, H, KW], F16, mem) for i in range(2)]
    nm = pr.sb(tag + "_nm", [P, 2, H], F16, mem)
    nmT = pr.sb(tag + "_nmT", [H, T], F16, mem)
    prob = [pr.sb(f"{tag}_prob{i}", [P, 2 * T], F32, mem) for i in range(4)]
    late = [pr.sb(f"{tag}_late{i}", [P, 2, P], F32, mem) for i in range(4)] if own else None
    ndT = [pr.sb(f"{tag}_ndT{i}", [P, G, 2 * T], F32, mem) for i in range(2)]
    rden = pr.sb(tag + "_rden", [P, 2, H], F32, mem)
    o = pr.sb(tag + "_o", [P, 2, H, D], F32, mem)
    oT = pr.sb(tag + "_oT", [P, G, T], F32, mem)
    res = pr.sb(tag + "_res", [P, 2, C], F32, mem)
    if own:
        V = [pr.sb(f"{tag}_V{i}", [P, 2, HID], F32, mem) for i in range(2)]
        zeroed = []
        sums = pr.ones[:, 0:D]
    else:
        V = [pr.sb(f"{tag}_V{i}", [P, H // 2, 2, D], F32, mem) for i in range(2)]
        pair_ones = pr.sb(tag + "_pair_ones", [P, 2, D], F32, mem)
        zeroed = [*V, pair_ones]
        sums = pair_ones[:, :, :].rearrange("p a d -> p (a d)")
        zc = [pr.sb(f"{tag}_zc{i}", [P, 1, CC], F32, mem) for i in range(2)]
        cT = [pr.sb(f"{tag}_cT{i}", [CC, P], F32, mem) for i in range(2)]
    s0 = pr.nc.alloc_semaphore(tag + "_init")
    for m in [*(m[...] for m in zeroed), *(m[:, :, :, NM:] for m in qtok + ktok)]:
        inst = nc.vector.memset(m, 0.0)
    inst.then_inc(s0, 1)
    nc.vector.wait_ge(s0, 1)
    if not own:
        for a in range(2):
            nc.vector.memset(pair_ones[TC * a:TC * a + TC, a, :], 1.0)
    for m in ktok:
        inst = nc.vector.memset(m[:, :, :, NM:NM + 1], 1.0)
    inst.then_inc(s0, 1)
    nc.vector.wait_ge(s0, 2)
    nc.sync.wait_ge(sem, v)
    pr.fence()
    fold_weights(pr, mem, tag, [(w["wq"][:, :], w["gx"][:, :], w["bx"][:, :], w["bq"][:, :], None),
                                (w["wk"][:, :], w["gy"][:, :], w["by"][:, :], w["bk"][:, :], None),
                                (w["wv"][:, :], w["gy"][:, :], w["by"][:, :], w["bv"][:, :], None)])

    SA, SP, SQ, SM, SE = (Stage(pr, tag + x) for x in "apqme")
    ln_in = LayerNorm(pr, SA, "lni", 2, mem, twice=own)
    ln_x = LayerNorm(pr, SA, "lnx", 2, mem)
    ln_c = None if own else LayerNorm(pr, SA, "lnc", 1, mem)
    pro = Ring(SP, "pro", [psum[:, 0, :]])
    pre = Ring(SQ, "pre", [psum[:, i, :] for i in (1, 2)])
    z_ready, high, low = SA.counter("z"), SP.counter("high"), SP.counter("low")
    chain_a = SA.chain(nc.vector, "chain")
    nm_placed = SQ.counter("nm_placed", 16)
    st_full, exp_done, sel_done, av_done, nd_ready = (SM.counter(x) for x in ("st_full", "exp", "sel", "av", "nd"))
    epi = Ring(SE, "epi", [psum[:, 7, :]])
    chain_e = SE.chain(nc.vector, "chain")
    src, u, xo, xs = (pr.x if own else pr.u), pr.u, pr.xo, pr.x
    two = lambda m, n: m[:, bass.ds(n * 2, 2), :]
    row2 = lambda m: m[:, :].unsqueeze(1).to_broadcast([P, 2, C])

    def stack(bank, bias, dst, turn, key, rows=P):
        pro.drain("v")
        f = qf[turn][0:rows, :]
        low.wait(nc.vector, SP.n - 1, turn + 1)
        pro.drained("v", nc.vector.tensor_tensor(f, bank[0:rows, :], bias[0:rows, :], ALU.add))
        pro.out["v"].latest(nc.scalar)
        f3 = f.rearrange("p (h d) -> p h d", d=D)
        d3 = dst[:, :, 0:NM].rearrange("p h (k d) -> p h k d", d=D)
        twice = d3[:, :, 0:2, :] if key else d3[:, :, 0:3:2, :]
        high.mark(nc.scalar.activation(twice, f3.unsqueeze(2).to_broadcast([rows, H, 2, D]), ACT.Copy))
        high.latest(nc.gpsimd)
        low.mark(nc.gpsimd.tensor_tensor(d3[:, :, 2 if key else 1, :], f3, d3[:, :, 0, :], ALU.subtract))

    def turned(tok, out, rows, width, who):
        bank16 = pre.claim(apart=rows < P).bitcast(F16)
        for h in range(8):
            inst = nc.tensor.transpose(bank16[0:R, h * width:h * width + width], tok[:, h, 0:R],
                                       pr.ident16[0:rows, 0:rows])
        pre.filled(inst)
        pre.drain(who)
        source = bank16[0:R, 0:8 * width].rearrange("p (h t) -> p h t", h=8)
        pre.drained(who, nc.vector.tensor_copy(out, source) if who == "v" else
                    nc.scalar.activation(out, source, ACT.Copy))

    def normed(n, p):
        SA.begin(n)
        un = two(u, n)
        ln_in(two(src, n))
        yield
        chain_a(ln_in.normalise(zi, two(src, n)))
        chain_a(nc.vector.tensor_tensor(zi[:, :, :], zi[:, :, :], row2(w["g"]), ALU.mult))
        chain_a(nc.vector.tensor_tensor(un, zi[:, :, :], row2(w["b"]), ALU.add))
        yield
        ln_x(un)
        cn = None if own else pr.ctx2[:, bass.ds(n, 1), :]
        if not own:
            ln_c(cn)
        yield
        pro.full.wait(nc.vector, n - 2, 1)
        z_ready.mark(ln_x.normalise(z[p], un))
        if not own:
            z_ready.mark(ln_c.normalise(zc[p], cn))
        yield

    def project(n, p):
        SP.begin(n)
        z_ready.wait_all(nc.tensor, n)
        bank = pro.claim()
        for t in range(2):
            inst = nc.tensor.transpose(bank[:, t * P:t * P + P], z[p][:, t, :], pr.ident[:, :])
        if not own:
            inst = nc.tensor.transpose(bank[0:CC, T:T + P], zc[p][:, 0, :], pr.ident[:, :])
        pro.filled(inst)
        pro.drain("a")
        if not own:
            nc.scalar.activation(cT[p][:, :], bank[0:CC, T:T + P], ACT.Copy)
        pro.drained("a", nc.scalar.activation(zT[p][:, :], bank[:, 0:T], ACT.Copy))
        yield
        uses = [(zT[p][:, t * P:t * P + P], x, tok[p][:, t, :, :], P) for t in range(2)
                for x, tok in (("q", qtok), ("k", ktok)) if own or x == "q"]
        if not own:
            uses.append((cT[p][:, :], "k", ktok[p][0:TC, 0, :, :], TC))
        for turn, (lhsT, x, dst, rows) in enumerate(uses):
            bank = pro.claim()
            pro.filled(nc.tensor.matmul(bank, lhsT, w["w" + x][:, :], start=True, stop=True))
            stack(bank, w["b" + x], dst, turn, x == "k", rows)
            yield

    def prepare(n, p):
        SQ.begin(n)
        for t in range(2 if own else 1):
            bank = pre.claim()
            pre.filled(nc.tensor.matmul(bank, zT[p][:, t * P:t * P + P] if own else cT[p][:, :], w["wv"][:, :],
                                        start=True, stop=True))
            pre.drain("v")
            if own:
                inst = nc.vector.tensor_tensor(V[p][:, t, :], bank, w["bv"][:, :], ALU.add)
            else:
                for a in range(2):
                    half = slice(TC * a, TC * a + TC)
                    pick = lambda m: m[half, :].rearrange("p (i a d) -> p i a d", a=2, d=D)[:, :, a, :]
                    inst = nc.vector.tensor_tensor(V[p][half, :, a, :], pick(bank), pick(w["bv"]), ALU.add)
            pre.drained("v", inst)
            yield
        low.wait_all(nc.tensor, n)
        for t in range(2):
            for e in range(2):
                turned(qtok[p][:, t, 8 * e:8 * e + 8, :], QT[p][:, 8 * e:8 * e + 8, t * P:t * P + P], P, P, "av"[e])
                yield
                if own:
                    turned(ktok[p][:, t, 8 * e:8 * e + 8, :], KT[p][:, 8 * e:8 * e + 8, t * P:t * P + P], P, P, "va"[e])
                    yield
        if not own:
            for e in range(2):
                turned(ktok[p][0:TC, 0, 8 * e:8 * e + 8, :], KT[p][:, 8 * e:8 * e + 8, :], TC, TC, "av"[e])
                yield
        pre.out["a"].latest(nc.tensor), pre.out["v"].latest(nc.tensor)

        def mx_use(matmuls, out, groups):
            bank = pre.claim()
            for i, (at, width, lhsT, rhs) in enumerate(matmuls):
                inst = nc.tensor.matmul(bank[:, at:at + width], lhsT, rhs, start=(i == 0), stop=True,
                                        skip_group_check=True)
            pre.filled(inst)
            pre.drain("v")
            pre.drained("v", nc.vector.tensor_reduce(out, bank.rearrange("p (a b) -> p a b", a=groups), X, ALU.max,
                                                     negate=True))

        if own:
            for h in range(H):
                mx_use([(t * T, T, QT[p][:, h, t * P:t * P + P], KT[p][:, h, :]) for t in range(2)], nm[:, :, h], 2)
                yield
        else:
            for t in range(2):
                for e in range(2):
                    mx_use([(i * TC, TC, QT[p][:, 8 * e + i, t * P:t * P + P], KT[p][:, 8 * e + i, :])
                            for i in range(8)], nm[:, t, 8 * e:8 * e + 8], 8)
                    yield
        pre.out["v"].latest(nc.tensor)
        bank16 = pre.claim().bitcast(F16)
        for t in range(2):
            inst = nc.tensor.transpose(bank16[0:H, t * P:t * P + P], nm[:, t, :], pr.ident16[:, :])
        pre.filled(inst)
        pre.drain("a")
        nm_placed.wait_all(nc.scalar, n - 1)
        pre.drained("a", nc.scalar.activation(nmT[:, :], bank16[0:H, 0:T], ACT.Copy))
        pre.out["a"].latest(nc.sync)
        nm_placed.mark(nc.sync.dma_start(QT[p][NM:NM + 1, :, :], nmT[:, :]))
        yield

    units = H if own else G

    def scores(n, p, i):
        exp_done.wait(nc.tensor, n, i - 1)
        bank = psum[:, 3 + i % 2, :]
        if own:
            for kb in range(2):
                inst = nc.tensor.matmul(bank[:, kb * T:kb * T + T], KT[p][:, i, kb * P:kb * P + P], QT[p][:, i, :],
                                        start=(kb == 0), stop=True, skip_group_check=True)
        else:
            for j in range(4):
                a, pair = j % 2, j // 2
                inst = nc.tensor.matmul(bank[TC * a:TC * a + TC, pair * T:pair * T + T], KT[p][:, 4 * i + j, :],
                                        QT[p][:, 4 * i + j, :], start=(pair == 0), stop=True, skip_group_check=True)
        st_full.mark(inst)
        st_full.latest(nc.scalar)
        av_done.wait(nc.scalar, n, i - 3)
        exp_done.mark(nc.scalar.activation(prob[i % 4][:, :], bank, ACT.Exp, scale=SCALE))
        if own:
            exp_done.latest(nc.gpsimd)
            av_done.wait(nc.gpsimd, n, i - 3)
            pm = prob[i % 4][:, :]
            for b, at in enumerate((0, T + P)):
                inst = nc.gpsimd.affine_select(out=late[i % 4][:, b, :], in_=pm[:, at:at + P], compare_op=ALU.is_gt,
                                               fill=0.0, base=0, pattern=[[-1, P]], channel_multiplier=1)
            sel_done.mark(inst)

    def values(n, p, i):
        g = i // 4 if own else i
        j = i % 4
        pb = prob[i % 4]
        bank = psum[:, 5 + g % 2, :]
        if j == 0 or not own:
            nd_ready.wait(nc.tensor, n, g - 1)
        exp_done.wait(nc.tensor, n, i + 1)
        if own:
            o_ = bank[32 * j:32 * j + 32, :]
            for kb in range(2):
                nc.tensor.matmul(o_[:, T:2 * T], sums, pb[:, kb * T:kb * T + T], start=(kb == 0), stop=(kb == 1),
                                 skip_group_check=True)
            yield
            sel_done.wait(nc.tensor, n, i + 1)
            vh = lambda kb: V[p][:, kb, i * D:i * D + D]
            nc.tensor.matmul(o_[:, 0:P], vh(1), pb[:, T:T + P], start=True, stop=False, skip_group_check=True)
            nc.tensor.matmul(o_[:, P:T], vh(1), late[i % 4][:, 1, :], start=False, stop=True, skip_group_check=True)
            inst = nc.tensor.matmul(o_[:, 0:P], vh(0), late[i % 4][:, 0, :], start=False, stop=True,
                                    skip_group_check=True)
        else:
            for pair in range(2):
                if pair:
                    yield
                o_ = bank[64 * pair:64 * pair + 64, :]
                q = pb[:, pair * T:pair * T + T]
                nc.tensor.matmul(o_[:, T:2 * T], sums, q, start=True, stop=True, skip_group_check=True)
                inst = nc.tensor.matmul(o_[:, 0:T], V[p][:, 2 * i + pair, :, :].rearrange("p a d -> p (a d)"), q,
                                        start=True, stop=True, skip_group_check=True)
        av_done.mark(inst)
        if j == 3 or not own:
            av_done.latest(nc.scalar)
            if g == 0:
                epi.full.wait(nc.scalar, n - 1, 1)
            nd_ready.mark(nc.scalar.activation(ndT[p][:, g, :], bank, ACT.Copy))
        yield

    def epilogue(n, p):
        SE.begin(n)
        nd_ready.wait(nc.tensor, n, G)
        for t in range(2):
            bank = epi.claim()
            for g in range(G):
                inst = nc.tensor.transpose(bank[:, g * P:g * P + P], ndT[p][:, g, T + t * P:T + t * P + P], pr.ident[:, :])
            epi.filled(inst)
            epi.drain("v")
            epi.drained("v", nc.vector.reciprocal(rden[:, t, :], bank.rearrange("p (h d) -> p h d", d=D)[:, :, 0]))
            yield
            bank = epi.claim()
            for g in range(G):
                inst = nc.tensor.transpose(bank[:, g * P:g * P + P], ndT[p][:, g, t * P:t * P + P], pr.ident[:, :])
            epi.filled(inst)
            epi.drain("v")
            epi.out["v"].latest(nc.vector)
            epi.drained("v", nc.vector.tensor_tensor(o[:, t, :, :], bank.rearrange("p (h d) -> p h d", d=D),
                                                     rden[:, t, :].unsqueeze(2).to_broadcast([P, H, D]), ALU.mult))
            yield
            bank = epi.claim()
            flat = o[:, t, :, :].rearrange("p h d -> p (h d)")
            for g in range(G):
                inst = nc.tensor.transpose(bank[:, g * P:g * P + P], flat[:, g * P:g * P + P], pr.ident[:, :])
            epi.filled(inst)
            epi.drain("a")
            epi.drained("a", nc.scalar.activation(oT[:, :, t * P:t * P + P], bank.rearrange("p (g t) -> p g t", g=G),
                                                  ACT.Copy))
            yield
        bank = epi.claim()
        for t in range(2):
            for g in range(G):
                inst = nc.tensor.matmul(bank[:, t * P:t * P + P], oT[:, g, t * P:t * P + P], w["li1"][:, g, :],
                                        start=(t == 0 and g == 0), stop=(g == G - 1), skip_group_check=True)
        epi.filled(inst)
        epi.drain("v")
        un, xon, xn, r = two(u, n), two(xo, n), two(xs, n), res[:, :, :]
        epi.drained("v", nc.vector.tensor_tensor(r, bank[:, 0:T].rearrange("p (t c) -> p t c", t=2), row2(w["li1_b"]),
                                                 ALU.add))
        epi.out["v"].latest(nc.vector)
        chain_e(nc.vector.tensor_tensor(xon, un, r, ALU.add))
        if own:
            chain_e(nc.vector.tensor_tensor(un, un, xon, ALU.add))
        else:
            chain_e(nc.vector.tensor_tensor(r, un, xon, ALU.add))
            chain_e(nc.vector.tensor_tensor(xn, xn, r, ALU.add))
        yield

    LAG = 2 if own else 1

    def main(n, p):
        SM.begin(n)
        nm_placed.wait_all(nc.tensor, n)
        for i in range(units + LAG):
            if i < units:
                scores(n, p, i)
                yield
            if i >= LAG:
                yield from values(n, p, i - LAG)

    run_pipeline(pr, tag, B, normed, project, prepare, main, epilogue)


def mha_ffn(pr, mem, tag, pre, dst):
    nc, io = pr.nc, pr.io
    q = lambda x: io[f"L1_xattn_{pre}_{x}"]
    sem = pr.nc.alloc_semaphore(tag + "_w")
    li2 = pr.sb(tag + "_li2", [P, HID], F32, mem)
    li3 = pr.sb(tag + "_li3", [P, K4, C], F32, mem)
    cols = pr.sb(tag + "_cols", [P, 2, 1], F32, mem)
    b2 = pr.sb(tag + "_b2", [P, K4], F32, mem)
    bias = pr.sb(tag + "_bias", [P, K4], F32, mem)
    b3 = pr.sb(tag + "_b3", [P, C], F32, mem)
    load(pr, li2[:, :], q("li2_w"), sem)
    load(pr, li3[:, :, :], q("li3_w"), sem)
    load(pr, cols[:, 0, :], q("ln3_g").unsqueeze(1), sem)
    load(pr, cols[:, 1, :], q("ln3_b").unsqueeze(1), sem)
    load(pr, b2[:, :], q("li2_b"), sem)
    load(pr, b3[:, :], q("li3_b").partition_broadcast(P), sem)
    nc.sync.wait_ge(sem, 96)
    pr.fence()
    fold_weights(pr, mem, tag, [(li2[:, :], cols[:, 0, :], cols[:, 1, :], bias[:, :], b2[:, :])])
    pr.fence()
    feed_forward(pr, mem, tag, pr.xo, dst, [([li2], None, bias)], [], [li3], None, b3[:, :])


E = 8
CAP = 640
CT = CAP // P


ROW = C + 1


def expert_rows(pr):
    nc = pr.nc
    pr.tokens_in = nc.dram_tensor("expert_in", [E * CAP + TILES * P, ROW], F32).ap()
    pr.tokens_out = nc.dram_tensor("expert_out", [TILES * P + CAP, C], F32).ap()
    pr.empty = pr.sb("empty", [P, CT, ROW])
    spare = pr.sb("spare", [P, CT], mybir.dt.int32)
    made, s = nc.alloc_semaphore("empty_made"), nc.alloc_semaphore("empty_v")
    pr.cleared = nc.alloc_semaphore("cleared")
    nc.gpsimd.iota(spare[:, :], [[P, CT]], base=TILES * P, channel_multiplier=1).then_inc(made, 1)
    nc.vector.memset(pr.empty[:, :, :], 0.0).then_inc(s, 1)
    nc.vector.wait_ge(made, 1)
    nc.vector.wait_ge(s, 1)
    nc.vector.tensor_copy(pr.empty[:, :, C], spare[:, :]).then_inc(made, 1)
    nc.sync.wait_ge(made, 2)


def by_tile(rows, first, tiles=CT):
    return rows[bass.ds(first, tiles * P), :].rearrange("(t p) c -> p t c", p=P)


def clear_rows(pr):
    with pr.nc.sync.Fori(0, E) as e:
        pr.nc.sync.dma_start(by_tile(pr.tokens_in, e * CAP), pr.empty[:, :, :]).then_inc(pr.cleared, 16)
        pr.nc.sync.dma_start(by_tile(pr.tokens_out, e * N4, 4), pr.empty[:, 0:4, 0:C]).then_inc(pr.cleared, 16)


def moe(pr, mem, dst):
    nc, io, psum, xn = pr.nc, pr.io, pr.psum, pr.u
    tokens_in, tokens_out = pr.tokens_in, pr.tokens_out
    sem = pr.nc.alloc_semaphore("m_w")
    gate_w = pr.sb("m_gate_w", [P, E], F32, mem)
    gate_b = pr.sb("m_gate_b", [P, E], F32, mem)
    load(pr, gate_w[:, :], io["gate_wT"], sem)
    load(pr, gate_b[:, :], io["L1_ffn_gate_b"].partition_broadcast(P), sem)
    nc.sync.wait_ge(sem, 32)

    w1 = [pr.sb(f"m_w1_{i}", [P, HID], F32, mem) for i in range(2)]
    w2 = [pr.sb(f"m_w2_{i}", [P, K4, C], F32, mem) for i in range(2)]
    b1 = [pr.sb(f"m_b1_{i}", [P, K4], F32, mem) for i in range(2)]
    b2 = [pr.sb(f"m_b2_{i}", [P, C], F32, mem) for i in range(2)]
    xt = [pr.sb(f"m_xt{i}", [P, CT, ROW], F32, mem) for i in range(2)]
    number = [pr.sb(f"m_number{i}", [P, CT], U32, mem) for i in range(2)]
    xT = [pr.sb(f"m_xT{i}", [P, CAP], F32, mem) for i in range(2)]
    hT = [pr.sb(f"m_hT{i}", [P, K4, CAP], F32, mem) for i in range(2)]
    ys = pr.sb("m_ys", [P, CT, C], F32, mem)
    SL0, SL1, SL2, ST, SX, SY = (Stage(pr, x) for x in ("ei", "el", "ek", "et", "ex", "ey"))
    loaded0, loaded1, loaded2 = (x.counter("loaded", 16) for x in (SL0, SL1, SL2))
    xT_full, xT_out = ST.counter("xT_full"), ST.counter("xT_out")
    h_full, h_out, numbered = SX.counter("h_full"), SX.counter("h_out"), SX.counter("numbered")
    y_full, y_out = SY.counter("y_full"), SY.counter("y_out")
    stored = SY.counter("stored", 16, base=0)
    sent = SY.counter("sent")
    HALF = CAP // 2

    def one(name, n):
        return io["L1_ffn_" + name][bass.ds(n, 1), :, :].rearrange("e p f -> (e p) f")

    def fetch_first(n, p):
        SL1.begin(n)
        h_out.wait_all(nc.sync, n - 2)
        loaded1.wait_all(nc.sync, n - 1)
        loaded1.mark(nc.sync.dma_start(w1[p][:, :], one("w1", n)))
        loaded1.mark(nc.sync.dma_start(b1[p][:, :], one("b1", n)))
        yield

    def fetch_tokens(n, p):
        SL0.begin(n)
        xT_full.wait_all(nc.sync, n - 2), numbered.wait_all(nc.sync, n - 2)
        loaded0.wait_all(nc.sync, n - 1)
        loaded0.mark(nc.sync.dma_start(xt[p][:, :, :], by_tile(tokens_in, n * CAP)))
        yield

    def fetch_second(n, p):
        SL2.begin(n)
        y_out.wait_all(nc.sync, n - 2)
        loaded2.wait_all(nc.sync, n - 1)
        loaded2.mark(nc.sync.dma_start(w2[p][:, :, :].rearrange("p k c -> p (k c)"), one("w2", n)))
        loaded2.mark(nc.sync.dma_start(b2[p][:, :], one("b2", n).partition_broadcast(P).rearrange("q e c -> q (e c)")))
        yield

    iota_i = pr.sb("m_iota_i", [P, 4, E], mybir.dt.int32, mem)
    token_i = pr.sb("m_token_i", [P, TILES], mybir.dt.int32, mem)
    iota_e, token = pr.sb("m_iota_e", [P, 4, E], F32, mem), pr.sb("m_token", [P, 2, TILES], F32, mem)
    tri = pr.sb("m_tri", [P, P], F32, mem)
    z = [pr.sb(f"m_z{i}", [P, 4, C], F32, mem) for i in range(2)]
    zT = pr.sb("m_zT", [P, N4], F32, mem)
    send = [pr.sb(f"m_send{i}", [P, 4, ROW], F32, mem) for i in range(2)]
    logits = [pr.sb(f"m_logits{i}", [P, 4, E], F32, mem) for i in range(2)]
    before = [pr.sb(f"m_before{i}", [P, 4, E], F32, mem) for i in range(2)]
    d, chance, pick, hot, count = (pr.sb("m_" + x, [P, 4, E], F32, mem) for x in "d chance pick hot count".split())
    top, total, idx, place, keep, row, tmp = (
        pr.sb("m_" + x, [P, 4], F32, mem) for x in "top total idx place keep row tmp".split())
    row_u = [pr.sb(f"m_row_u{i}", [P, 4], U32, mem) for i in range(2)]
    gate = pr.sb("m_gate", [P, TILES], F32, mem)
    sg, sc = nc.alloc_semaphore("m_g"), nc.alloc_semaphore("m_c")
    nc.gpsimd.iota(iota_i[:, :, :], [[0, 4], [1, E]], base=0, channel_multiplier=0).then_inc(sg, 1)
    nc.gpsimd.iota(token_i[:, :], [[P, TILES]], base=0, channel_multiplier=1).then_inc(sg, 1)
    nc.gpsimd.affine_select(out=tri[:, :], in_=pr.ones[:, :], compare_op=ALU.is_ge, fill=0.0, base=0,
                            pattern=[[1, P]], channel_multiplier=-1).then_inc(sg, 1)
    nc.vector.wait_ge(sg, 3)
    nc.vector.memset(before[0][:, 0, :], 0.0)
    nc.vector.tensor_copy(iota_e[:, :, :], iota_i[:, :, :])
    nc.vector.tensor_copy(token[:, 0, :], token_i[:, :]).then_inc(sc, 1)
    nc.vector.wait_ge(sc, 1)
    nc.vector.tensor_scalar(token[:, 1, :], token[:, 0, :], float(E * CAP), None, ALU.add).then_inc(sc, 1)
    nc.vector.wait_ge(sc, 2)
    nc.gpsimd.wait_ge(pr.cleared, 16 * 2 * E)

    SA, SP, SM = (Stage(pr, "m" + x) for x in "apm")
    ln = LayerNorm(pr, SA, "ln", 4, mem)
    pro = Ring(SP, "pro", [psum[:, 0, :], psum[:, 1, :]])
    z_ready, logits_ready = SA.counter("z"), SP.counter("logits")
    copied = SM.counter("copied")
    there = SM.counter("there", 16, base=0)
    hot_ready, place_full, chance_ready = SM.counter("hot"), SM.counter("place"), SM.counter("chance")
    v = SM.chain(nc.vector, "v")
    four = lambda m, n: m[:, bass.ds(n * 4, 4)]
    own_row = token[:, 1, :]

    def normed(n, p):
        SA.begin(n)
        tokens = pr.x[:, bass.ds(n * 4, 4), :]
        ln(tokens)
        yield
        copied.wait_all(nc.vector, n - 2)
        z_ready.mark(ln.normalise(z[p], tokens))
        yield

    def score(n, p):
        SP.begin(n)
        z_ready.wait_all(nc.tensor, n)
        bank = pro.claim()
        for t in range(4):
            inst = nc.tensor.transpose(bank[:, t * P:t * P + P], z[p][:, t, :], pr.ident[:, :])
        pro.filled(inst)
        pro.drain("a")
        pro.drained("a", nc.scalar.activation(zT[:, :], bank, ACT.Copy))
        yield
        pro.out["a"].latest(nc.tensor)
        bank = pro.claim()
        for t in range(4):
            inst = nc.tensor.matmul(bank[:, t * E:t * E + E], zT[:, t * P:t * P + P], gate_w[:, :], start=(t == 0),
                                    stop=True, skip_group_check=True)
        pro.filled(inst)
        pro.drain("v")
        pro.drained("v", nc.vector.tensor_tensor(logits[p][:, :, :], bank[:, 0:4 * E].rearrange("p (t e) -> p t e", e=E),
                                                 gate_b[:, :].unsqueeze(1).to_broadcast([P, 4, E]), ALU.add))
        pro.out["v"].latest(nc.vector)
        yield

    def route(n, p):
        SM.begin(n)
        flat = lambda m: m[:, :, :].rearrange("p t e -> p (t e)")
        wide = lambda m: m[:, :].unsqueeze(2).to_broadcast([P, 4, E])
        v(nc.vector.tensor_reduce(tmp[:, :], logits[p][:, :, :], X, ALU.max))
        v(nc.vector.tensor_tensor(d[:, :, :], logits[p][:, :, :], wide(tmp), ALU.subtract))
        v.event.latest(nc.scalar)
        chance_ready.mark(nc.scalar.activation(chance[:, :, :], d[:, :, :], ACT.Exp))
        v(nc.vector.tensor_scalar(pick[:, :, :], d[:, :, :], 0.0, float(E), ALU.is_ge, ALU.mult))
        v(nc.vector.tensor_tensor(pick[:, :, :], iota_e[:, :, :], pick[:, :, :], ALU.subtract))
        v(nc.vector.tensor_reduce(idx[:, :], pick[:, :, :], X, ALU.min))
        v(nc.vector.tensor_tensor(hot[:, :, :], pick[:, :, :], wide(idx), ALU.is_equal))
        for t in range(4):
            to = before[p][:, t + 1, :] if t < 3 else before[1 - p][:, 0, :]
            v(nc.vector.tensor_tensor(to, before[p][:, t, :], hot[:, t, :], ALU.add))
        yield
        v.event.latest(nc.tensor)
        bank = psum[:, 2, 0:4 * E]
        nc.tensor.matmul(bank, tri[:, :], flat(hot), start=True, stop=False)
        place_full.mark(nc.tensor.matmul(bank, pr.ones[:, :], flat(before[p]), start=False, stop=True))
        there.wait_all(nc.scalar, n - 1)
        copied.mark(nc.scalar.activation(send[p][:, :, 0:C], z[p][:, :, :], ACT.Copy))
        chance_ready.latest(nc.vector)
        v(nc.vector.tensor_reduce(total[:, :], chance[:, :, :], X, ALU.add))
        v(nc.vector.reciprocal(top[:, :], total[:, :]))
        v(nc.vector.tensor_scalar(idx[:, :], idx[:, :], float(E), float(CAP), ALU.add, ALU.mult))
        place_full.latest(nc.vector)
        v(nc.vector.tensor_tensor(flat(count), bank, flat(hot), ALU.mult))
        v(nc.vector.tensor_reduce(place[:, :], count[:, :, :], X, ALU.add))
        v(nc.vector.tensor_scalar(place[:, :], place[:, :], -1.0, None, ALU.add))
        v(nc.vector.tensor_scalar(keep[:, :], place[:, :], float(CAP), None, ALU.is_lt))
        v(nc.vector.tensor_tensor(tmp[:, :], place[:, :], idx[:, :], ALU.add))
        v(nc.vector.tensor_tensor(tmp[:, :], tmp[:, :], four(own_row, n), ALU.subtract))
        v(nc.vector.tensor_tensor(tmp[:, :], tmp[:, :], keep[:, :], ALU.mult))
        v(nc.vector.tensor_tensor(row[:, :], tmp[:, :], four(own_row, n), ALU.add))
        there.wait_all(nc.vector, n - 1)
        nc.vector.tensor_copy(send[p][:, :, C], four(token[:, 0, :], n))
        v(nc.vector.tensor_copy(row_u[p][:, :], row[:, :]))
        v.event.latest(nc.gpsimd), copied.latest(nc.gpsimd)
        for t in range(4):
            there.mark(nc.gpsimd.indirect_dma_start(
                out=tokens_in, out_offset=bass.IndirectOffsetOnAxis(ap=row_u[p][:, t:t + 1], axis=0),
                in_=send[p][:, t, :], in_offset=None))
        v(nc.vector.tensor_tensor(four(gate, n), top[:, :], keep[:, :], ALU.mult))
        yield

    def step(n, p, left):
        parts = [("route", route(n, p), *STRETCH["r"][0])]
        if left >= 1:
            parts.append(("score", score(n + 1, 1 - p), *STRETCH["r"][1]))
        if left >= 2:
            parts.append(("ahead", normed(n + 2, p), *STRETCH["r"][2]))
        weave(pr, *parts)

    pr.fence()
    finish(fetch_first(0, 0))
    finish(fetch_second(0, 0))
    finish(fetch_first(1, 1))
    finish(normed(0, 0))
    finish(score(0, 0))
    finish(normed(1, 1))
    pipeline(nc, TILES // 4, step, tail=2)
    pr.fence()
    there.wait_all(nc.sync, TILES // 4 - 1)

    def turn(n, p):
        ST.begin(n)
        loaded0.wait_all(nc.tensor, n)
        xT_out.wait_all(nc.tensor, n - 1)
        for t in range(CT):
            inst = nc.tensor.transpose(psum[:, t // 4, (t % 4) * P:(t % 4) * P + P], xt[p][:, t, 0:C], pr.ident[:, :])
        xT_full.mark(inst)
        xT_full.latest(nc.vector)
        nc.vector.tensor_copy(xT[p][:, 0:N4], psum[:, 0, :])
        xT_out.mark(nc.vector.tensor_copy(xT[p][:, N4:CAP], psum[:, 1, 0:CAP - N4]))
        yield

    def hidden(n, p):
        SX.begin(n)
        xT_out.wait_all(nc.tensor, n), loaded1.wait_all(nc.tensor, n)
        xT_out.wait_all(nc.vector, n)
        sent.wait_all(nc.vector, n - 2)
        numbered.mark(nc.vector.tensor_copy(number[p][:, :], xt[p][:, :, C]))
        for m in range(K4):
            h_out.wait(nc.tensor, n, m - 1)
            b = 2 + 2 * (m % 2)
            for half in range(2):
                inst = nc.tensor.matmul(psum[:, b + half, 0:HALF], w1[p][:, m * P:m * P + P],
                                        xT[p][:, half * HALF:half * HALF + HALF], start=True, stop=True)
            h_full.mark(inst)
            h_full.latest(nc.scalar)
            h_out.mark(nc.scalar.activation(hT[p][:, m, :].rearrange("p (a f) -> p a f", a=2), psum[:, b:b + 2, 0:HALF],
                                            ACT.Relu, bias=b1[p][:, m:m + 1]))
            yield

    def outputs(n, p):
        SY.begin(n)
        y_out.wait_all(nc.tensor, n - 1)
        loaded2.wait_all(nc.tensor, n)
        h_out.wait_all(nc.tensor, n)
        for t in range(CT):
            for k in range(K4):
                inst = nc.tensor.matmul(psum[:, 6 + t // 4, (t % 4) * P:(t % 4) * P + P], hT[p][:, k, t * P:t * P + P],
                                        w2[p][:, k, :], start=(t % 4 == 0 and k == 0), stop=(k == K4 - 1),
                                        skip_group_check=True)
            if t == CT - 1:
                y_full.mark(inst)
            yield
        y_full.latest(nc.vector)
        sent.wait_all(nc.vector, n - 1)
        b2w = b2[p][:, :].unsqueeze(1).to_broadcast([P, 4, C])
        nc.vector.tensor_tensor(ys[:, 0:4, :], psum[:, 6, :].rearrange("p (t c) -> p t c", c=C), b2w, ALU.add)
        y_out.mark(nc.vector.tensor_tensor(ys[:, 4, :], psum[:, 7, 0:C], b2[p][:, :], ALU.add))
        y_out.latest(nc.gpsimd)
        for t in range(CT):
            stored.mark(nc.gpsimd.indirect_dma_start(
                out=tokens_out, out_offset=bass.IndirectOffsetOnAxis(ap=number[p][:, t:t + 1], axis=0),
                in_=ys[:, t, :], in_offset=None))
        stored.wait_all(nc.gpsimd, n)
        sent.mark(nc.gpsimd.nop(nofuse=True))
        yield

    def expert_step(n, p, left):
        parts = [("hidden", hidden(n, p), *STRETCH["x"][0])]
        if not isinstance(n, int) or n > 0:
            parts.append(("outputs", outputs(n - 1, 1 - p), *STRETCH["x"][1]))
        if left >= 1:
            parts.append(("turn", turn(n + 1, 1 - p), *STRETCH["x"][2]))
        if left >= 2:
            parts.append(("fetch_first", fetch_first(n + 2, p), 0.99, 1.0))
            parts.append(("fetch_tokens", fetch_tokens(n + 2, p), 0.98, 1.0))
        if left >= 1:
            parts.append(("fetch_second", fetch_second(n + 1, 1 - p), 0.99, 1.0))
        weave(pr, *parts)

    finish(fetch_tokens(0, 0))
    finish(fetch_tokens(1, 1))
    finish(turn(0, 0))
    pipeline(nc, E, expert_step, tail=2)
    finish(outputs(E - 1, (E - 1) % 2))

    s_back, s_sum, s_out = (nc.alloc_semaphore("m_" + x) for x in ("back", "sum", "out"))
    sent.wait_all(nc.sync, E - 1)
    for i in range(4):
        tiles = slice(8 * i, 8 * i + 8)
        nc.sync.dma_start(xn[:, tiles, :], by_tile(tokens_out, 8 * i * P, 8)).then_inc(s_back, 16)
        nc.sync.wait_ge(s_back, 16 * (i + 1))
        nc.vector.wait_ge(s_back, 16 * (i + 1))
        for t in range(8 * i, 8 * i + 8):
            inst = nc.vector.scalar_tensor_tensor(out=pr.x[:, t, :], in0=xn[:, t, :], scalar=gate[:, t:t + 1],
                                                  in1=pr.x[:, t, :], op0=ALU.mult, op1=ALU.add)
        inst.then_inc(s_sum, 1)
    for i in range(4):
        tiles = slice(8 * i, 8 * i + 8)
        nc.scalar.wait_ge(s_sum, i + 1)
        nc.scalar.dma_start(dst[:, tiles, :], pr.x[:, tiles, :]).then_inc(s_out, 16)
    nc.sync.wait_ge(s_out, 16 * 4)
    pr.fence()


def program(nc, io, out, per):
    with ExitStack() as ctx:
        pr = Prog(nc, ctx, per, io)
        pr.psum = ctx.enter_context(nc.psum_tensor("psum", [P, 8, 512], F32))
        constants(pr)
        pr.x = pr.sb("x_sb", [P, TILES, C])
        expert_rows(pr)
        io_in = ctx.enter_context(nc.semaphore("io_in"))
        nc.sync.dma_start(pr.x[:, :, :], io["x"].rearrange("b (t p) c -> p (b t) c", p=P)).then_inc(io_in, 16)
        pr.ctxT = pr.sb("ctxT", [CC, B, TC])
        nc.scalar.dma_start(pr.ctxT[:, :, :], io["ctxT"]).then_inc(io_in, 16)
        pr.ctx2 = pr.sb("ctx2", [P, B, CC])
        for a in range(2):
            nc.scalar.dma_start(pr.ctx2[TC * a:TC * a + TC, :, :], io["ctx"]).then_inc(io_in, 16)
        nc.sync.wait_ge(io_in, 64)
        pr.fence()
        with pr.phase() as mem:
            l0_attention(pr, mem)
        with pr.phase() as mem:
            l0_ffn(pr, mem)
        pr.u = pr.sb("u_sb", [P, TILES, C])
        pr.xo = pr.sb("xo_sb", [P, TILES, C])
        for tag, own, dst in (("b", True, pr.u), ("c", False, pr.x)):
            with pr.phase() as mem:
                mha_attention(pr, mem, tag, own)
            with pr.phase() as mem:
                mha_ffn(pr, mem, tag + "f", "a1" if own else "a2", dst)
        with pr.phase() as mem:
            moe(pr, mem, out.rearrange("b (t p) c -> p (b t) c", p=P))
        return pr.seen


def by_chunk(v):
    return np.ascontiguousarray(v.reshape(-1, P, *v.shape[1:]).swapaxes(0, 1))


def ffn_layout(k, v):
    if k.endswith("_w"):
        v = by_chunk(v.T)
        return np.ascontiguousarray(v[:, 0]) if v.shape[1] == 1 else v
    return v if k.endswith("w3_s") else by_chunk(v)


def layout(inputs):
    a = {k: np.ascontiguousarray(v) for k, v in inputs.items()}
    for k, v in list(a.items()):
        if k.startswith("L0_ffn_"):
            a[k] = ffn_layout(k, v)
        elif k[-3:] in ("_wq", "_wk", "_wv"):
            a[k] = np.ascontiguousarray(v.transpose(1, 0, 2).reshape(v.shape[1], -1))
        elif k.endswith(("li1_w", "li3_w", "li2_b")):
            a[k] = by_chunk(v)
    for k in ("w2", "b1", "b2"):
        v = a["L1_ffn_" + k].reshape(E, -1, P if k == "b1" else C)
        a["L1_ffn_" + k] = np.ascontiguousarray(
            v if k == "b2" else v.transpose(0, 2, 1) if k == "b1" else
            v.reshape(E, K4, P, C).transpose(0, 2, 1, 3).reshape(E, P, K4 * C))
    a["gate_wT"] = np.ascontiguousarray(a.pop("L1_ffn_gate_w").T)
    a["ctx"] = np.ascontiguousarray(a["ctx_512"].transpose(1, 0, 2))
    a["ctxT"] = np.ascontiguousarray(a.pop("ctx_512").transpose(2, 0, 1))
    return a


def kernel(**inputs):
    import concourse.bacc as bacc
    from concourse.bass_utils import run_bass_kernel_spmd

    arrays = layout({k: np.asarray(v) for k, v in inputs.items()})
    per = {}
    for _ in range(2):
        nc = bacc.Bacc("TRN2", target_bir_lowering=False, num_devices=1)
        io = {k: nc.dram_tensor(f"in_{k}_dram", v.shape, mybir.dt.from_np(v.dtype), kind="ExternalInput").ap()
              for k, v in arrays.items()}
        out = nc.dram_tensor("out_0_dram", (B, T, C), F32, kind="ExternalOutput").ap()
        per = program(nc, io, out, per)
    r = run_bass_kernel_spmd(nc, [{f"in_{k}_dram": v for k, v in arrays.items()}], core_ids=[0])
    return r.results[0]["out_0_dram"]
```
